# Optimizing a Trainium2 kernel written in Bass

```python
import numpy as np
import jax
import jax.numpy as jnp

def _softmax(x, axis=-1):
    return jax.nn.softmax(x, axis=axis)

def _gelu(x):
    return jax.nn.gelu(x, approximate=True)

def _silu(x):
    return jax.nn.silu(x)

def _sigmoid(x):
    return jax.nn.sigmoid(x)

def _layernorm(x, axis=-1, eps=1e-05):
    m = jnp.mean(x, axis=axis, keepdims=True)
    v = jnp.var(x, axis=axis, keepdims=True)
    return (x - m) / jnp.sqrt(v + eps)

def _scatter_add(tgt, idx, src, axis=0):
    return tgt.at[idx].add(src)

def _segment_sum(src, seg, n):
    return jax.ops.segment_sum(src, seg, n)
kernel_name = 'mk_xattn_ffn_d2_seqx_r8_035b3a'

def setup_inputs(seed: int=0):
    np.random.seed(seed)
    _w = jnp.asarray

    def _rec_inputs():
        import jax
        import jax.numpy as jnp
        _rk = jax.random.key(seed)
        x = -0.0002928 + 1 * jax.random.normal(jax.random.fold_in(_rk, 1), (8, 256, 128), jnp.float32)
        _lenS = 256 - jax.random.randint(jax.random.fold_in(_rk, 7), (8,), 0, max(1, 256 // 4) + 1, jnp.int32)
        _lenS2 = 256 - jax.random.randint(jax.random.fold_in(_rk, 8), (8,), 0, max(1, 256 // 4) + 1, jnp.int32)
        _ctx_1024P = jax.random.normal(jax.random.fold_in(_rk, 11), (8, 16, 128), jnp.float32)
        _ctx_1024c = jax.random.dirichlet(jax.random.fold_in(_rk, 511), 0.3 * jnp.ones((16,), jnp.float32), (8, 256))
        _ctx_1024t = jnp.einsum('bsk,bkd->bsd', _ctx_1024c, _ctx_1024P)
        _ctx_1024t = _ctx_1024t * jax.lax.rsqrt(jnp.mean(jnp.square(_ctx_1024t)) + 1e-12) * 0.953939
        ctx_1024 = -1.39393e-06 + 0.999914 * (_ctx_1024t + 0.3 * jax.random.normal(jax.random.fold_in(_rk, 611), (8, 256, 128), jnp.float32))
        _validS = jnp.arange(256)[None, :] < _lenS[:, None]
        _validS2 = jnp.arange(256)[None, :] < _lenS2[:, None]
        _causal = jnp.tril(jnp.ones((256, 256), dtype=bool))
        mask_1x1xSxS2_ik0 = jnp.where(jnp.broadcast_to(_validS2[0:1, None, None, :], (1, 1, 256, 256)), 0, 1).astype(jnp.int32)
        return (x, ctx_1024, mask_1x1xSxS2_ik0)
    x, ctx_1024, mask_1x1xSxS2_ik0 = _rec_inputs()

    def _L0_xattn_setup():
        import math
        import jax, jax.numpy as jnp
        import numpy as np
        N_HEAD = 16

        def _slopes(n_head):
            cp2 = 2 ** int(math.floor(math.log2(n_head)))
            slopes = 0.5 ** np.arange(1, cp2 + 1)
            if cp2 < n_head:
                intra = 1.0 / math.sqrt(2.0)
                pair = intra ** np.arange(1, 1 + 2 * (n_head - cp2), 2)
                slopes = np.sort(np.concatenate([slopes, pair]))[::-1]
            return jnp.asarray(slopes, dtype=jnp.float32)

        def _alibi_bias(S):
            d = jnp.arange(S)[:, None] - jnp.arange(S)[None, :]
            return -jnp.maximum(d, 0).astype(jnp.float32)
        key = jax.random.key(seed)
        B, S, D = (2, 256, 128)
        ks = jax.random.split(key, 12)
        f = lambda k, sh: jax.random.normal(k, sh, dtype=jnp.float32)
        inp = {'q': f(ks[0], (B, S, D)), 'k': f(ks[1], (B, S, D)), 'v': f(ks[2], (B, S, D)), 'mask': jnp.tril(jnp.ones((S, S), dtype=jnp.int32))[None, None], 'wq_w': f(ks[3], (D, D)) * 0.02, 'wq_b': f(ks[4], (D,)) * 0.02, 'wk_w': f(ks[5], (D, D)) * 0.02, 'wk_b': f(ks[6], (D,)) * 0.02, 'wv_w': f(ks[7], (D, D)) * 0.02, 'wv_b': f(ks[8], (D,)) * 0.02, 'out_w': f(ks[9], (D, D)) * 0.02, 'out_b': f(ks[10], (D,)) * 0.02}
        return inp
    _L0_xattn_all = _L0_xattn_setup()
    _L0_xattn_in = {k: v for k, v in _L0_xattn_all.items() if k in ('wq_w', 'wq_b', 'wk_w', 'wk_b', 'wv_w', 'wv_b', 'out_w', 'out_b')}
    del _L0_xattn_all

    def _L0_ffn_setup():
        import jax, jax.numpy as jnp
        import numpy as np
        B, S, HID, DFF, E, K = (4, 256, 128, 512, 8, 256)
        key = jax.random.key(seed)
        ks = jax.random.split(key, 4)
        sc_h = 1.0 / np.sqrt(HID)
        sc_f = 1.0 / np.sqrt(DFF)
        return {'x': jax.random.normal(ks[0], (B, S, HID), jnp.float32), 'router_w': jax.random.normal(ks[1], (HID, E), jnp.float32) * sc_h, 'router_b': jnp.zeros((E,), jnp.float32), 'w1': jax.random.normal(ks[2], (E, HID, DFF), jnp.float32) * sc_h, 'b1': jnp.zeros((E, DFF), jnp.float32), 'w2': jax.random.normal(ks[3], (E, DFF, HID), jnp.float32) * sc_f, 'b2': jnp.zeros((E, HID), jnp.float32)}
    _L0_ffn_all = _L0_ffn_setup()
    _L0_ffn_in = {k: v for k, v in _L0_ffn_all.items() if k in ('router_w', 'router_b', 'w1', 'b1', 'w2', 'b2')}
    del _L0_ffn_all

    def _L1_xattn_setup():
        import jax, jax.numpy as jnp
        import numpy as np
        D_MODEL = 128
        NUM_HEADS = 16

        def _split_heads(x, n_heads):
            B, L, D = x.shape
            return x.reshape(B, L, n_heads, D // n_heads).transpose(0, 2, 1, 3)
        key = jax.random.key(seed)
        ks = jax.random.split(key, 11)
        B, L, D = (1, 512, D_MODEL)
        s = 1.0 / np.sqrt(D)
        inp = {'Q': jax.random.normal(ks[0], (B, L, D), jnp.float32), 'K': jax.random.normal(ks[1], (B, L, D), jnp.float32), 'V': jax.random.normal(ks[2], (B, L, D), jnp.float32), 'w_q': jax.random.normal(ks[3], (D, D), jnp.float32) * s, 'b_q': jax.random.normal(ks[4], (D,), jnp.float32) * s, 'w_k': jax.random.normal(ks[5], (D, D), jnp.float32) * s, 'b_k': jax.random.normal(ks[6], (D,), jnp.float32) * s, 'w_v': jax.random.normal(ks[7], (D, D), jnp.float32) * s, 'b_v': jax.random.normal(ks[8], (D,), jnp.float32) * s, 'w_o': jax.random.normal(ks[9], (D, D), jnp.float32) * s, 'b_o': jax.random.normal(ks[10], (D,), jnp.float32) * s}
        return inp
    _L1_xattn_all = _L1_xattn_setup()
    _L1_xattn_in = {k: v for k, v in _L1_xattn_all.items() if k in ('w_q', 'b_q', 'w_k', 'b_k', 'w_v', 'b_v', 'w_o', 'b_o')}
    del _L1_xattn_all

    def _L1_ffn_setup():
        import jax, jax.numpy as jnp
        import numpy as np
        LN_EPS = 1e-05

        def layer_norm(x, g, b):
            mu = jnp.mean(x, axis=-1, keepdims=True)
            var = jnp.var(x, axis=-1, keepdims=True)
            return (x - mu) / jnp.sqrt(var + LN_EPS) * g + b

        def balanced_assignment(scores):
            T, E = scores.shape
            C = T // E
            taken = jnp.zeros((T,), dtype=bool)
            parts = []
            for e in range(E):
                s = jnp.where(taken, -jnp.inf, scores[:, e])
                _, idx = jax.lax.top_k(s, C)
                parts.append(idx)
                taken = taken.at[idx].set(True)
            return jnp.concatenate(parts)
        key = jax.random.key(seed)
        ks = jax.random.split(key, 4)
        B, S, D, F, E = (4, 256, 128, 512, 8)
        return {'x': jax.random.normal(ks[0], (B, S, D), dtype=jnp.float32), 'centroids': jax.random.normal(ks[1], (E, D), dtype=jnp.float32) * 0.1, 'ln_g': jnp.ones((D,), dtype=jnp.float32), 'ln_b': jnp.zeros((D,), dtype=jnp.float32), 'w1': jax.random.normal(ks[2], (E, D, F), dtype=jnp.float32) * 0.02, 'b1': jnp.zeros((E, F), dtype=jnp.float32), 'w2': jax.random.normal(ks[3], (E, F, D), dtype=jnp.float32) * 0.02, 'b2': jnp.zeros((E, D), dtype=jnp.float32)}
    _L1_ffn_all = _L1_ffn_setup()
    _L1_ffn_in = {k: v for k, v in _L1_ffn_all.items() if k in ('centroids', 'ln_g', 'ln_b', 'w1', 'b1', 'w2', 'b2')}
    del _L1_ffn_all
    return {'x': x, 'ctx_1024': ctx_1024, 'mask_1x1xSxS2_ik0': mask_1x1xSxS2_ik0, 'L0_xattn_wq_w': _L0_xattn_in['wq_w'], 'L0_xattn_wq_b': _L0_xattn_in['wq_b'], 'L0_xattn_wk_w': _L0_xattn_in['wk_w'], 'L0_xattn_wk_b': _L0_xattn_in['wk_b'], 'L0_xattn_wv_w': _L0_xattn_in['wv_w'], 'L0_xattn_wv_b': _L0_xattn_in['wv_b'], 'L0_xattn_out_w': _L0_xattn_in['out_w'], 'L0_xattn_out_b': _L0_xattn_in['out_b'], 'L0_ffn_router_w': _L0_ffn_in['router_w'], 'L0_ffn_router_b': _L0_ffn_in['router_b'], 'L0_ffn_w1': _L0_ffn_in['w1'], 'L0_ffn_b1': _L0_ffn_in['b1'], 'L0_ffn_w2': _L0_ffn_in['w2'], 'L0_ffn_b2': _L0_ffn_in['b2'], 'L1_xattn_w_q': _L1_xattn_in['w_q'], 'L1_xattn_b_q': _L1_xattn_in['b_q'], 'L1_xattn_w_k': _L1_xattn_in['w_k'], 'L1_xattn_b_k': _L1_xattn_in['b_k'], 'L1_xattn_w_v': _L1_xattn_in['w_v'], 'L1_xattn_b_v': _L1_xattn_in['b_v'], 'L1_xattn_w_o': _L1_xattn_in['w_o'], 'L1_xattn_b_o': _L1_xattn_in['b_o'], 'L1_ffn_centroids': _L1_ffn_in['centroids'], 'L1_ffn_ln_g': _L1_ffn_in['ln_g'], 'L1_ffn_ln_b': _L1_ffn_in['ln_b'], 'L1_ffn_w1': _L1_ffn_in['w1'], 'L1_ffn_b1': _L1_ffn_in['b1'], 'L1_ffn_w2': _L1_ffn_in['w2'], 'L1_ffn_b2': _L1_ffn_in['b2']}

def reference(x, ctx_1024, mask_1x1xSxS2_ik0, L0_xattn_wq_w, L0_xattn_wq_b, L0_xattn_wk_w, L0_xattn_wk_b, L0_xattn_wv_w, L0_xattn_wv_b, L0_xattn_out_w, L0_xattn_out_b, L0_ffn_router_w, L0_ffn_router_b, L0_ffn_w1, L0_ffn_b1, L0_ffn_w2, L0_ffn_b2, L1_xattn_w_q, L1_xattn_b_q, L1_xattn_w_k, L1_xattn_b_k, L1_xattn_w_v, L1_xattn_b_v, L1_xattn_w_o, L1_xattn_b_o, L1_ffn_centroids, L1_ffn_ln_g, L1_ffn_ln_b, L1_ffn_w1, L1_ffn_b1, L1_ffn_w2, L1_ffn_b2):
    import jax
    import jax.numpy as jnp

    def _L0_xattn_ref(q, k, v, mask, wq_w, wq_b, wk_w, wk_b, wv_w, wv_b, out_w, out_b):
        import math
        import jax, jax.numpy as jnp
        import numpy as np
        N_HEAD = 16

        def _slopes(n_head):
            cp2 = 2 ** int(math.floor(math.log2(n_head)))
            slopes = 0.5 ** np.arange(1, cp2 + 1)
            if cp2 < n_head:
                intra = 1.0 / math.sqrt(2.0)
                pair = intra ** np.arange(1, 1 + 2 * (n_head - cp2), 2)
                slopes = np.sort(np.concatenate([slopes, pair]))[::-1]
            return jnp.asarray(slopes, dtype=jnp.float32)

        def _alibi_bias(S):
            d = jnp.arange(S)[:, None] - jnp.arange(S)[None, :]
            return -jnp.maximum(d, 0).astype(jnp.float32)
        B, S, D = q.shape
        H = N_HEAD
        hd = D // H
        lin = lambda x, w, b: x @ w.T + b
        split = lambda x: x.reshape(B, S, H, hd).transpose(0, 2, 1, 3)
        wq = split(lin(q, wq_w, wq_b))
        wk = split(lin(k, wk_w, wk_b))
        wv = split(lin(v, wv_w, wv_b))
        qk = jnp.einsum('bhsd,bhtd->bhst', wq, wk)
        alibi = _alibi_bias(S)[None, :, :] * _slopes(H)[:, None, None]
        attn = qk + alibi[None]
        attn = jnp.where(mask == 0, jnp.float32(-1000000000.0), attn)
        attn = jax.nn.softmax(attn, axis=-1)
        out = jnp.einsum('bhst,bhtd->bhsd', attn, wv)
        out = out.transpose(0, 2, 1, 3).reshape(B, S, D)
        return lin(out, out_w, out_b)

    def _L0_ffn_ref(x, router_w, router_b, w1, b1, w2, b2):
        import jax, jax.numpy as jnp
        import numpy as np
        B, S, HID, DFF, E, K = (4, 256, 128, 512, 8, 256)
        b, s, h = x.shape
        xf = x.reshape(-1, h)
        logits = xf @ router_w + router_b
        scores = jax.nn.softmax(logits, axis=-1)
        G, idx = jax.lax.top_k(scores.T, K)
        toks = xf[idx]
        h1 = jax.nn.relu(jnp.einsum('ekh,ehf->ekf', toks, w1) + b1[:, None, :])
        eo = jnp.einsum('ekf,efh->ekh', h1, w2) + b2[:, None, :]
        contrib = (eo * G[..., None]).reshape(-1, h)
        y = jnp.zeros_like(xf).at[idx.reshape(-1)].add(contrib)
        return y.reshape(b, s, h)

    def _L1_xattn_ref(Q, K, V, w_q, b_q, w_k, b_k, w_v, b_v, w_o, b_o):
        import jax, jax.numpy as jnp
        import numpy as np
        D_MODEL = 128
        NUM_HEADS = 16

        def _split_heads(x, n_heads):
            B, L, D = x.shape
            return x.reshape(B, L, n_heads, D // n_heads).transpose(0, 2, 1, 3)
        H = NUM_HEADS
        q = _split_heads(Q @ w_q.T + b_q, H)
        k = _split_heads(K @ w_k.T + b_k, H)
        v = _split_heads(V @ w_v.T + b_v, H)
        d_h = q.shape[-1]
        scores = jnp.einsum('bhqd,bhkd->bhqk', q, k) / jnp.sqrt(jnp.float32(d_h))
        attn = jax.nn.softmax(scores, axis=-1)
        out = jnp.einsum('bhqk,bhkd->bhqd', attn, v)
        B, _, L, _ = out.shape
        out = out.transpose(0, 2, 1, 3).reshape(B, L, H * d_h)
        return out @ w_o.T + b_o

    def _L1_ffn_ref(x, centroids, ln_g, ln_b, w1, b1, w2, b2):
        import jax, jax.numpy as jnp
        import numpy as np
        LN_EPS = 1e-05

        def layer_norm(x, g, b):
            mu = jnp.mean(x, axis=-1, keepdims=True)
            var = jnp.var(x, axis=-1, keepdims=True)
            return (x - mu) / jnp.sqrt(var + LN_EPS) * g + b

        def balanced_assignment(scores):
            T, E = scores.shape
            C = T // E
            taken = jnp.zeros((T,), dtype=bool)
            parts = []
            for e in range(E):
                s = jnp.where(taken, -jnp.inf, scores[:, e])
                _, idx = jax.lax.top_k(s, C)
                parts.append(idx)
                taken = taken.at[idx].set(True)
            return jnp.concatenate(parts)
        D = x.shape[-1]
        feat = x.reshape(-1, D)
        T = feat.shape[0]
        E = centroids.shape[0]
        C = T // E
        norm = layer_norm(feat, ln_g, ln_b)
        scores = jax.lax.stop_gradient(norm @ centroids.T)
        sort_by_expert = balanced_assignment(scores)
        routed = feat[sort_by_expert].reshape(E, C, D)
        h = layer_norm(routed, ln_g, ln_b)
        h = jax.nn.gelu(jnp.einsum('ecd,edf->ecf', h, w1) + b1[:, None, :])
        h = jnp.einsum('ecf,efd->ecd', h, w2) + b2[:, None, :]
        out = routed + h
        inv = jnp.zeros((T,), dtype=jnp.int32).at[sort_by_expert].set(jnp.arange(T, dtype=jnp.int32))
        return out.reshape(T, D)[inv].reshape(x.shape)
    x = x + _L0_xattn_ref(_layernorm(x, axis=-1), ctx_1024, ctx_1024, mask_1x1xSxS2_ik0, L0_xattn_wq_w, L0_xattn_wq_b, L0_xattn_wk_w, L0_xattn_wk_b, L0_xattn_wv_w, L0_xattn_wv_b, L0_xattn_out_w, L0_xattn_out_b)
    x = x + _L0_ffn_ref(_layernorm(x, axis=-1), L0_ffn_router_w, L0_ffn_router_b, L0_ffn_w1, L0_ffn_b1, L0_ffn_w2, L0_ffn_b2)
    x = x + _L1_xattn_ref(_layernorm(x, axis=-1), ctx_1024, ctx_1024, L1_xattn_w_q, L1_xattn_b_q, L1_xattn_w_k, L1_xattn_b_k, L1_xattn_w_v, L1_xattn_b_v, L1_xattn_w_o, L1_xattn_b_o)
    x = x + _L1_ffn_ref(_layernorm(x, axis=-1), L1_ffn_centroids, L1_ffn_ln_g, L1_ffn_ln_b, L1_ffn_w1, L1_ffn_b1, L1_ffn_w2, L1_ffn_b2)
    return x

_drawn_inputs = setup_inputs


def setup_inputs(seed=0):
    import zlib

    import numpy as np

    out = dict(_drawn_inputs(seed))
    spreads = {'L0_ffn_router_b': (0.0, 0.286),
     'L0_ffn_b1': (0.0, 0.306),
     'L0_ffn_b2': (0.0, 0.1),
     'L1_ffn_ln_g': (1.0, 0.2),
     'L1_ffn_ln_b': (0.0, 2.0),
     'L1_ffn_b1': (0.0, 0.71),
     'L1_ffn_b2': (0.0, 0.1)}
    factors = {'L0_xattn_wq_w': 6.119,
     'L0_xattn_wq_b': 8.0,
     'L0_xattn_wk_w': 6.466,
     'L0_xattn_wk_b': 64.0,
     'L0_xattn_wv_b': 6.107,
     'L1_xattn_b_q': 2.878,
     'L1_xattn_b_k': 64.0}
    for name, (base, spread) in spreads.items():
        noise = np.random.default_rng([zlib.crc32(name.encode()), seed]).standard_normal(out[name].shape)
        drawn = base * np.exp(spread * noise) if base else spread * noise
        out[name] = jnp.asarray(drawn.astype(out[name].dtype))
    for name, factor in factors.items():
        out[name] = (out[name] * factor).astype(out[name].dtype)
    return out
```

```python
from contextlib import ExitStack

import concourse.bass as bass
from concourse import mybir

F32 = mybir.dt.float32
BF16 = mybir.dt.bfloat16
I32 = mybir.dt.int32
ALU = mybir.AluOpType
ACT = mybir.ActivationFunctionType
AX = mybir.AxisListType

P = 128
B, S, D = 8, 256, 128
H, HD = 16, 8
NT = B * S // P
T = B * S
E = 8
CAP = T // E
F = 512
FC = F // P
PARTS = 3
PAIRS = PARTS * PARTS * HD
ROWS = PAIRS + PARTS
VW = HD + 1
CH = 512
NCH = T // CH
BIG = float(2 ** 47)
EPS = 1e-5
AUG = D + E
LOOK = [3, 3, 3, 3, 3, 1, 0, 0]


class Chain:

    def __init__(self, eng, sem):
        self.eng, self.sem, self.n = eng, sem, 0

    def link(self, ins):
        self.n += 1
        ins.then_inc(self.sem, 1)
        self.eng.wait_ge(self.sem, self.n)


class LoopChain:

    def __init__(self, eng, sem, it, per, start=0):
        self.eng, self.sem, self.it, self.per, self.n = eng, sem, it, per, start

    def link(self, ins):
        self.n += 1
        ins.then_inc(self.sem, 1)
        self.eng.wait_ge(self.sem, self.it * self.per + self.n)


def build(nc, a, out):
    ctx = ExitStack()
    with ctx:
        def sb(name, shape, dt=F32):
            return ctx.enter_context(nc.sbuf_tensor(name, shape, dt))

        def sem(name):
            return ctx.enter_context(nc.semaphore(name))

        def dram(name, shape, dt=F32):
            return nc.dram_tensor(name, shape, dt, kind="Internal").ap()

        ps = ctx.enter_context(nc.psum_tensor("ps", [P, 8, 512], F32))

        kimg = [dram(f"kimg{l}", [B * PARTS * HD, H * S], BF16) for l in range(2)]
        qimg = [dram(f"qimg{l}", [B * PARTS * HD, H * S], BF16) for l in range(2)]
        xaug = dram("xaug", [T, AUG])
        acc = dram("acc", [T, D])
        nsort = dram("nsort", [T, D])
        ysort = dram("ysort", [T, D])

        identf = sb("identf", [P, P])
        identb = sb("identb", [P, P], BF16)
        onesf = sb("onesf", [P, P])
        onesb = sb("onesb", [P, P], BF16)
        tri = sb("tri", [P, P], BF16)
        iotaf = sb("iotaf", [P, CAP])
        iotab = sb("iotab", [P, CAP], BF16)
        tokf = sb("tokf", [P, NT, 2])
        tokid = sb("tokid", [P, NT, 2], BF16)
        step0 = sb("step0", [P, 8, 3])
        step1 = sb("step1", [P, 4, 15])
        seg = sb("seg", [P, 2 * E, NT])
        ebase = sb("ebase", [P, E])
        diag = sb("diag", [P, H, P], BF16)
        dist = sb("dist", [P, 2, S])
        maski = sb("maski", [P, 2, S], I32)
        mz = sb("mz", [P, 2, S])
        rv = sb("rv", [P, 2])
        rvrep = sb("rvrep", [P, 2, P], BF16)
        rvrow = sb("rvrow", [P, 2, S])
        bias = sb("bias", [P, 2, S], BF16)
        biasT = sb("biasT", [P, 2, S], BF16)
        x = sb("x", [P, NT, D])
        xn = sb("xn", [P, NT, AUG])
        xT = sb("xT", [P, T])
        on = sb("on", [P, NT, D])
        cT = sb("cT", [P, T])
        wst = sb("wst", [P, 8, P])
        wT = sb("wT", [P, 8, P])
        bcol = sb("bcol", [P, 4])
        brow = sb("brow", [P, 4, P])
        v9 = [sb(f"v9_{l}", [P, NT, H, VW]) for l in range(2)]
        fbuf = sb("fbuf", [P, 2, CH])
        rbuf = sb("rbuf", [P, 2, CH])
        parts = sb("parts", [P, 3, PARTS, CH], BF16)
        qs = sb("qs", [P, 2, H * S], BF16)
        ks = sb("ks", [P, 2, H * S], BF16)
        pbuf = sb("pbuf", [P, 2, 1024])
        vb = sb("vb", [P, 2, 2 * H * VW])
        mx = sb("mx", [P, 2, 2 * H])
        m3 = sb("m3", [2 * H, 2, PARTS, P], BF16)
        mr = sb("mr", [2 * H, P])
        rec = sb("rec", [P, 2, 2 * H])
        stats = sb("stats", [P, NT, 6])
        mv = sb("mv", [P, NT, 2])
        ve_ = sb("ve_", [P, NT])
        sd = sb("sd", [P, NT])
        rs = sb("rs", [P, NT])
        t1 = sb("t1", [P, NT])
        rw = sb("rw", [P, E])
        rb = sb("rb", [P, E])
        cen = sb("cen", [E, P])
        cenT = sb("cenT", [P, E])
        lng = sb("lng", [P, P])
        lnb = sb("lnb", [P, P])
        b1r = sb("b1r", [E * FC, 2, P])
        b1T = sb("b1T", [P, 2, E * FC])
        b2 = sb("b2", [P, 2, E * D])
        lg = sb("lg", [P, NT, E])
        lmx = sb("lmx", [P, NT])
        keyi = sb("keyi", [P, NT, E], I32)
        keym = sb("keym", [P, NT, E], I32)
        hi = sb("hi", [P, E, NT])
        lo = sb("lo", [P, E, NT])
        cmpb = sb("cmpb", [P, 384], BF16)
        cnt = sb("cnt", [P, 24], BF16)
        thr = sb("thr", [P, 24])
        cst = sb("cst", [P, 24])
        sat = sb("sat", [P, 24])
        nsat = sb("nsat", [P, E])
        base = sb("base", [P, E])
        v2 = sb("v2", [P, E, NT])
        dif = sb("dif", [P, E, NT])
        ge = sb("ge", [P, 2, E, NT], BF16)
        pre = sb("pre", [P, 2, E, NT])
        scn = sb("scn", [P, 2, E, NT])
        er = sb("er", [P, E, NT])
        sel = sb("sel", [P, E, NT])
        pos = sb("pos", [P, E, NT])
        avail = sb("avail", [P, NT])
        hie = sb("hie", [P, NT])
        place = sb("place", [P, NT])
        placei = sb("placei", [P, NT], I32)
        oh = qs[:].rearrange("p a b -> p (a b)").rearrange("p (a i c) -> p a i c", a=2, i=NT)
        idx = sb("idx", [P, 2 * E], I32)
        w1 = sb("w1", [P, E, F])
        w2 = sb("w2", [P, E * FC, D])
        gt = ks[:].rearrange("p a b -> p (a b)")[:, 0:4 * E * AUG].bitcast(F32).rearrange(
            "p (c d) -> p c d", d=AUG)
        xg = sb("xg", [P, 2, CAP])
        hb = pbuf[:].rearrange("p a (c s) -> p a c s", c=FC)
        yb = cT[:].rearrange("p (c d) -> p c d", d=D)

        ld = {n: sem("ld_" + n) for n in ("ctx", "x", "w", "small", "ffn0", "ffn1")}
        pool_const = sem("pool_const")
        pool_own = sem("pool_own")
        dve_own = sem("dve_own")
        act_own = sem("act_own")
        phase = sem("phase")
        filled = sem("filled")
        drained = sem("drained")
        v_full = sem("v_full")
        v_free = sem("v_free")
        f_ready = sem("f_ready")
        p1_ready = sem("p1_ready")
        r_ready = sem("r_ready")
        p2_ready = sem("p2_ready")
        p3_ready = sem("p3_ready")
        img_written = [sem(f"img_written{i}") for i in range(3)]
        rv_ready = sem("rv_ready")
        ps_rv = sem("ps_rv")
        bias_ready = sem("bias_ready")
        ln_done = sem("ln_done")
        var_ready = sem("var_ready")
        sd_ready = sem("sd_ready")
        x_moved = sem("x_moved")
        out_full = sem("out_full")
        lg_full = sem("lg_full")
        lg_shift = sem("lg_shift")
        lg_exp = sem("lg_exp")
        sc_ready = sem("sc_ready")
        aug_out = sem("aug_out")
        cnt_ready = [sem(f"cnt_ready{l}") for l in range(2)]
        tot_ready = [sem(f"tot_ready{l}") for l in range(2)]
        loop_own = {n: sem("own_" + n) for n in ("oh", "route1")}
        oh_ready = sem("oh_ready")
        idx_full = sem("idx_full")
        idx_ready = sem("idx_ready")
        row_got = [sem(f"row_got{e}") for e in range(E)]
        xg_full = sem("xg_full")
        xg_ready = sem("xg_ready")
        h_full = sem("h_full")
        h_ready = sem("h_ready")
        y_full = sem("y_full")
        y_ready = sem("y_ready")
        added = sem("added")
        place_ready = sem("place_ready")
        rows_sorted = sem("rows_sorted")
        rows_loaded = sem("rows_loaded")
        y_stored = sem("y_stored")
        y_back = sem("y_back")
        out_ready = sem("out_ready")
        stored = sem("stored")
        at = [{n: sem(f"{n}{l}") for n in
               ("stk00", "stk01", "stk10", "stk11", "vcopy", "mx_ps", "mx_red", "mxT", "mx_split",
                "mrow0", "mrow1", "st_ps", "exp_done", "pv_done", "o_norm", "own_split")}
              for l in range(2)]

        def dview(ap, i=None):
            return ap.rearrange("b s d -> (b s) d").rearrange("(i p) d -> p i d", p=P)

        names = [["L0_xattn_wq_w", "L0_xattn_wk_w", "L0_xattn_wv_w", "L0_xattn_out_w"],
                 ["L1_xattn_w_q", "L1_xattn_w_k", "L1_xattn_w_v", "L1_xattn_w_o"]]
        bnames = [["L0_xattn_wq_b", "L0_xattn_wk_b", "L0_xattn_wv_b", "L0_xattn_out_b"],
                  ["L1_xattn_b_q", "L1_xattn_b_k", "L1_xattn_b_v", "L1_xattn_b_o"]]
        N_SMALL = 9 + 4 + 4

        block = ctx.enter_context(nc.Block())
        phases = {}

        def meet(eng):
            phases[eng] = phases.get(eng, 0) + 1
            eng.drain().then_inc(phase, 1)
            eng.wait_ge(phase, 5 * phases[eng])

        def bcast(ap, n):
            return ap.unsqueeze(0).to_broadcast([P, n])

        @block.sync
        def _(sp):
            for half in range(2):
                sp.dma_start(on[:, 8 * half:8 * half + 8, :],
                             dview(a["ctx_1024"])[:, 8 * half:8 * half + 8, :]).then_inc(ld["ctx"], 16)
            for l in range(2):
                for j in range(4):
                    sp.dma_start(wst[:, 4 * l + j, :], a[names[l][j]]).then_inc(ld["w"], 16)
            for half in range(2):
                sp.dma_start(x[:, 8 * half:8 * half + 8, :],
                             dview(a["x"])[:, 8 * half:8 * half + 8, :]).then_inc(ld["x"], 16)
            small = []
            for l in range(2):
                for j in range(2):
                    small.append((bcol[:, 2 * l + j:2 * l + j + 1], a[bnames[l][j]].unsqueeze(1)))
                    small.append((brow[:, 2 * l + j, :], bcast(a[bnames[l][2 + j]], P)))
            small += [(maski[:], a["mask_1x1xSxS2_ik0"].rearrange("a b s t -> (a b s) t")
                       .rearrange("(i p) t -> p i t", p=P)),
                      (rw[:], a["L0_ffn_router_w"]),
                      (rb[:], bcast(a["L0_ffn_router_b"], E)),
                      (cen[:], a["L1_ffn_centroids"]),
                      (lng[:], bcast(a["L1_ffn_ln_g"], P)),
                      (lnb[:], bcast(a["L1_ffn_ln_b"], P))]
            for l in range(2):
                small.append((b1r[:, l, :], a[f"L{l}_ffn_b1"].rearrange("e (c p) -> (e c) p", p=P)))
            small.append((b2[:, 0, :], bcast(a["L0_ffn_b2"].rearrange("e d -> (e d)"), E * D)))
            assert len(small) == N_SMALL
            for dst, src in small:
                sp.dma_start(dst, src).then_inc(ld["small"], 16)
            sp.dma_start(b2[:, 1, :], bcast(a["L1_ffn_b2"].rearrange("e d -> (e d)"), E * D)
                         ).then_inc(ld["ffn0"], 16)
            sp.dma_start(w1[:], a["L0_ffn_w1"].rearrange("e d f -> d e f")).then_inc(ld["ffn0"], 16)
            sp.dma_start(w2[:], a["L0_ffn_w2"].rearrange("e f d -> (e f) d")
                         .rearrange("(c p) d -> p c d", p=P)).then_inc(ld["ffn0"], 16)

            def write_images(first, imgs):
                for n in range(first, first + NCH * len(imgs)):
                    img = imgs[(n - first) // NCH]
                    c = n % NCH
                    sp.wait_ge(p3_ready, n + 1)
                    for bb in range(2):
                        for i in range(PARTS):
                            row = ((2 * c + bb) * PARTS + i) * HD
                            sp.dma_start(img[row:row + HD, :].rearrange("d (h s) -> h d s", h=H),
                                         parts[:, n % 3, i, bb * S:bb * S + S]
                                         ).then_inc(img_written[n % 3], 16)
                for n in range(first + NCH * len(imgs) - 3, first + NCH * len(imgs)):
                    sp.wait_ge(img_written[n % 3], 96 * (n // 3 + 1))

            def load_stack(l, b, par, half, it=None):
                cols = slice(half * 2048, half * 2048 + 2048)
                s = at[l][f"stk{par}{half}"]
                r0 = b * (PARTS * HD)
                for pa in range(PARTS):
                    rows = slice(pa * 24, pa * 24 + 24)
                    sp.dma_start(qs[rows, par, cols], qimg[l][bass.ds(r0, 24), cols]).then_inc(s, 16)
                    for pc in range(PARTS):
                        k0 = pa * 24 + pc * HD
                        sp.dma_start(ks[k0:k0 + HD, par, cols],
                                     kimg[l][bass.ds(r0 + pa * HD, HD), cols]).then_inc(s, 16)

            def max_rows(l, par):
                for i in range(PARTS):
                    sp.dma_start(qs[PAIRS + i:PAIRS + i + 1, par, :], m3[:, par, i, :]
                                 ).then_inc(at[l][f"mrow{par}"], 16)

            def attention(l):
                A = at[l]
                for b in range(2):
                    for half in range(2):
                        load_stack(l, b, b, half)
                sp.wait_ge(A["mx_split"], 1)
                max_rows(l, 0)
                with sp.Fori(0, B // 2 - 1) as it:
                    for par in range(2):
                        b = sp.snap(it * 2 + (par + 2))
                        v4 = sp.snap(it * 16 + (8 * par + 4))
                        v8 = sp.snap(it * 16 + (8 * par + 8))
                        vs = sp.snap(it * 2 + (par + 2))
                        sp.wait_ge(A["st_ps"], v4)
                        load_stack(l, b, par, 0)
                        sp.wait_ge(A["mx_split"], vs)
                        max_rows(l, 1 - par)
                        sp.wait_ge(A["st_ps"], v8)
                        load_stack(l, b, par, 1)
                sp.wait_ge(A["mx_split"], B)
                max_rows(l, 1)

            write_images(0, [kimg[0], kimg[1], qimg[0]])
            meet(sp)
            attention(0)
            meet(sp)
            meet(sp)
            sp.dma_start(acc.rearrange("(i p) d -> p i d", p=P), x[:]).then_inc(x_moved, 16)
            sp.wait_ge(sc_ready, 1)
            sp.dma_start(xaug.rearrange("(i p) c -> p i c", p=P), xn[:]).then_inc(aug_out, 16)
            sp.wait_ge(x_moved, 16)
            meet(sp)
            meet(sp)
            sp.dma_start(x[:], acc.rearrange("(i p) d -> p i d", p=P)).then_inc(x_moved, 16)
            sp.dma_start(w1[:], a["L1_ffn_w1"].rearrange("e d f -> d e f")).then_inc(ld["ffn1"], 16)
            sp.dma_start(w2[:], a["L1_ffn_w2"].rearrange("e f d -> (e f) d")
                         .rearrange("(c p) d -> p c d", p=P)).then_inc(ld["ffn1"], 16)
            write_images(12, [qimg[1]])
            meet(sp)
            attention(1)
            meet(sp)
            meet(sp)
            meet(sp)
            sp.wait_ge(rows_sorted, 16 * NT)
            sp.dma_start(gt[:, :, 0:D], nsort.rearrange("(c p) d -> p c d", p=P)
                         ).then_inc(rows_loaded, 16)
            for e in range(E):
                sp.wait_ge(y_ready, E + e + 1)
                sp.dma_start(ysort[e * CAP:(e + 1) * CAP, :].rearrange("(c p) d -> p c d", p=P),
                             yb[:, 2 * e:2 * e + 2, :]).then_inc(y_stored, 16)
            for half in range(2):
                sp.wait_ge(out_ready, half + 1)
                sp.dma_start(dview(out)[:, 8 * half:8 * half + 8, :],
                             x[:, 8 * half:8 * half + 8, :]).then_inc(stored, 16)
            sp.wait_ge(stored, 32)

        @block.tensor
        def _(pe):
            ring = [0]

            def fill(instructions):
                n = ring[0]
                ring[0] += 1
                if n >= 6:
                    pe.wait_ge(drained, n - 5)
                for f in instructions:
                    last = f(ps[:, n % 6, :])
                last.then_inc(filled, 1)

            def tiles(src, lo_, n=4, width=P):
                return [lambda bank, j=j: pe.transpose(bank[:, j * P:j * P + P], src(lo_ + j), identf[:])
                        for j in range(n)]

            def project(w, srcT, c):
                return [lambda bank: pe.matmul(bank, wT[:, w, :], srcT[:, c * CH:c * CH + CH],
                                               start=True, stop=True)]

            def transpose_x():
                for c in range(4):
                    fill(tiles(lambda i: xn[:, i, 0:D], 4 * c))

            pe.wait_ge(pool_const, 1)
            pe.wait_ge(ld["w"], 16 * 8)
            for l in range(2):
                fill(tiles(lambda j: wst[:, j, :], 4 * l))
            pe.wait_ge(ld["ctx"], 32)
            for c in range(4):
                fill(tiles(lambda i: on[:, i, :], 4 * c))
            pe.wait_ge(ld["small"], 16 * N_SMALL)
            fill([lambda bank: pe.transpose(bank[:, 0:E], cen[:], identf[0:E, 0:E])]
                 + [lambda bank, l=l: pe.transpose(bank[:, 32 + 32 * l:64 + 32 * l], b1r[:, l, :],
                                                   identf[0:32, 0:32]) for l in range(2)])
            pe.wait_ge(drained, 6)
            for l in range(2):
                for q in range(4):
                    fill(project(4 * l + 1, cT, q))
                    n = 4 * l + q
                    if n >= 1:
                        pe.wait_ge(v_free, n)
                    for j in range(4):
                        i = 4 * q + j
                        mm = pe.matmul(ps[:, 6, j * P:j * P + P], cT[:, i * P:i * P + P],
                                       wT[:, 4 * l + 2, :], start=True, stop=True)
                    mm.then_inc(v_full, 1)
            pe.wait_ge(rv_ready, 1)
            for st in range(2):
                pe.matmul(ps[:, 7, st * P:st * P + P], rvrep[:, st, :], identb[:], start=True, stop=True)
            pb = ps[:, 7, 256:512].bitcast(BF16)
            for st in range(2):
                for tt in range(2):
                    mm = pe.transpose(pb[:, tt * S + st * P:tt * S + st * P + P],
                                      bias[:, st, tt * P:tt * P + P], identb[:])
            mm.then_inc(ps_rv, 1)
            pe.wait_ge(ln_done, 1)
            transpose_x()
            pe.wait_ge(drained, ring[0])
            for c in range(NCH):
                fill(project(0, xT, c))
            meet(pe)

            def attention(l):
                A = at[l]

                def value(it, per, c):
                    return c if it is None else it * per + c

                def max_head(it, b2_, par, h):
                    m = 16 * b2_ + h
                    if it is not None or m >= 2:
                        pe.wait_ge(A["mx_red"], value(it, 32, m - 1))
                    if h % 8 == 0:
                        pe.wait_ge(A[f"stk{par}{h // 8}"], value(it, 192, 192 * (b2_ // 2 + 1)))
                    bank = ps[:, h % 2, :]
                    for st in range(2):
                        o = bank[:, st * S:st * S + S]
                        mm = pe.matmul(o, qs[0:PAIRS, par, h * S + st * P:h * S + st * P + P],
                                       ks[0:PAIRS, par, h * S:h * S + S], start=True, stop=l == 1)
                        if l == 0:
                            mm = pe.matmul(o, diag[:, h, :], bias[:, st, :], start=False, stop=True)
                    mm.then_inc(A["mx_ps"], 1)

                def scores(it, b2_, par, g):
                    u = 8 * b2_ + g
                    if it is not None or u >= 2:
                        pe.wait_ge(A["exp_done"], value(it, 16, u - 1))
                    if g == 0:
                        pe.wait_ge(A[f"mrow{par}"], value(it, 48, 48 * (b2_ // 2 + 1)))
                    for hh in range(2):
                        h = 2 * g + hh
                        for tt in range(2):
                            o = ps[:, 2 + 2 * (g % 2) + hh, tt * S:tt * S + S]
                            mm = pe.matmul(o, ks[0:ROWS, par, h * S + tt * P:h * S + tt * P + P],
                                           qs[0:ROWS, par, h * S:h * S + S], start=True, stop=l == 1)
                            if l == 0:
                                mm = pe.matmul(o, diag[:, h, :], biasT[:, tt, :], start=False, stop=True)
                    mm.then_inc(A["st_ps"], 1)

                def values(it, b2_, par, g):
                    u = 8 * b2_ + g
                    pe.wait_ge(A["exp_done"], value(it, 16, u + 1))
                    if g == 0:
                        pe.wait_ge(A["vcopy"], value(it, 2, b2_ + 1))
                        if it is not None or b2_ >= 2:
                            pe.wait_ge(A["o_norm"], value(it, 4, 2 * (b2_ - 1)))
                    for hh in range(2):
                        h = 2 * g + hh
                        for st in range(2):
                            for tt in range(2):
                                p0 = hh * 512 + tt * S + st * P
                                mm = pe.matmul(
                                    ps[:, 6 + par, (st * H + h) * VW:(st * H + h + 1) * VW],
                                    pbuf[:, g % 2, p0:p0 + P],
                                    vb[:, par, (tt * H + h) * VW:(tt * H + h + 1) * VW],
                                    start=tt == 0, stop=tt == 1)
                    mm.then_inc(A["pv_done"], 1)

                def turn_maxima(it, b2_, par):
                    pe.wait_ge(A["mx_red"], value(it, 32, 16 * (b2_ + 1)))
                    if it is not None or b2_ >= 2:
                        pe.wait_ge(A["mx_split"], value(it, 2, b2_ - 1))
                        pe.wait_ge(A["o_norm"], value(it, 4, 2 * (b2_ - 1)))
                    pe.transpose(ps[0:2 * H, 6 + par, 2 * H * VW:2 * H * VW + P], mx[:, par, :],
                                 identf[:]).then_inc(A["mxT"], 1)

                def batch(it, b2_, par, ahead):
                    h = 0
                    for g in range(H // 2):
                        if ahead:
                            for _ in range(LOOK[g]):
                                max_head(it, b2_ + 1, 1 - par, h)
                                h += 1
                        scores(it, b2_, par, g)
                        if ahead and g == 6:
                            turn_maxima(it, b2_ + 1, 1 - par)
                        if g >= 1:
                            values(it, b2_, par, g - 1)
                    values(it, b2_, par, H // 2 - 1)

                for h in range(H):
                    max_head(None, 0, 0, h)
                turn_maxima(None, 0, 0)
                batch(None, 0, 0, True)
                with pe.Fori(0, B // 2 - 1) as it:
                    batch(it, 1, 1, True)
                    batch(it, 2, 0, True)
                batch(None, B - 1, 1, False)

            def project_out(l):
                for c in range(4):
                    fill(tiles(lambda i: on[:, i, :], 4 * c))
                for c in range(4):
                    pe.wait_ge(drained, ring[0] - 3 + c)
                    if c >= 2:
                        pe.wait_ge(v_free, 8 + 4 * l + c - 1)
                    for j in range(4):
                        i = 4 * c + j
                        mm = pe.matmul(ps[:, 6 + c % 2, j * P:j * P + P], xT[:, i * P:i * P + P],
                                       wT[:, 4 * l + 3, :], start=True, stop=True)
                    mm.then_inc(out_full, 1)

            def logits(rhs, n):
                pe.wait_ge(drained, ring[0])
                for i in range(NT):
                    mm = pe.matmul(ps[:, 6, i * E:(i + 1) * E], xT[:, i * P:i * P + P], rhs,
                                   start=True, stop=True)
                mm.then_inc(lg_full, 1)

            def ffn(l):
                def rows_in(e):
                    if l == 0:
                        pe.wait_ge(row_got[e], 32)
                    elif e == 0:
                        pe.wait_ge(rows_loaded, 16)
                    n = 8 * l + e
                    if n >= 2:
                        pe.wait_ge(xg_ready, n - 1)
                    for half in range(2):
                        mm = pe.transpose(ps[:, e % 2, half * P:half * P + P],
                                          gt[:, 2 * e + half, 0:D], identf[:])
                    mm.then_inc(xg_full, 1)

                def hidden(e):
                    n = 8 * l + e
                    pe.wait_ge(xg_ready, n + 1)
                    if e == 0:
                        pe.wait_ge(ld[f"ffn{l}"], [48, 32][l])
                    if n >= 2:
                        pe.wait_ge(h_ready, 4 * (n - 1))
                    for c in range(FC):
                        mm = pe.matmul(ps[:, 2 + 2 * (e % 2) + c // 2,
                                          (c % 2) * CAP:(c % 2) * CAP + CAP],
                                       w1[:, e, c * P:c * P + P], xg[:, e % 2, :],
                                       start=True, stop=True)
                        if c % 2 == 1:
                            mm.then_inc(h_full, 1)

                def outputs(e):
                    n = 8 * l + e
                    pe.wait_ge(h_ready, 4 * (n + 1))
                    if n >= 2:
                        pe.wait_ge(y_ready, n - 1)
                    for half in range(2):
                        for c in range(FC):
                            mm = pe.matmul(ps[:, 6 + e % 2, half * D:half * D + D],
                                           hb[:, e % 2, c, half * P:half * P + P],
                                           w2[:, e * FC + c, :], start=c == 0, stop=c == FC - 1)
                    mm.then_inc(y_full, 1)

                for e in range(E):
                    rows_in(e)
                    hidden(e)
                    if e >= 1:
                        outputs(e - 1)
                outputs(E - 1)

            attention(0)
            meet(pe)
            project_out(0)
            meet(pe)
            pe.wait_ge(ln_done, 2)
            transpose_x()
            logits(rw[:], 1)
            for r in range(16):
                pe.wait_ge(cnt_ready[0], r + 1)
                pe.matmul(ps[:, 7, 0:24], onesb[:], cnt[:], start=True, stop=True
                          ).then_inc(tot_ready[0], 1)
            pe.wait_ge(cnt_ready[0], 17)
            flat = ge[:].rearrange("p g e i -> p (g e i)")
            pe.matmul(ps[:, 0, 0:256], tri[:], flat, start=True, stop=True)
            pe.matmul(ps[:, 0, 256:512], onesb[:], flat, start=True, stop=True).then_inc(tot_ready[0], 1)
            with pe.Fori(0, E // 2) as it:
                for par in range(2):
                    pe.wait_ge(oh_ready, it * 2 + (par + 1))
                    for half in range(2):
                        for i in range(NT):
                            mm = pe.matmul(ps[:, 1 + par, 2 * half:2 * half + 2],
                                           oh[:, par, i, half * P:half * P + P], tokid[:, i, :],
                                           start=i == 0, stop=i == NT - 1)
                    mm.then_inc(idx_full, 1)
            meet(pe)
            ffn(0)
            meet(pe)
            pe.wait_ge(ln_done, 3)
            transpose_x()
            pe.wait_ge(drained, ring[0])
            for c in range(NCH):
                fill(project(4, xT, c))
            meet(pe)
            attention(1)
            meet(pe)
            project_out(1)
            meet(pe)
            pe.wait_ge(ln_done, 4)
            transpose_x()
            logits(cenT[:], 2)
            with pe.Fori(0, E) as it:
                for r in range(8):
                    pe.wait_ge(cnt_ready[1], it * 9 + (r + 1))
                    pe.matmul(ps[:, 7, 0:15], onesb[:], cnt[:, 0:15], start=True, stop=True
                              ).then_inc(tot_ready[1], 1)
                pe.wait_ge(cnt_ready[1], it * 9 + 9)
                pe.matmul(ps[:, 0, 0:32], tri[:], ge[:, :, 0, :], start=True, stop=True)
                pe.matmul(ps[:, 0, 32:64], onesb[:], ge[:, :, 0, :], start=True, stop=True
                          ).then_inc(tot_ready[1], 1)
            meet(pe)
            ffn(1)

        @block.scalar
        def _(act):
            ring = [0]

            def drain(dst, bias_=None, wait=None):
                n = ring[0]
                ring[0] += 1
                act.wait_ge(filled, n + 1)
                if wait:
                    act.wait_ge(*wait)
                src = ps[:, n % 6, 0:dst.shape[-1]]
                if bias_ is None:
                    return act.copy(dst, src)
                return act.activation(dst, src, ACT.Identity, bias=bias_, scale=1.0)

            def drain_x():
                for c in range(4):
                    drain(xT[:, c * CH:c * CH + CH]).then_inc(drained, 1)

            def chunk(n, bias_):
                wait = (r_ready, n - 1) if n >= 2 else None
                ins = drain(fbuf[:, n % 2, :], bias_, wait)
                ins.then_inc(drained, 1)
                act.wait_ge(drained, ring[0])
                act.sem_inc(f_ready, 1)

            for l in range(2):
                drain(wT[:, 4 * l:4 * l + 4, :].rearrange("p a b -> p (a b)")).then_inc(drained, 1)
            for c in range(4):
                drain(cT[:, c * CH:c * CH + CH]).then_inc(drained, 1)
            n = ring[0]
            ring[0] += 1
            act.wait_ge(filled, n + 1)
            act.copy(cenT[:], ps[:, n % 6, 0:E])
            act.copy(b1T[:].rearrange("p l c -> p (l c)"), ps[:, n % 6, 32:96]).then_inc(drained, 1)
            act.wait_ge(var_ready, 1)
            act.activation(sd[:], ve_[:], ACT.Sqrt).then_inc(sd_ready, 1)
            for l in range(2):
                for c in range(NCH):
                    chunk(4 * l + c, bcol[:, 2 * l + 1:2 * l + 2])
            drain_x()
            for c in range(NCH):
                chunk(8 + c, bcol[:, 0:1])
            meet(act)

            def attention(l):
                A = at[l]
                scale = 1.0 if l == 0 else HD ** -0.5

                def pair(it, n):
                    act.wait_ge(A["st_ps"], n + 1 if it is None else it * 16 + (n + 1))
                    if it is not None or n >= 2:
                        act.wait_ge(A["pv_done"], n - 1 if it is None else it * 16 + (n - 1))
                    act.activation(pbuf[:, n % 2, :], ps[:, 2 + 2 * (n % 2):4 + 2 * (n % 2), :]
                                   .rearrange("p a b -> p (a b)"), ACT.Exp, bias=0.0, scale=scale
                                   ).then_inc(A["exp_done"], 1)

                for n in range(8):
                    pair(None, n)
                with act.Fori(0, B // 2 - 1) as it:
                    for n in range(8, 24):
                        pair(it, n)
                for n in range(8 * B - 8, 8 * B):
                    pair(None, n)

            def ffn(l):
                def hidden(e):
                    n = 8 * l + e
                    if n >= 2:
                        act.wait_ge(y_full, n - 1)
                    for c in range(FC):
                        act.wait_ge(h_full, 2 * n + c // 2 + 1)
                        act.activation(hb[:, e % 2, c, :],
                                       ps[:, 2 + 2 * (e % 2) + c // 2,
                                          (c % 2) * CAP:(c % 2) * CAP + CAP],
                                       [ACT.Relu, ACT.Gelu_apprx_tanh][l],
                                       bias=b1T[:, l, e * FC + c:e * FC + c + 1], scale=1.0
                                       ).then_inc(h_ready, 1)
                for e in range(E):
                    hidden(e)

            attention(0)
            meet(act)
            drain_x()
            meet(act)
            act.wait_ge(var_ready, 2)
            act.activation(sd[:], ve_[:], ACT.Sqrt).then_inc(sd_ready, 1)
            drain_x()
            act.wait_ge(lg_shift, 1)
            act.activation(lg[:], lg[:], ACT.Exp).then_inc(lg_exp, 1)
            meet(act)
            ffn(0)
            meet(act)
            act.wait_ge(var_ready, 3)
            act.activation(sd[:], ve_[:], ACT.Sqrt).then_inc(sd_ready, 1)
            drain_x()
            for c in range(NCH):
                chunk(12 + c, bcol[:, 2:3])
            meet(act)
            attention(1)
            meet(act)
            drain_x()
            meet(act)
            for r in range(2):
                act.wait_ge(var_ready, 4 + r)
                act.activation(sd[:], ve_[:], ACT.Sqrt).then_inc(sd_ready, 1)
            drain_x()
            meet(act)
            ffn(1)

        @block.vector
        def _(ve):
            own = Chain(ve, dve_own)
            link = own.link
            norms = [0]

            def normalise(src, dst, last):
                for i in range(NT):
                    ins = ve.bn_stats(stats[:, i, :], src[:, i, :])
                link(ins)
                for i in range(NT):
                    ins = ve.bn_aggr(mv[:, i, :], stats[:, i, :])
                link(ins)
                n = norms[0] = norms[0] + 1
                ve.tensor_scalar(ve_[:], mv[:, :, 1], EPS, None, ALU.add).then_inc(var_ready, 1)
                ve.wait_ge(sd_ready, n)
                link(ve.reciprocal(rs[:], sd[:]))
                link(ve.tensor_tensor(t1[:], rs[:], rs[:], ALU.mult))
                link(ve.tensor_tensor(t1[:], t1[:], ve_[:], ALU.mult))
                link(ve.tensor_scalar(t1[:], t1[:], -0.5, 1.5, ALU.mult, ALU.add))
                link(ve.tensor_tensor(rs[:], rs[:], t1[:], ALU.mult))
                for i in range(NT):
                    ins = ve.tensor_scalar(dst[:, i, 0:D], src[:, i, :], mv[:, i, 0:1], rs[:, i:i + 1],
                                           ALU.subtract, ALU.mult)
                return ins

            def split_rest(n, masked):
                f, r = fbuf[:, n % 2, :], rbuf[:, n % 2, :]
                ve.wait_ge(p1_ready, n + 1)
                if n >= 2:
                    ve.wait_ge(p3_ready, n - 1)
                ve.tensor_tensor(r, f, parts[:, n % 3, 0, :], ALU.subtract).then_inc(r_ready, 1)
                ve.wait_ge(p2_ready, n + 1)
                ve.tensor_tensor(parts[:, n % 3, 2, :], r, parts[:, n % 3, 1, :], ALU.subtract
                                 ).then_inc(p3_ready, 1)

            ve.memset(ks[64:96, :, :], 1.0)
            ve.wait_ge(ld["small"], 16 * N_SMALL)
            ve.wait_ge(pool_const, 1)
            link(ve.tensor_scalar(mz[:], maski[:], 0, None, ALU.is_equal))
            link(ve.tensor_reduce(rv[:], mz[:], AX.X, ALU.min))
            link(ve.tensor_scalar(rv[:], rv[:], -1.0, 1.0, ALU.mult, ALU.add))
            link(ve.scalar_tensor_tensor(mz[:], mz[:], BIG, dist[:], ALU.mult, ALU.max))
            for st in range(2):
                ve.tensor_scalar(bias[:, st, :], mz[:, st, :], rv[:, st:st + 1], None, ALU.mult)
                ins = ve.tensor_scalar(rvrep[:, st, :], onesf[:], rv[:, st:st + 1], None, ALU.mult)
            ins.then_inc(rv_ready, 1)
            ve.wait_ge(ld["x"], 32)
            normalise(x, xn, True).then_inc(ln_done, 1)
            for l in range(2):
                ve.memset(v9[l][:, :, :, HD:VW], 1.0)
            for n in range(8):
                l, q = n // 4, n % 4
                ve.wait_ge(v_full, n + 1)
                ve.tensor_tensor(v9[l][:, 4 * q:4 * q + 4, :, 0:HD],
                                 ps[:, 6, :].rearrange("p (i h d) -> p i h d", i=4, h=H),
                                 brow[:, 2 * l, :].rearrange("p (h d) -> p h d", h=H).unsqueeze(1)
                                 .to_broadcast([P, 4, H, HD]), ALU.add).then_inc(v_free, 1)
                split_rest(n, False)
            ve.wait_ge(ps_rv, 1)
            ve.tensor_copy(rvrow[:, 0, :], ps[:, 7, 0:256])
            ve.tensor_copy(rvrow[:, 1, :], ps[:, 7, 0:256])
            link(ve.tensor_copy(biasT[:].rearrange("p a b -> p (a b)"), ps[:, 7, 256:512].bitcast(BF16)))
            for c in range(NCH):
                n = 8 + c
                ve.wait_ge(f_ready, n + 1)
                ve.tensor_tensor(fbuf[:, n % 2, :], fbuf[:, n % 2, :],
                                 rvrow[:].rearrange("p a b -> p (a b)"), ALU.mult).then_inc(bias_ready, 1)
                split_rest(n, True)
            meet(ve)

            def attention(l):
                A = at[l]

                def value(it, per, c):
                    return c if it is None else it * per + c

                def reduce_head(it, b2_, par, h):
                    ve.wait_ge(A["mx_ps"], value(it, 32, 16 * b2_ + h + 1))
                    ve.tensor_reduce(mx[:, par, 2 * h:2 * h + 2],
                                     ps[:, h % 2, :].rearrange("p (a b) -> p a b", a=2), AX.X,
                                     ALU.max, negate=True).then_inc(A["mx_red"], 1)

                def split_max(it, b2_, par):
                    ch = [4 * b2_]

                    def lk(ins):
                        ch[0] += 1
                        ins.then_inc(A["own_split"], 1)
                        ve.wait_ge(A["own_split"], value(it, 8, ch[0]))

                    src = ps[0:2 * H, 6 + par, 2 * H * VW:2 * H * VW + P]
                    ve.wait_ge(A["mxT"], value(it, 2, b2_ + 1))
                    if it is not None or b2_ >= 2:
                        ve.wait_ge(A[f"mrow{par}"], value(it, 48, 48 * (b2_ // 2)))
                    lk(ve.tensor_copy(m3[:, par, 0, :], src))
                    lk(ve.tensor_tensor(mr[:], src, m3[:, par, 0, :], ALU.subtract))
                    lk(ve.tensor_copy(m3[:, par, 1, :], mr[:]))
                    lk(ve.tensor_tensor(m3[:, par, 2, :], mr[:], m3[:, par, 1, :], ALU.subtract))
                    ve.sem_inc(A["mx_split"], 1)

                def normalise_rows(it, b2_, par):
                    ve.wait_ge(A["pv_done"], value(it, 16, 8 * (b2_ + 1)))
                    o = ps[:, 6 + par, 0:2 * H * VW].rearrange("p (i h d) -> p i h d", i=2, h=H)
                    r = rec[:, par, :].rearrange("p (i h) -> p i h", i=2)
                    if it is None:
                        dst = on[:, 2 * b2_:2 * b2_ + 2, :]
                    else:
                        dst = on[:, bass.ds(it * 4 + 2 * b2_, 2), :]
                    ins = ve.reciprocal(r, o[:, :, :, HD])
                    ins.then_inc(A["o_norm"], 1)
                    ve.wait_ge(A["o_norm"], value(it, 4, 2 * b2_ + 1))
                    ve.tensor_tensor(dst.rearrange("p i (h d) -> p i h d", h=H), o[:, :, :, 0:HD],
                                     r.unsqueeze(3).to_broadcast([P, 2, H, HD]), ALU.mult
                                     ).then_inc(A["o_norm"], 1)

                def batch(it, b2_, par, ahead):
                    if ahead:
                        for h in range(H):
                            reduce_head(it, b2_ + 1, 1 - par, h)
                        split_max(it, b2_ + 1, 1 - par)
                    normalise_rows(it, b2_, par)

                for h in range(H):
                    reduce_head(None, 0, 0, h)
                split_max(None, 0, 0)
                batch(None, 0, 0, True)
                with ve.Fori(0, B // 2 - 1) as it:
                    batch(it, 1, 1, True)
                    batch(it, 2, 0, True)
                batch(None, B - 1, 1, False)

            def project_out(l):
                for c in range(4):
                    ve.wait_ge(out_full, 4 * l + c + 1)
                    ve.tensor_tensor(x[:, 4 * c:4 * c + 4, :].rearrange("p a b -> p (a b)"),
                                     ps[:, 6 + c % 2, :],
                                     x[:, 4 * c:4 * c + 4, :].rearrange("p a b -> p (a b)"),
                                     ALU.add).then_inc(v_free, 1)

            def add_bias(l):
                ve.tensor_tensor(x[:], x[:], brow[:, 2 * l + 1, :].unsqueeze(1)
                                 .to_broadcast([P, NT, D]), ALU.add)

            def make_keys(link_, src):
                bits = src.bitcast(I32)
                link_(ve.tensor_scalar(keym[:], bits, 31, None, ALU.arith_shift_right))
                link_(ve.tensor_scalar(keym[:], keym[:], -2 ** 31, None, ALU.bitwise_or))
                link_(ve.tensor_tensor(keyi[:], bits, keym[:], ALU.bitwise_xor))
                link_(ve.tensor_scalar(keym[:], keyi[:], 16, None, ALU.logical_shift_right))
                ve.tensor_copy(hi[:].rearrange("p e i -> p i e"), keym[:])
                link_(ve.tensor_scalar(keyi[:], keyi[:], 65535, None, ALU.bitwise_and))
                link_(ve.tensor_copy(lo[:].rearrange("p e i -> p i e"), keyi[:]))

            def search(link_, data, n_e, bits_, steps, l, tot, value):
                J = 2 ** bits_ - 1
                rounds = 16 // bits_
                w = n_e * J
                bs = base[:, 0:n_e]
                th = thr[:, 0:w].rearrange("p (e j) -> p e j", e=n_e)
                cs = cst[:, 0:w].rearrange("p (e j) -> p e j", e=n_e)
                sa = sat[:, 0:w].rearrange("p (e j) -> p e j", e=n_e)
                ns = nsat[:, 0:n_e]
                cm = cmpb[:, 0:w * NT].rearrange("p (e j i) -> p e j i", e=n_e, j=J)
                ve.memset(bs, 0.0)
                link_(ve.tensor_copy(th, steps[:, 0, :].unsqueeze(1).to_broadcast([P, n_e, J])))
                for r in range(rounds):
                    step = float(2 ** (16 - bits_ * (r + 1)))
                    link_(ve.tensor_tensor(cm, data.unsqueeze(2).to_broadcast([P, n_e, J, NT]),
                                           th.unsqueeze(3).to_broadcast([P, n_e, J, NT]), ALU.is_ge))
                    with nc.allow_low_precision(reason="counts up to 16 are exact in bf16"):
                        ve.tensor_reduce(cnt[:, 0:w].rearrange("p (e j) -> p e j", e=n_e), cm, AX.X,
                                         ALU.add).then_inc(cnt_ready[l], 1)
                    if r + 1 < rounds:
                        link_(ve.tensor_tensor(cs, bs.unsqueeze(2).to_broadcast([P, n_e, J]),
                                               steps[:, r + 1, :].unsqueeze(1)
                                               .to_broadcast([P, n_e, J]), ALU.add))
                    tot[0] += 1
                    ve.wait_ge(tot_ready[l], value(tot[0]))
                    link_(ve.tensor_scalar(sat[:, 0:w], ps[:, 7, 0:w], float(CAP), None, ALU.is_ge))
                    link_(ve.tensor_reduce(ns, sa, AX.X, ALU.add))
                    if r + 1 < rounds:
                        ve.scalar_tensor_tensor(th, ns.unsqueeze(2).to_broadcast([P, n_e, J]), step,
                                                cs, ALU.mult, ALU.add)
                    link_(ve.scalar_tensor_tensor(bs, ns, step, bs, ALU.mult, ALU.add))

            def route(link_, hi_, lo_, n_e, bits_, steps, l, value):
                tot = [0]
                df, v_ = dif[:, 0:n_e, :], v2[:, 0:n_e, :]
                bs = base[:, 0:n_e]
                bcast_b = bs.unsqueeze(2).to_broadcast([P, n_e, NT])
                search(link_, hi_, n_e, bits_, steps, l, tot, value)
                link_(ve.tensor_tensor(df, hi_, bcast_b, ALU.subtract))
                link_(ve.scalar_tensor_tensor(v_, df, 65536.0, lo_, ALU.mult, ALU.add))
                search(link_, v_, n_e, bits_, steps, l, tot, value)
                g, q = ge[:, 0, 0:n_e, :], ge[:, 1, 0:n_e, :]
                ve.tensor_tensor(g, v_, bcast_b, ALU.is_gt)
                ve.tensor_tensor(q, v_, bcast_b, ALU.is_equal).then_inc(cnt_ready[l], 1)
                tot[0] += 1
                ve.wait_ge(tot_ready[l], value(tot[0]))
                w = 2 * n_e * NT
                view = dict(g=2, e=n_e)
                sc_ = scn[:, :, 0:n_e, :]
                pr_ = pre[:, :, 0:n_e, :]
                flat_s = scn[:].rearrange("p g e i -> p (g e i)")[:, 0:w]
                inside = ps[:, 0, 0:w].rearrange("p (g e i) -> p g e i", **view)
                whole = ps[:, 0, w:2 * w]
                flat_p = pre[:].rearrange("p g e i -> p (g e i)")[:, 0:w]
                link_(ve.tensor_tensor_scan(flat_s, seg[:].rearrange("p a i -> p (a i)")[:, 0:w],
                                            whole, 0.0, ALU.mult, ALU.add))
                link_(ve.tensor_tensor(flat_p, flat_s, whole, ALU.subtract))
                link_(ve.tensor_tensor(flat_p, flat_p, ps[:, 0, 0:w], ALU.add))
                sv = flat_s.rearrange("p (g e i) -> p g e i", **view)
                pv = flat_p.rearrange("p (g e i) -> p g e i", **view)
                er_, se_, po_ = er[:, 0:n_e, :], sel[:, 0:n_e, :], pos[:, 0:n_e, :]
                link_(ve.tensor_tensor(er_, pv[:, 1], sv[:, 0, :, NT - 1:NT]
                                       .to_broadcast([P, n_e, NT]), ALU.add))
                link_(ve.scalar_tensor_tensor(df, er_, float(CAP), q, ALU.is_lt, ALU.mult))
                ve.tensor_tensor(se_, g, df, ALU.add)
                link_(ve.tensor_tensor(er_, er_, df, ALU.mult))
                link_(ve.tensor_tensor(po_, pv[:, 0], g, ALU.mult))
                link_(ve.tensor_tensor(po_, po_, er_, ALU.add))

            def ffn(l):
                for e in range(E):
                    n = 8 * l + e
                    ve.wait_ge(xg_full, n + 1)
                    if n >= 2:
                        ve.wait_ge(h_full, 2 * (n - 1))
                    ve.tensor_copy(xg[:, e % 2, :], ps[:, e % 2, 0:CAP]).then_inc(xg_ready, 1)
                    if e >= 1:
                        finish(l, e - 1)
                finish(l, E - 1)

            def finish(l, e):
                n = 8 * l + e
                ve.wait_ge(y_full, n + 1)
                y = yb[:, 2 * e:2 * e + 2, :]
                bb = b2[:, l, e * D:(e + 1) * D].unsqueeze(1).to_broadcast([P, 2, D])
                ins = ve.tensor_tensor(y, ps[:, 6 + e % 2, 0:2 * D].rearrange("p (a b) -> p a b", a=2),
                                       bb, ALU.add)
                if l == 0:
                    link(ins)
                    ins = ve.tensor_tensor(y, y, gt[:, 2 * e:2 * e + 2, D + e:D + e + 1]
                                           .to_broadcast([P, 2, D]), ALU.mult)
                ins.then_inc(y_ready, 1)

            link(ve.tensor_tensor(x[:], x[:], brow[:, 1, :].unsqueeze(1).to_broadcast([P, NT, D]),
                                  ALU.add))
            attention(0)
            meet(ve)
            project_out(0)
            meet(ve)
            normalise(x, xn, True).then_inc(ln_done, 1)
            ve.wait_ge(lg_full, 1)
            link(ve.tensor_tensor(lg[:], ps[:, 6, 0:P].rearrange("p (i e) -> p i e", e=E),
                                  rb[:].unsqueeze(1).to_broadcast([P, NT, E]), ALU.add))
            link(ve.tensor_reduce(lmx[:], lg[:], AX.X, ALU.max))
            ve.tensor_tensor(lg[:], lg[:], lmx[:].unsqueeze(2).to_broadcast([P, NT, E]),
                             ALU.subtract).then_inc(lg_shift, 1)
            ve.wait_ge(lg_exp, 1)
            link(ve.tensor_reduce(lmx[:], lg[:], AX.X, ALU.add))
            link(ve.reciprocal(lmx[:], lmx[:]))
            link(ve.tensor_tensor(lg[:], lg[:], lmx[:].unsqueeze(2).to_broadcast([P, NT, E]), ALU.mult))
            ve.tensor_copy(xn[:, :, D:AUG], lg[:]).then_inc(sc_ready, 1)
            make_keys(link, lg[:])
            route(link, hi[:], lo[:], E, 2, step0, 0, lambda v: v)
            link(ve.scalar_tensor_tensor(pos[:], pos[:], 1.0, sel[:], ALU.add, ALU.mult))
            link(ve.tensor_scalar(pos[:], pos[:], -1.0, None, ALU.add))
            with ve.Fori(0, E // 2) as it:
                for par in range(2):
                    for i in range(NT):
                        ins = ve.tensor_scalar(oh[:, par, i, :], iotab[:],
                                               pos[:, bass.ds(it * 2 + par, 1), i], None, ALU.is_equal)
                    ins.then_inc(oh_ready, 1)
                    ve.wait_ge(idx_full, it * 2 + (par + 1))
                    ve.tensor_copy(sat[:, 4 * par:4 * par + 4], ps[:, 1 + par, 0:4]
                                   ).then_inc(loop_own["oh"], 1)
                    ve.wait_ge(loop_own["oh"], it * 2 + (par + 1))
                    ve.tensor_tensor(idx[:, bass.ds(it * 4 + 2 * par, 2)],
                                     sat[:, 4 * par:4 * par + 4:2], sat[:, 4 * par + 1:4 * par + 4:2],
                                     ALU.add).then_inc(idx_ready, 1)
            meet(ve)
            ffn(0)
            meet(ve)
            ve.wait_ge(x_moved, 32)
            normalise(x, xn, True).then_inc(ln_done, 1)
            ve.wait_ge(ln_done, 3)
            link(ve.tensor_tensor(x[:], x[:], brow[:, 3, :].unsqueeze(1).to_broadcast([P, NT, D]),
                                  ALU.add))
            ve.memset(ks[64:96, :, :], 1.0)
            for c in range(NCH):
                split_rest(12 + c, False)
            meet(ve)
            attention(1)
            meet(ve)
            project_out(1)
            meet(ve)
            link(normalise(x, xn, False))
            link(ve.tensor_tensor(x[:], x[:], xn[:, :, 0:D], ALU.add))
            link(normalise(xn[:, :, 0:D], on, False))
            link(ve.tensor_tensor(on[:], on[:], lng[:].unsqueeze(1).to_broadcast([P, NT, D]), ALU.mult))
            ve.tensor_tensor(xn[:, :, 0:D], on[:], lnb[:].unsqueeze(1).to_broadcast([P, NT, D]),
                             ALU.add).then_inc(ln_done, 1)
            ve.wait_ge(ln_done, 4)
            ve.wait_ge(lg_full, 2)
            link(ve.tensor_scalar(lg[:], ps[:, 6, 0:P].rearrange("p (i e) -> p i e", e=E), 0.0, None,
                                  ALU.add))
            make_keys(link, lg[:])
            ve.memset(avail[:], 1.0)
            link(ve.memset(place[:], 0.0))
            with ve.Fori(0, E) as it:
                counter = LoopChain(ve, loop_own["route1"], it, ROUTE1_LINKS)
                lk = counter.link
                hi_e = hi[:, bass.ds(it, 1), :]
                lo_e = lo[:, bass.ds(it, 1), :]
                h1 = hie[:].unsqueeze(1)
                lk(ve.scalar_tensor_tensor(h1, hi_e, 1.0, avail[:].unsqueeze(1), ALU.add, ALU.mult))
                lk(ve.tensor_scalar(hie[:], hie[:], -1.0, None, ALU.add))
                route(lk, h1, lo_e, 1, 4, step1, 1, lambda v: it * 9 + v)
                ve.tensor_tensor(avail[:], avail[:], sel[:, 0, :], ALU.subtract)
                lk(ve.scalar_tensor_tensor(er[:, 0, :], sel[:, 0, :], ebase[:, bass.ds(it, 1)],
                                           pos[:, 0, :], ALU.mult, ALU.add))
                lk(ve.tensor_tensor(place[:], place[:], er[:, 0, :], ALU.add))
                assert counter.n == ROUTE1_LINKS, counter.n
            ve.tensor_copy(placei[:], place[:]).then_inc(place_ready, 1)
            meet(ve)
            ffn(1)
            ve.wait_ge(y_back, 16 * NT)
            for half in range(2):
                s = slice(8 * half, 8 * half + 8)
                ve.tensor_tensor(x[:, s, :], x[:, s, :], on[:, s, :], ALU.add).then_inc(out_ready, 1)

        @block.gpsimd
        def _(gp):
            own = Chain(gp, pool_own)
            link = own.link
            nb = dict(allow_small_or_imprecise_dtypes=True)
            gp.memset(identf[:], 0.0)
            gp.memset(onesf[:], 1.0)
            gp.memset(onesb[:], 1.0)
            gp.memset(seg[:], 1.0)
            gp.iota(iotaf[:], [[1, CAP]], base=0, channel_multiplier=0, **nb)
            gp.iota(tokf[:, :, 0], [[0, NT]], base=0, channel_multiplier=1, **nb)
            gp.iota(tokf[:, :, 1], [[P, NT]], base=0, channel_multiplier=0, **nb)
            gp.iota(ebase[:], [[CAP, E]], base=0, channel_multiplier=0, **nb)
            for r in range(8):
                s = 2 ** (14 - 2 * r)
                gp.iota(step0[:, r, :], [[s, 3]], base=s, channel_multiplier=0, **nb)
            for r in range(4):
                s = 2 ** (12 - 4 * r)
                gp.iota(step1[:, r, :], [[s, 15]], base=s, channel_multiplier=0, **nb)
            link(gp.iota(dist[:], [[P, 2], [-1, S]], base=0, channel_multiplier=1, **nb))
            gp.memset(seg[:, :, 0:1], 0.0)
            gp.tensor_copy(iotab[:], iotaf[:])
            gp.tensor_copy(tokid[:], tokf[:])
            gp.affine_select(tri[:], onesb[:], [[1, P]], ALU.is_gt, 0.0, base=0, channel_multiplier=-1)
            link(gp.affine_select(identf[:], identf[:], [[1, P]], ALU.not_equal, 1.0, base=0,
                                  channel_multiplier=-1))
            link(gp.tensor_copy(identb[:], identf[:]))
            for h in range(H):
                ins = gp.tensor_scalar(diag[:, h, :], identf[:], -(2.0 ** -(h + 1)), None, ALU.mult)
            ins.then_inc(pool_const, 1)

            def casts(first, count, l0q):
                for n in range(first, first + count):
                    gp.wait_ge(f_ready, n + 1)
                    if l0q:
                        gp.wait_ge(bias_ready, n - first + 1)
                    if n >= 3:
                        gp.wait_ge(img_written[n % 3], 96 * (n // 3))
                    gp.tensor_copy(parts[:, n % 3, 0, :], fbuf[:, n % 2, :]).then_inc(p1_ready, 1)
                    gp.wait_ge(r_ready, n + 1)
                    gp.tensor_copy(parts[:, n % 3, 1, :], rbuf[:, n % 2, :]).then_inc(p2_ready, 1)

            def attention(l):
                A = at[l]

                def copy(it, b2_, par):
                    if it is not None or b2_ >= 2:
                        gp.wait_ge(A["pv_done"], 8 * (b2_ - 1) if it is None
                                   else it * 16 + 8 * (b2_ - 1))
                    src = (v9[l][:, 2 * b2_:2 * b2_ + 2] if it is None
                           else v9[l][:, bass.ds(it * 4 + 2 * b2_, 2)])
                    gp.tensor_copy(vb[:, par, :].rearrange("p (i c) -> p i c", i=2),
                                   src.rearrange("p i h d -> p i (h d)")).then_inc(A["vcopy"], 1)

                copy(None, 0, 0)
                copy(None, 1, 1)
                with gp.Fori(0, B // 2 - 1) as it:
                    copy(it, 2, 0)
                    copy(it, 3, 1)

            casts(0, 8, False)
            casts(8, 4, True)
            meet(gp)
            attention(0)
            meet(gp)
            meet(gp)
            gp.wait_ge(aug_out, 16)
            for e in range(E):
                gp.wait_ge(idx_ready, e + 1)
                for half in range(2):
                    c = 2 * e + half
                    gp.indirect_dma_start(gt[:, c, :], None, xaug[:, :],
                                          bass.IndirectOffsetOnAxis(ap=idx[:, c:c + 1], axis=0)
                                          ).then_inc(row_got[e], 16)
            meet(gp)
            gp.wait_ge(x_moved, 16)
            for e in range(E):
                gp.wait_ge(y_ready, e + 1)
                if e >= 1:
                    gp.wait_ge(added, 32 * e)
                for half in range(2):
                    c = 2 * e + half
                    gp.indirect_dma_start(acc[:, :], bass.IndirectOffsetOnAxis(ap=idx[:, c:c + 1], axis=0),
                                          yb[:, c, :], None, compute_op=ALU.add).then_inc(added, 16)
            gp.wait_ge(added, 32 * E)
            meet(gp)
            casts(12, 4, False)
            meet(gp)
            attention(1)
            meet(gp)
            meet(gp)
            gp.wait_ge(place_ready, 1)
            for i in range(NT):
                gp.indirect_dma_start(nsort[:, :], bass.IndirectOffsetOnAxis(ap=placei[:, i:i + 1], axis=0),
                                      xn[:, i, 0:D], None).then_inc(rows_sorted, 16)
            meet(gp)
            gp.wait_ge(y_stored, 16 * E)
            for i in range(NT):
                gp.indirect_dma_start(on[:, i, :], None, ysort[:, :],
                                      bass.IndirectOffsetOnAxis(ap=placei[:, i:i + 1], axis=0)
                                      ).then_inc(y_back, 16)


ROUTE1_LINKS = 54


_INPUTS = None


def kernel(**inputs):
    import numpy as np
    import concourse.bacc as bacc
    from concourse.bass_utils import run_bass_kernel_spmd

    nc = bacc.Bacc("TRN2", target_bir_lowering=False, num_devices=1)
    arrays, aps = {}, {}
    for name, value in inputs.items():
        v = np.ascontiguousarray(value)
        arrays["in_" + name] = v
        aps[name] = nc.dram_tensor("in_" + name, v.shape, mybir.dt.from_np(v.dtype),
                                   kind="ExternalInput").ap()
    out = nc.dram_tensor("out", (B, S, D), F32, kind="ExternalOutput").ap()
    build(nc, aps, out)
    r = run_bass_kernel_spmd(nc, [arrays], core_ids=[0])
    return r.results[0]["out"]
```

```python
from contextlib import ExitStack

import concourse.bass as bass
from concourse import mybir

F32 = mybir.dt.float32
BF16 = mybir.dt.bfloat16
I32 = mybir.dt.int32
ALU = mybir.AluOpType
ACT = mybir.ActivationFunctionType
AX = mybir.AxisListType

P = 128
B, S, D = 8, 256, 128
H, HD = 16, 8
NT = B * S // P
T = B * S
E = 8
CAP = T // E
F = 512
FC = F // P
PARTS = 3
PAIRS = PARTS * PARTS * HD
ROWS = PAIRS + PARTS
VW = HD + 1
CH = 512
NCH = T // CH
BIG = float(2 ** 47)
EPS = 1e-5
AUG = D + E
UH = H // 2
UNITS = 2 * B
PAIRS_N = UNITS * UH // 2
QUADS = PAIRS_N // 2
VP = 32


class Chain:

    def __init__(self, eng, sem):
        self.eng, self.sem, self.n = eng, sem, 0

    def link(self, ins):
        self.n += 1
        ins.then_inc(self.sem, 1)
        self.eng.wait_ge(self.sem, self.n)


class LoopChain:

    def __init__(self, eng, sem, it, per, start=0):
        self.eng, self.sem, self.it, self.per, self.n = eng, sem, it, per, start

    def link(self, ins):
        self.n += 1
        ins.then_inc(self.sem, 1)
        self.eng.wait_ge(self.sem, self.it * self.per + self.n)


def build(nc, a, out):
    ctx = ExitStack()
    with ctx:
        def sb(name, shape, dt=F32):
            return ctx.enter_context(nc.sbuf_tensor(name, shape, dt))

        def sem(name):
            return ctx.enter_context(nc.semaphore(name))

        def dram(name, shape, dt=F32):
            return nc.dram_tensor(name, shape, dt, kind="Internal").ap()

        ps = ctx.enter_context(nc.psum_tensor("ps", [P, 8, 512], F32))

        kimg = [dram(f"kimg{l}", [B * PAIRS, H * S], BF16) for l in range(2)]
        qimg = [dram(f"qimg{l}", [B * PARTS * HD, H * S], BF16) for l in range(2)]
        xaug = dram("xaug", [T, AUG])
        acc = dram("acc", [T, D])
        nsort = dram("nsort", [T, D])
        ysort = dram("ysort", [T, D])

        identf = sb("identf", [P, P])
        identb = sb("identb", [P, P], BF16)
        onesf = sb("onesf", [P, P])
        onesb = sb("onesb", [P, P], BF16)
        tri = sb("tri", [P, P], BF16)
        iotaf = sb("iotaf", [P, CAP])
        iotab = sb("iotab", [P, CAP], BF16)
        tokf = sb("tokf", [P, NT, 2])
        tokid = sb("tokid", [P, NT, 2], BF16)
        step0 = sb("step0", [P, 8, 3])
        step1 = sb("step1", [P, 4, 15])
        seg = sb("seg", [P, 2 * E, NT])
        ebase = sb("ebase", [P, E])
        diag = sb("diag", [P, H, P], BF16)
        rv = sb("rv", [P, 2])
        rvrep = sb("rvrep", [P, 2, P], BF16)
        rvrow = sb("rvrow", [P, 2, S])
        bias = sb("bias", [P, 2, S], BF16)
        biasT = sb("biasT", [P, 2, S], BF16)
        x = sb("x", [P, NT, D])
        xn = sb("xn", [P, NT, AUG])
        xT = sb("xT", [P, T])
        on = sb("on", [P, NT, D])
        cT = sb("cT", [P, T])
        wst = sb("wst", [P, 8, P])
        wT = sb("wT", [P, 8, P])
        bcol = sb("bcol", [P, 4])
        brow = sb("brow", [P, 4, P])
        v9 = [sb(f"v9_{l}", [P, NT, H, VW]) for l in range(2)]
        parts = sb("parts", [P, 3, PARTS, CH], BF16)
        qs = sb("qs", [P, 2, H * S], BF16)
        ks = sb("ks", [P, 2, H * S], BF16)
        pbuf = sb("pbuf", [P, 4, 1024])
        flat_pb = pbuf[:].rearrange("p a b -> p (a b)")
        fbuf = flat_pb[:, 0:2 * CH].rearrange("p (a b) -> p a b", a=2)
        rbuf = flat_pb[:, 2 * CH:4 * CH].rearrange("p (a b) -> p a b", a=2)
        flat_qs = qs[:].rearrange("p a b -> p (a b)")
        dist = flat_qs[:, 0:1024].bitcast(F32).rearrange("p (a b) -> p a b", a=2)
        maski = flat_qs[:, 1024:2048].bitcast(I32).rearrange("p (a b) -> p a b", a=2)
        mz = flat_qs[:, 2048:3072].bitcast(F32).rearrange("p (a b) -> p a b", a=2)
        vb = sb("vb", [P, 2, 2, H, VP])
        mx = sb("mx", [P, 2, 2 * UH])
        m3 = sb("m3", [2 * UH, 2, PARTS, P], BF16)
        mr = sb("mr", [2 * UH, P])
        ob = sb("ob", [P, 2, S])
        rec = sb("rec", [P, 2, 8])
        stats = sb("stats", [P, NT, 6])
        mv = sb("mv", [P, NT, 2])
        ve_ = sb("ve_", [P, NT])
        sd = sb("sd", [P, NT])
        rs = sb("rs", [P, NT])
        t1 = sb("t1", [P, NT])
        rw = sb("rw", [P, E])
        rb = sb("rb", [P, E])
        cen = sb("cen", [E, P])
        cenT = sb("cenT", [P, E])
        lng = sb("lng", [P, P])
        lnb = sb("lnb", [P, P])
        b1r = sb("b1r", [E * FC, 2, P])
        b1T = sb("b1T", [P, 2, E * FC])
        b2 = sb("b2", [P, 2, E * D])
        lg = sb("lg", [P, NT, E])
        lmx = sb("lmx", [P, NT])
        keyi = sb("keyi", [P, NT, E], I32)
        keym = sb("keym", [P, NT, E], I32)
        hi = sb("hi", [P, E, NT])
        lo = sb("lo", [P, E, NT])
        cmpb = sb("cmpb", [P, 384], BF16)
        cnt = sb("cnt", [P, 24], BF16)
        thr = sb("thr", [P, 24])
        cst = sb("cst", [P, 24])
        sat = sb("sat", [P, 24])
        nsat = sb("nsat", [P, E])
        base = sb("base", [P, E])
        v2 = sb("v2", [P, E, NT])
        dif = sb("dif", [P, E, NT])
        ge = sb("ge", [P, 2, E, NT], BF16)
        pre = sb("pre", [P, 2, E, NT])
        scn = sb("scn", [P, 2, E, NT])
        er = sb("er", [P, E, NT])
        sel = sb("sel", [P, E, NT])
        pos = sb("pos", [P, E, NT])
        avail = sb("avail", [P, NT])
        hie = sb("hie", [P, NT])
        place = sb("place", [P, NT])
        placei = sb("placei", [P, NT], I32)
        oh = qs[:].rearrange("p a b -> p (a b)").rearrange("p (a i c) -> p a i c", a=2, i=NT)
        idx = sb("idx", [P, 2 * E], I32)
        w1 = sb("w1", [P, E, F])
        w2 = sb("w2", [P, E * FC, D])
        gt = ks[:].rearrange("p a b -> p (a b)")[:, 0:4 * E * AUG].bitcast(F32).rearrange(
            "p (c d) -> p c d", d=AUG)
        xg = sb("xg", [P, 2, CAP])
        hb = pbuf[:, 0:2, :].rearrange("p a (c s) -> p a c s", c=FC)
        yb = cT[:].rearrange("p (c d) -> p c d", d=D)

        ld = {n: sem("ld_" + n) for n in ("ctx", "x", "w", "small", "ffn0", "ffn1")}
        pool_const = sem("pool_const")
        pool_own = sem("pool_own")
        dve_own = sem("dve_own")
        act_own = sem("act_own")
        phase = sem("phase")
        filled = sem("filled")
        drained = sem("drained")
        v_full = sem("v_full")
        v_free = sem("v_free")
        f_ready = sem("f_ready")
        p1_ready = sem("p1_ready")
        r_ready = sem("r_ready")
        p2_ready = sem("p2_ready")
        p3_ready = sem("p3_ready")
        img_written = [sem(f"img_written{i}") for i in range(3)]
        rv_ready = sem("rv_ready")
        ps_rv = sem("ps_rv")
        bias_ready = sem("bias_ready")
        ln_done = sem("ln_done")
        var_ready = sem("var_ready")
        sd_ready = sem("sd_ready")
        x_moved = sem("x_moved")
        out_full = sem("out_full")
        lg_full = sem("lg_full")
        lg_shift = sem("lg_shift")
        lg_exp = sem("lg_exp")
        sc_ready = sem("sc_ready")
        aug_out = sem("aug_out")
        cnt_ready = [sem(f"cnt_ready{l}") for l in range(2)]
        tot_ready = [sem(f"tot_ready{l}") for l in range(2)]
        loop_own = {n: sem("own_" + n) for n in ("oh", "route1")}
        oh_ready = sem("oh_ready")
        idx_full = sem("idx_full")
        idx_ready = sem("idx_ready")
        row_got = [sem(f"row_got{e}") for e in range(E)]
        xg_full = sem("xg_full")
        xg_ready = sem("xg_ready")
        h_full = sem("h_full")
        h_ready = sem("h_ready")
        y_full = sem("y_full")
        y_ready = sem("y_ready")
        added = sem("added")
        place_ready = sem("place_ready")
        rows_sorted = sem("rows_sorted")
        rows_loaded = sem("rows_loaded")
        y_stored = sem("y_stored")
        y_back = sem("y_back")
        out_ready = sem("out_ready")
        stored = sem("stored")
        at = [{n: sem(f"{n}{l}") for n in
               ("stk0", "stk1", "stk2", "stk3", "mrow0", "mrow1", "mrow2", "mrow3", "vcopy", "mx_ps",
                "mx_red", "mxT", "mx_split", "st_ps", "exp_done", "pv_done", "o_out", "oT", "o_rec",
                "o_norm", "own_split")}
              for l in range(2)]

        def dview(ap, i=None):
            return ap.rearrange("b s d -> (b s) d").rearrange("(i p) d -> p i d", p=P)

        names = [["L0_xattn_wq_w", "L0_xattn_wk_w", "L0_xattn_wv_w", "L0_xattn_out_w"],
                 ["L1_xattn_w_q", "L1_xattn_w_k", "L1_xattn_w_v", "L1_xattn_w_o"]]
        bnames = [["L0_xattn_wq_b", "L0_xattn_wk_b", "L0_xattn_wv_b", "L0_xattn_out_b"],
                  ["L1_xattn_b_q", "L1_xattn_b_k", "L1_xattn_b_v", "L1_xattn_b_o"]]
        N_SMALL = 9 + 4 + 4

        block = ctx.enter_context(nc.Block())
        phases = {}

        def meet(eng):
            phases[eng] = phases.get(eng, 0) + 1
            eng.drain().then_inc(phase, 1)
            eng.wait_ge(phase, 5 * phases[eng])

        def bcast(ap, n):
            return ap.unsqueeze(0).to_broadcast([P, n])

        @block.sync
        def _(sp):
            for half in range(2):
                sp.dma_start(on[:, 8 * half:8 * half + 8, :],
                             dview(a["ctx_1024"])[:, 8 * half:8 * half + 8, :]).then_inc(ld["ctx"], 16)
            for l in range(2):
                for j in range(4):
                    sp.dma_start(wst[:, 4 * l + j, :], a[names[l][j]]).then_inc(ld["w"], 16)
            for half in range(2):
                sp.dma_start(x[:, 8 * half:8 * half + 8, :],
                             dview(a["x"])[:, 8 * half:8 * half + 8, :]).then_inc(ld["x"], 16)
            small = []
            for l in range(2):
                for j in range(2):
                    small.append((bcol[:, 2 * l + j:2 * l + j + 1], a[bnames[l][j]].unsqueeze(1)))
                    small.append((brow[:, 2 * l + j, :], bcast(a[bnames[l][2 + j]], P)))
            small += [(maski[:], a["mask_1x1xSxS2_ik0"].rearrange("a b s t -> (a b s) t")
                       .rearrange("(i p) t -> p i t", p=P)),
                      (rw[:], a["L0_ffn_router_w"]),
                      (rb[:], bcast(a["L0_ffn_router_b"], E)),
                      (cen[:], a["L1_ffn_centroids"]),
                      (lng[:], bcast(a["L1_ffn_ln_g"], P)),
                      (lnb[:], bcast(a["L1_ffn_ln_b"], P))]
            for l in range(2):
                small.append((b1r[:, l, :], a[f"L{l}_ffn_b1"].rearrange("e (c p) -> (e c) p", p=P)))
            small.append((b2[:, 0, :], bcast(a["L0_ffn_b2"].rearrange("e d -> (e d)"), E * D)))
            assert len(small) == N_SMALL
            for dst, src in small:
                sp.dma_start(dst, src).then_inc(ld["small"], 16)
            sp.dma_start(b2[:, 1, :], bcast(a["L1_ffn_b2"].rearrange("e d -> (e d)"), E * D)
                         ).then_inc(ld["ffn0"], 16)
            sp.dma_start(w1[:], a["L0_ffn_w1"].rearrange("e d f -> d e f")).then_inc(ld["ffn0"], 16)
            sp.dma_start(w2[:], a["L0_ffn_w2"].rearrange("e f d -> (e f) d")
                         .rearrange("(c p) d -> p c d", p=P)).then_inc(ld["ffn0"], 16)

            def write_images(first, imgs):
                for n in range(first, first + NCH * len(imgs)):
                    img = imgs[(n - first) // NCH]
                    sp.wait_ge(p3_ready, n + 1)
                    for bb in range(2):
                        b = 2 * (n % NCH) + bb
                        cols = slice(bb * S, bb * S + S)
                        if img in kimg:
                            for i in range(PARTS):
                                row = b * PAIRS + i * PARTS * HD
                                sp.dma_start(img[row:row + PARTS * HD, :]
                                             .rearrange("r (h s) -> h r s", h=H),
                                             parts[:, n % 3, i, cols].unsqueeze(1)
                                             .to_broadcast([P, PARTS, S])
                                             ).then_inc(img_written[n % 3], 16)
                        else:
                            row = b * PARTS * HD
                            sp.dma_start(img[row:row + PARTS * HD, :].rearrange("r (h s) -> h r s", h=H),
                                         parts[:, n % 3, :, cols]).then_inc(img_written[n % 3], 16)
                for n in range(first + NCH * len(imgs) - 3, first + NCH * len(imgs)):
                    sp.wait_ge(img_written[n % 3], WRITTEN[n])

            def load_stack(l, b, slot):
                par, half = slot // 2, slot % 2
                cols = slice(half * UH * S, (half + 1) * UH * S)
                s = at[l][f"stk{slot}"]
                sp.dma_start(ks[0:PAIRS, par, cols], kimg[l][bass.ds(b * PAIRS, PAIRS), cols]
                             ).then_inc(s, 16)
                for pa in range(PARTS):
                    sp.dma_start(qs[pa * 24:pa * 24 + 24, par, cols],
                                 qimg[l][bass.ds(b * (PARTS * HD), PARTS * HD), cols]).then_inc(s, 16)

            def max_rows(l, slot):
                par, half = slot // 2, slot % 2
                cols = slice(half * UH * S, (half + 1) * UH * S)
                for i in range(PARTS):
                    sp.dma_start(qs[PAIRS + i:PAIRS + i + 1, par, cols], m3[:, slot % 2, i, :]
                                 ).then_inc(at[l][f"mrow{slot}"], 16)

            def attention(l):
                A = at[l]
                for w in range(4):
                    load_stack(l, w // 2, w)
                for w in range(2):
                    sp.wait_ge(A["mx_split"], w + 1)
                    max_rows(l, w)
                with sp.Fori(0, UNITS // 4 - 1) as it:
                    for w in range(4):
                        b = sp.snap(it * 2 + (w // 2 + 2))
                        used = sp.snap(it * 16 + 4 * (w + 1))
                        split = sp.snap(it * 4 + (w + 3))
                        sp.wait_ge(A["st_ps"], used)
                        load_stack(l, b, w)
                        sp.wait_ge(A["mx_split"], split)
                        max_rows(l, (w + 2) % 4)
                for w in range(UNITS - 2, UNITS):
                    sp.wait_ge(A["mx_split"], w + 1)
                    max_rows(l, w % 4)

            write_images(0, [kimg[0], kimg[1], qimg[0]])
            meet(sp)
            attention(0)
            meet(sp)
            meet(sp)
            sp.dma_start(acc.rearrange("(i p) d -> p i d", p=P), x[:]).then_inc(x_moved, 16)
            sp.wait_ge(sc_ready, 1)
            sp.dma_start(xaug.rearrange("(i p) c -> p i c", p=P), xn[:]).then_inc(aug_out, 16)
            sp.wait_ge(x_moved, 16)
            meet(sp)
            meet(sp)
            sp.dma_start(x[:], acc.rearrange("(i p) d -> p i d", p=P)).then_inc(x_moved, 16)
            sp.dma_start(w1[:], a["L1_ffn_w1"].rearrange("e d f -> d e f")).then_inc(ld["ffn1"], 16)
            sp.dma_start(w2[:], a["L1_ffn_w2"].rearrange("e f d -> (e f) d")
                         .rearrange("(c p) d -> p c d", p=P)).then_inc(ld["ffn1"], 16)
            write_images(12, [qimg[1]])
            meet(sp)
            attention(1)
            meet(sp)
            meet(sp)
            meet(sp)
            sp.wait_ge(rows_sorted, 16 * NT)
            sp.dma_start(gt[:, :, 0:D], nsort.rearrange("(c p) d -> p c d", p=P)
                         ).then_inc(rows_loaded, 16)
            for e in range(E):
                sp.wait_ge(y_ready, E + e + 1)
                sp.dma_start(ysort[e * CAP:(e + 1) * CAP, :].rearrange("(c p) d -> p c d", p=P),
                             yb[:, 2 * e:2 * e + 2, :]).then_inc(y_stored, 16)
            for half in range(2):
                sp.wait_ge(out_ready, half + 1)
                sp.dma_start(dview(out)[:, 8 * half:8 * half + 8, :],
                             x[:, 8 * half:8 * half + 8, :]).then_inc(stored, 16)
            sp.wait_ge(stored, 32)

        @block.tensor
        def _(pe):
            ring = [0]

            def fill(instructions):
                n = ring[0]
                ring[0] += 1
                if n >= 6:
                    pe.wait_ge(drained, n - 5)
                for f in instructions:
                    last = f(ps[:, n % 6, :])
                last.then_inc(filled, 1)

            def tiles(src, lo_, n=4, width=P):
                return [lambda bank, j=j: pe.transpose(bank[:, j * P:j * P + P], src(lo_ + j), identf[:])
                        for j in range(n)]

            def project(w, srcT, c):
                return [lambda bank: pe.matmul(bank, wT[:, w, :], srcT[:, c * CH:c * CH + CH],
                                               start=True, stop=True)]

            def transpose_x():
                for c in range(4):
                    fill(tiles(lambda i: xn[:, i, 0:D], 4 * c))

            pe.wait_ge(pool_const, 1)
            pe.wait_ge(ld["w"], 16 * 8)
            for l in range(2):
                fill(tiles(lambda j: wst[:, j, :], 4 * l))
            pe.wait_ge(ld["ctx"], 32)
            for c in range(4):
                fill(tiles(lambda i: on[:, i, :], 4 * c))
            pe.wait_ge(ld["small"], 16 * N_SMALL)
            fill([lambda bank: pe.transpose(bank[:, 0:E], cen[:], identf[0:E, 0:E])]
                 + [lambda bank, l=l: pe.transpose(bank[:, 32 + 32 * l:64 + 32 * l], b1r[:, l, :],
                                                   identf[0:32, 0:32]) for l in range(2)])
            pe.wait_ge(drained, 6)
            for l in range(2):
                for q in range(4):
                    fill(project(4 * l + 1, cT, q))
                    n = 4 * l + q
                    if n >= 1:
                        pe.wait_ge(v_free, n)
                    for j in range(4):
                        i = 4 * q + j
                        mm = pe.matmul(ps[:, 6, j * P:j * P + P], cT[:, i * P:i * P + P],
                                       wT[:, 4 * l + 2, :], start=True, stop=True)
                    mm.then_inc(v_full, 1)
            pe.wait_ge(rv_ready, 1)
            for st in range(2):
                pe.matmul(ps[:, 7, st * P:st * P + P], rvrep[:, st, :], identb[:], start=True, stop=True)
            pb = ps[:, 7, 256:512].bitcast(BF16)
            for st in range(2):
                for tt in range(2):
                    mm = pe.transpose(pb[:, tt * S + st * P:tt * S + st * P + P],
                                      bias[:, st, tt * P:tt * P + P], identb[:])
            mm.then_inc(ps_rv, 1)
            pe.wait_ge(ln_done, 1)
            transpose_x()
            pe.wait_ge(drained, ring[0])
            for c in range(NCH):
                fill(project(0, xT, c))
            meet(pe)

            def attention(l):
                A = at[l]

                def value(it, per, c):
                    return c if it is None else it * per + c

                def max_head(it, w, h):
                    m, slot = UH * w + h, w % 4
                    if it is not None or m >= 2:
                        pe.wait_ge(A["mx_red"], value(it, 32, m - 1))
                    if h == 0:
                        pe.wait_ge(A[f"stk{slot}"], value(it, 64, 64 * (w // 4 + 1)))
                    c0 = (slot % 2 * UH + h) * S
                    for st in range(2):
                        o = ps[:, h % 2, st * S:st * S + S]
                        mm = pe.matmul(o, qs[0:PAIRS, slot // 2, c0 + st * P:c0 + st * P + P],
                                       ks[0:PAIRS, slot // 2, c0:c0 + S], start=True, stop=l == 1)
                        if l == 0:
                            mm = pe.matmul(o, diag[:, slot % 2 * UH + h, :], bias[:, st, :],
                                           start=False, stop=True)
                    mm.then_inc(A["mx_ps"], 1)

                def scores(it, u):
                    w, g = u // 4, u % 4
                    slot = w % 4
                    if it is not None or u >= 2:
                        pe.wait_ge(A["exp_done"], value(it, 16, u - 1))
                    if g == 0:
                        pe.wait_ge(A[f"mrow{slot}"], value(it, 48, 48 * (w // 4 + 1)))
                    for hh in range(2):
                        h = slot % 2 * UH + 2 * g + hh
                        for tt in range(2):
                            o = ps[:, 2 + 2 * (u % 2) + hh, tt * S:tt * S + S]
                            mm = pe.matmul(o, ks[0:ROWS, slot // 2, h * S + tt * P:h * S + tt * P + P],
                                           qs[0:ROWS, slot // 2, h * S:h * S + S],
                                           start=True, stop=l == 1)
                            if l == 0:
                                mm = pe.matmul(o, diag[:, h, :], biasT[:, tt, :], start=False, stop=True)
                    mm.then_inc(A["st_ps"], 1)

                def values(it, q):
                    b, par = q // 4, q // 4 % 2
                    pe.wait_ge(A["exp_done"], value(it, 16, 2 * q + 2))
                    if q % 4 == 0:
                        pe.wait_ge(A["vcopy"], value(it, 2, b + 1))
                    if it is not None or q >= 1:
                        pe.wait_ge(A["o_out"], value(it, 8, q))
                    for tt in range(2):
                        for j in range(4):
                            p0 = j % 2 * 512 + tt * S
                            mm = pe.matmul(ps[VP * j:VP * j + VP, 6, 0:S],
                                           vb[:, par, tt, q % 4 * 4 + j, :],
                                           pbuf[:, (2 * q + j // 2) % 4, p0:p0 + S],
                                           start=tt == 0, stop=tt == 1, tile_position=(0, VP * j))
                    mm.then_inc(A["pv_done"], 1)

                def turn_quad(it, q, turned):
                    pe.wait_ge(A["o_out"], value(it, 8, q + 1))
                    if it is not None or q >= 1:
                        pe.wait_ge(A["o_norm"], value(it, 8, q))
                    pe.wait_ge(A["mx_split"], value(it, 4, turned))
                    for st in range(2):
                        mm = pe.transpose(ps[:, 7, st * P:st * P + P], ob[:, q % 2, st * P:st * P + P],
                                          identf[:])
                    mm.then_inc(A["oT"], 1)

                def turn_maxima(it, w):
                    pe.wait_ge(A["mx_red"], value(it, 32, UH * (w + 1)))
                    if it is not None or w >= 1:
                        pe.wait_ge(A["mx_split"], value(it, 4, w))
                    if it is not None or w >= 2:
                        pe.wait_ge(A["o_norm"], value(it, 8, 2 * w - 3))
                    pe.transpose(ps[0:2 * UH, 7, 2 * P:3 * P], mx[:, w % 2, :], identf[:]
                                 ).then_inc(A["mxT"], 1)

                def step(it, u):
                    w, g = u // 4, u % 4
                    if w + 2 < UNITS:
                        max_head(it, w + 2, 2 * g)
                        max_head(it, w + 2, 2 * g + 1)
                    if u < PAIRS_N:
                        scores(it, u)
                    if u % 2 == 0 and u >= 4:
                        turn_quad(it, (u - 4) // 2, min(w + 1 + g // 2, UNITS))
                    if g == 1 and w >= 1 and w + 1 < UNITS:
                        turn_maxima(it, w + 1)
                    if u % 2 == 1 and u >= 3:
                        values(it, (u - 3) // 2)

                for w in range(2):
                    for h in range(UH):
                        max_head(None, w, h)
                    turn_maxima(None, w)
                for u in range(8):
                    step(None, u)
                with pe.Fori(0, UNITS // 4 - 1) as it:
                    for u in range(8, 24):
                        step(it, u)
                for u in range(PAIRS_N - 8, PAIRS_N + 3):
                    step(None, u)

            def project_out(l):
                for c in range(4):
                    fill(tiles(lambda i: on[:, i, :], 4 * c))
                for c in range(4):
                    pe.wait_ge(drained, ring[0] - 3 + c)
                    if c >= 2:
                        pe.wait_ge(v_free, 8 + 4 * l + c - 1)
                    for j in range(4):
                        i = 4 * c + j
                        mm = pe.matmul(ps[:, 6 + c % 2, j * P:j * P + P], xT[:, i * P:i * P + P],
                                       wT[:, 4 * l + 3, :], start=True, stop=True)
                    mm.then_inc(out_full, 1)

            def logits(rhs, n):
                pe.wait_ge(drained, ring[0])
                for i in range(NT):
                    mm = pe.matmul(ps[:, 6, i * E:(i + 1) * E], xT[:, i * P:i * P + P], rhs,
                                   start=True, stop=True)
                mm.then_inc(lg_full, 1)

            def ffn(l):
                def rows_in(e):
                    if l == 0:
                        pe.wait_ge(row_got[e], 32)
                    elif e == 0:
                        pe.wait_ge(rows_loaded, 16)
                    n = 8 * l + e
                    if n >= 2:
                        pe.wait_ge(xg_ready, n - 1)
                    for half in range(2):
                        mm = pe.transpose(ps[:, e % 2, half * P:half * P + P],
                                          gt[:, 2 * e + half, 0:D], identf[:])
                    mm.then_inc(xg_full, 1)

                def hidden(e):
                    n = 8 * l + e
                    pe.wait_ge(xg_ready, n + 1)
                    if e == 0:
                        pe.wait_ge(ld[f"ffn{l}"], [48, 32][l])
                    if n >= 2:
                        pe.wait_ge(h_ready, 4 * (n - 1))
                    for c in range(FC):
                        mm = pe.matmul(ps[:, 2 + 2 * (e % 2) + c // 2,
                                          (c % 2) * CAP:(c % 2) * CAP + CAP],
                                       w1[:, e, c * P:c * P + P], xg[:, e % 2, :],
                                       start=True, stop=True)
                        if c % 2 == 1:
                            mm.then_inc(h_full, 1)

                def outputs(e):
                    n = 8 * l + e
                    pe.wait_ge(h_ready, 4 * (n + 1))
                    if n >= 2:
                        pe.wait_ge(y_ready, n - 1)
                    for half in range(2):
                        for c in range(FC):
                            mm = pe.matmul(ps[:, 6 + e % 2, half * D:half * D + D],
                                           hb[:, e % 2, c, half * P:half * P + P],
                                           w2[:, e * FC + c, :], start=c == 0, stop=c == FC - 1)
                    mm.then_inc(y_full, 1)

                for e in range(E):
                    rows_in(e)
                    hidden(e)
                    if e >= 1:
                        outputs(e - 1)
                outputs(E - 1)

            attention(0)
            meet(pe)
            project_out(0)
            meet(pe)
            pe.wait_ge(ln_done, 2)
            transpose_x()
            logits(rw[:], 1)
            for r in range(16):
                pe.wait_ge(cnt_ready[0], r + 1)
                pe.matmul(ps[:, 7, 0:24], onesb[:], cnt[:], start=True, stop=True
                          ).then_inc(tot_ready[0], 1)
            pe.wait_ge(cnt_ready[0], 17)
            flat = ge[:].rearrange("p g e i -> p (g e i)")
            pe.matmul(ps[:, 0, 0:256], tri[:], flat, start=True, stop=True)
            pe.matmul(ps[:, 0, 256:512], onesb[:], flat, start=True, stop=True).then_inc(tot_ready[0], 1)
            with pe.Fori(0, E // 2) as it:
                for par in range(2):
                    pe.wait_ge(oh_ready, it * 2 + (par + 1))
                    for half in range(2):
                        for i in range(NT):
                            mm = pe.matmul(ps[:, 1 + par, 2 * half:2 * half + 2],
                                           oh[:, par, i, half * P:half * P + P], tokid[:, i, :],
                                           start=i == 0, stop=i == NT - 1)
                    mm.then_inc(idx_full, 1)
            meet(pe)
            ffn(0)
            meet(pe)
            pe.wait_ge(ln_done, 3)
            transpose_x()
            pe.wait_ge(drained, ring[0])
            for c in range(NCH):
                fill(project(4, xT, c))
            meet(pe)
            attention(1)
            meet(pe)
            project_out(1)
            meet(pe)
            pe.wait_ge(ln_done, 4)
            transpose_x()
            logits(cenT[:], 2)
            with pe.Fori(0, E) as it:
                for r in range(8):
                    pe.wait_ge(cnt_ready[1], it * 9 + (r + 1))
                    pe.matmul(ps[:, 7, 0:15], onesb[:], cnt[:, 0:15], start=True, stop=True
                              ).then_inc(tot_ready[1], 1)
                pe.wait_ge(cnt_ready[1], it * 9 + 9)
                pe.matmul(ps[:, 0, 0:32], tri[:], ge[:, :, 0, :], start=True, stop=True)
                pe.matmul(ps[:, 0, 32:64], onesb[:], ge[:, :, 0, :], start=True, stop=True
                          ).then_inc(tot_ready[1], 1)
            meet(pe)
            ffn(1)

        @block.scalar
        def _(act):
            ring = [0]

            def drain(dst, bias_=None, wait=None):
                n = ring[0]
                ring[0] += 1
                act.wait_ge(filled, n + 1)
                if wait:
                    act.wait_ge(*wait)
                src = ps[:, n % 6, 0:dst.shape[-1]]
                if bias_ is None:
                    return act.copy(dst, src)
                return act.activation(dst, src, ACT.Identity, bias=bias_, scale=1.0)

            def drain_x():
                for c in range(4):
                    drain(xT[:, c * CH:c * CH + CH]).then_inc(drained, 1)

            def chunk(n, bias_):
                wait = (r_ready, n - 1) if n >= 2 else None
                ins = drain(fbuf[:, n % 2, :], bias_, wait)
                ins.then_inc(drained, 1)
                act.wait_ge(drained, ring[0])
                act.sem_inc(f_ready, 1)

            for l in range(2):
                drain(wT[:, 4 * l:4 * l + 4, :].rearrange("p a b -> p (a b)")).then_inc(drained, 1)
            for c in range(4):
                drain(cT[:, c * CH:c * CH + CH]).then_inc(drained, 1)
            n = ring[0]
            ring[0] += 1
            act.wait_ge(filled, n + 1)
            act.copy(cenT[:], ps[:, n % 6, 0:E])
            act.copy(b1T[:].rearrange("p l c -> p (l c)"), ps[:, n % 6, 32:96]).then_inc(drained, 1)
            act.wait_ge(var_ready, 1)
            act.activation(sd[:], ve_[:], ACT.Sqrt).then_inc(sd_ready, 1)
            for l in range(2):
                for c in range(NCH):
                    chunk(4 * l + c, bcol[:, 2 * l + 1:2 * l + 2])
            drain_x()
            for c in range(NCH):
                chunk(8 + c, bcol[:, 0:1])
            meet(act)

            def attention(l):
                A = at[l]
                scale = 1.0 if l == 0 else HD ** -0.5

                def step(it, u):
                    def value(per, c):
                        return c if it is None else it * per + c

                    if u < PAIRS_N:
                        act.wait_ge(A["st_ps"], value(16, u + 1))
                        if it is not None or u >= 4:
                            act.wait_ge(A["pv_done"], value(8, (u - 4) // 2 + 1))
                        b0 = 2 + 2 * (u % 2)
                        act.activation(pbuf[:, u % 4, :], ps[:, b0:b0 + 2, :].rearrange("p a b -> p (a b)"),
                                       ACT.Exp, bias=0.0, scale=scale).then_inc(A["exp_done"], 1)
                    if u % 2 == 1 and u >= 3:
                        q = (u - 3) // 2
                        act.wait_ge(A["pv_done"], value(8, q + 1))
                        if it is not None or q >= 2:
                            act.wait_ge(A["oT"], value(8, q - 1))
                        act.copy(ob[:, q % 2, :], ps[:, 6, 0:S]).then_inc(A["o_out"], 1)

                for u in range(8):
                    step(None, u)
                with act.Fori(0, UNITS // 4 - 1) as it:
                    for u in range(8, 24):
                        step(it, u)
                for u in range(PAIRS_N - 8, PAIRS_N + 3):
                    step(None, u)

            def ffn(l):
                def hidden(e):
                    n = 8 * l + e
                    if n >= 2:
                        act.wait_ge(y_full, n - 1)
                    for c in range(FC):
                        act.wait_ge(h_full, 2 * n + c // 2 + 1)
                        act.activation(hb[:, e % 2, c, :],
                                       ps[:, 2 + 2 * (e % 2) + c // 2,
                                          (c % 2) * CAP:(c % 2) * CAP + CAP],
                                       [ACT.Relu, ACT.Gelu_apprx_tanh][l],
                                       bias=b1T[:, l, e * FC + c:e * FC + c + 1], scale=1.0
                                       ).then_inc(h_ready, 1)
                for e in range(E):
                    hidden(e)

            attention(0)
            meet(act)
            drain_x()
            meet(act)
            act.wait_ge(var_ready, 2)
            act.activation(sd[:], ve_[:], ACT.Sqrt).then_inc(sd_ready, 1)
            drain_x()
            act.wait_ge(lg_shift, 1)
            act.activation(lg[:], lg[:], ACT.Exp).then_inc(lg_exp, 1)
            meet(act)
            ffn(0)
            meet(act)
            act.wait_ge(var_ready, 3)
            act.activation(sd[:], ve_[:], ACT.Sqrt).then_inc(sd_ready, 1)
            drain_x()
            for c in range(NCH):
                chunk(12 + c, bcol[:, 2:3])
            meet(act)
            attention(1)
            meet(act)
            drain_x()
            meet(act)
            for r in range(2):
                act.wait_ge(var_ready, 4 + r)
                act.activation(sd[:], ve_[:], ACT.Sqrt).then_inc(sd_ready, 1)
            drain_x()
            meet(act)
            ffn(1)

        @block.vector
        def _(ve):
            own = Chain(ve, dve_own)
            link = own.link
            norms = [0]

            def normalise(src, dst, last):
                for i in range(NT):
                    ins = ve.bn_stats(stats[:, i, :], src[:, i, :])
                link(ins)
                for i in range(NT):
                    ins = ve.bn_aggr(mv[:, i, :], stats[:, i, :])
                link(ins)
                n = norms[0] = norms[0] + 1
                ve.tensor_scalar(ve_[:], mv[:, :, 1], EPS, None, ALU.add).then_inc(var_ready, 1)
                ve.wait_ge(sd_ready, n)
                link(ve.reciprocal(rs[:], sd[:]))
                link(ve.tensor_tensor(t1[:], rs[:], rs[:], ALU.mult))
                link(ve.tensor_tensor(t1[:], t1[:], ve_[:], ALU.mult))
                link(ve.tensor_scalar(t1[:], t1[:], -0.5, 1.5, ALU.mult, ALU.add))
                link(ve.tensor_tensor(rs[:], rs[:], t1[:], ALU.mult))
                for i in range(NT):
                    ins = ve.tensor_scalar(dst[:, i, 0:D], src[:, i, :], mv[:, i, 0:1], rs[:, i:i + 1],
                                           ALU.subtract, ALU.mult)
                return ins

            def split_rest(n, masked):
                f, r = fbuf[:, n % 2, :], rbuf[:, n % 2, :]
                ve.wait_ge(p1_ready, n + 1)
                if n >= 2:
                    ve.wait_ge(p3_ready, n - 1)
                ve.tensor_tensor(r, f, parts[:, n % 3, 0, :], ALU.subtract).then_inc(r_ready, 1)
                ve.wait_ge(p2_ready, n + 1)
                ve.tensor_tensor(parts[:, n % 3, 2, :], r, parts[:, n % 3, 1, :], ALU.subtract
                                 ).then_inc(p3_ready, 1)

            ve.memset(ks[64:96, :, :], 1.0)
            ve.memset(vb[:], 0.0)
            ve.wait_ge(ld["small"], 16 * N_SMALL)
            ve.wait_ge(pool_const, 1)
            link(ve.tensor_scalar(mz[:], maski[:], 0, None, ALU.is_equal))
            link(ve.tensor_reduce(rv[:], mz[:], AX.X, ALU.min))
            link(ve.tensor_scalar(rv[:], rv[:], -1.0, 1.0, ALU.mult, ALU.add))
            link(ve.scalar_tensor_tensor(mz[:], mz[:], BIG, dist[:], ALU.mult, ALU.max))
            for st in range(2):
                ve.tensor_scalar(bias[:, st, :], mz[:, st, :], rv[:, st:st + 1], None, ALU.mult)
                ins = ve.tensor_scalar(rvrep[:, st, :], onesf[:], rv[:, st:st + 1], None, ALU.mult)
            ins.then_inc(rv_ready, 1)
            ve.wait_ge(ld["x"], 32)
            normalise(x, xn, True).then_inc(ln_done, 1)
            for l in range(2):
                ve.memset(v9[l][:, :, :, HD:VW], 1.0)
            for n in range(8):
                l, q = n // 4, n % 4
                ve.wait_ge(v_full, n + 1)
                ve.tensor_tensor(v9[l][:, 4 * q:4 * q + 4, :, 0:HD],
                                 ps[:, 6, :].rearrange("p (i h d) -> p i h d", i=4, h=H),
                                 brow[:, 2 * l, :].rearrange("p (h d) -> p h d", h=H).unsqueeze(1)
                                 .to_broadcast([P, 4, H, HD]), ALU.add).then_inc(v_free, 1)
                split_rest(n, False)
            ve.wait_ge(ps_rv, 1)
            ve.tensor_copy(rvrow[:, 0, :], ps[:, 7, 0:256])
            ve.tensor_copy(rvrow[:, 1, :], ps[:, 7, 0:256])
            link(ve.tensor_copy(biasT[:].rearrange("p a b -> p (a b)"), ps[:, 7, 256:512].bitcast(BF16)))
            for c in range(NCH):
                n = 8 + c
                ve.wait_ge(f_ready, n + 1)
                ve.tensor_tensor(fbuf[:, n % 2, :], fbuf[:, n % 2, :],
                                 rvrow[:].rearrange("p a b -> p (a b)"), ALU.mult).then_inc(bias_ready, 1)
                split_rest(n, True)
            meet(ve)

            def attention(l):
                A = at[l]

                def value(it, per, c):
                    return c if it is None else it * per + c

                def reduce_head(it, w, h):
                    ve.wait_ge(A["mx_ps"], value(it, 32, UH * w + h + 1))
                    ve.tensor_reduce(mx[:, w % 2, 2 * h:2 * h + 2],
                                     ps[:, h % 2, :].rearrange("p (a b) -> p a b", a=2), AX.X,
                                     ALU.max, negate=True).then_inc(A["mx_red"], 1)

                def split_max(it, w):
                    done = [4 * w]

                    def lk(ins):
                        done[0] += 1
                        ins.then_inc(A["own_split"], 1)
                        ve.wait_ge(A["own_split"], value(it, 16, done[0]))

                    src = ps[0:2 * UH, 7, 2 * P:3 * P]
                    ve.wait_ge(A["mxT"], value(it, 4, w + 1))
                    if it is not None or w >= 2:
                        ve.wait_ge(A[f"mrow{(w - 2) % 4}"], value(it, 48, 48 * ((w - 2) // 4 + 1)))
                    lk(ve.tensor_copy(m3[:, w % 2, 0, :], src))
                    lk(ve.tensor_tensor(mr[:], src, m3[:, w % 2, 0, :], ALU.subtract))
                    lk(ve.tensor_copy(m3[:, w % 2, 1, :], mr[:]))
                    lk(ve.tensor_tensor(m3[:, w % 2, 2, :], mr[:], m3[:, w % 2, 1, :], ALU.subtract))
                    ve.sem_inc(A["mx_split"], 1)

                def normalise_quad(it, q):
                    b, h0 = q // 4, q % 4 * 4 * HD
                    ve.wait_ge(A["oT"], value(it, 8, q + 1))
                    o = ps[:, 7, 0:2 * P].rearrange("p (i h d) -> p i h d", i=2, h=4)
                    r = rec[:, q % 2, :].rearrange("p (i h) -> p i h", i=2)
                    dst = (on[:, 2 * b:2 * b + 2, h0:h0 + 4 * HD] if it is None
                           else on[:, bass.ds(it * 4 + 2 * b, 2), h0:h0 + 4 * HD])
                    ve.reciprocal(r, o[:, :, :, HD]).then_inc(A["o_rec"], 1)
                    ve.wait_ge(A["o_rec"], value(it, 8, q + 1))
                    ve.tensor_tensor(dst.rearrange("p i (h d) -> p i h d", h=4), o[:, :, :, 0:HD],
                                     r.unsqueeze(3).to_broadcast([P, 2, 4, HD]), ALU.mult
                                     ).then_inc(A["o_norm"], 1)

                def step(it, u):
                    w, g = u // 4, u % 4
                    if w + 2 < UNITS:
                        reduce_head(it, w + 2, 2 * g)
                        reduce_head(it, w + 2, 2 * g + 1)
                    if u % 2 == 0 and u >= 4:
                        normalise_quad(it, (u - 4) // 2)
                    if g == 1 and w >= 1 and w + 1 < UNITS:
                        split_max(it, w + 1)

                for w in range(2):
                    for h in range(UH):
                        reduce_head(None, w, h)
                    split_max(None, w)
                for u in range(8):
                    step(None, u)
                with ve.Fori(0, UNITS // 4 - 1) as it:
                    for u in range(8, 24):
                        step(it, u)
                for u in range(PAIRS_N - 8, PAIRS_N + 3):
                    step(None, u)

            def project_out(l):
                for c in range(4):
                    ve.wait_ge(out_full, 4 * l + c + 1)
                    ve.tensor_tensor(x[:, 4 * c:4 * c + 4, :].rearrange("p a b -> p (a b)"),
                                     ps[:, 6 + c % 2, :],
                                     x[:, 4 * c:4 * c + 4, :].rearrange("p a b -> p (a b)"),
                                     ALU.add).then_inc(v_free, 1)

            def add_bias(l):
                ve.tensor_tensor(x[:], x[:], brow[:, 2 * l + 1, :].unsqueeze(1)
                                 .to_broadcast([P, NT, D]), ALU.add)

            def make_keys(link_, src):
                bits = src.bitcast(I32)
                link_(ve.tensor_scalar(keym[:], bits, 31, None, ALU.arith_shift_right))
                link_(ve.tensor_scalar(keym[:], keym[:], -2 ** 31, None, ALU.bitwise_or))
                link_(ve.tensor_tensor(keyi[:], bits, keym[:], ALU.bitwise_xor))
                link_(ve.tensor_scalar(keym[:], keyi[:], 16, None, ALU.logical_shift_right))
                ve.tensor_copy(hi[:].rearrange("p e i -> p i e"), keym[:])
                link_(ve.tensor_scalar(keyi[:], keyi[:], 65535, None, ALU.bitwise_and))
                link_(ve.tensor_copy(lo[:].rearrange("p e i -> p i e"), keyi[:]))

            def search(link_, data, n_e, bits_, steps, l, tot, value):
                J = 2 ** bits_ - 1
                rounds = 16 // bits_
                w = n_e * J
                bs = base[:, 0:n_e]
                th = thr[:, 0:w].rearrange("p (e j) -> p e j", e=n_e)
                cs = cst[:, 0:w].rearrange("p (e j) -> p e j", e=n_e)
                sa = sat[:, 0:w].rearrange("p (e j) -> p e j", e=n_e)
                ns = nsat[:, 0:n_e]
                cm = cmpb[:, 0:w * NT].rearrange("p (e j i) -> p e j i", e=n_e, j=J)
                ve.memset(bs, 0.0)
                link_(ve.tensor_copy(th, steps[:, 0, :].unsqueeze(1).to_broadcast([P, n_e, J])))
                for r in range(rounds):
                    step = float(2 ** (16 - bits_ * (r + 1)))
                    link_(ve.tensor_tensor(cm, data.unsqueeze(2).to_broadcast([P, n_e, J, NT]),
                                           th.unsqueeze(3).to_broadcast([P, n_e, J, NT]), ALU.is_ge))
                    with nc.allow_low_precision(reason="counts up to 16 are exact in bf16"):
                        ve.tensor_reduce(cnt[:, 0:w].rearrange("p (e j) -> p e j", e=n_e), cm, AX.X,
                                         ALU.add).then_inc(cnt_ready[l], 1)
                    if r + 1 < rounds:
                        link_(ve.tensor_tensor(cs, bs.unsqueeze(2).to_broadcast([P, n_e, J]),
                                               steps[:, r + 1, :].unsqueeze(1)
                                               .to_broadcast([P, n_e, J]), ALU.add))
                    tot[0] += 1
                    ve.wait_ge(tot_ready[l], value(tot[0]))
                    link_(ve.tensor_scalar(sat[:, 0:w], ps[:, 7, 0:w], float(CAP), None, ALU.is_ge))
                    link_(ve.tensor_reduce(ns, sa, AX.X, ALU.add))
                    if r + 1 < rounds:
                        ve.scalar_tensor_tensor(th, ns.unsqueeze(2).to_broadcast([P, n_e, J]), step,
                                                cs, ALU.mult, ALU.add)
                    link_(ve.scalar_tensor_tensor(bs, ns, step, bs, ALU.mult, ALU.add))

            def route(link_, hi_, lo_, n_e, bits_, steps, l, value):
                tot = [0]
                df, v_ = dif[:, 0:n_e, :], v2[:, 0:n_e, :]
                bs = base[:, 0:n_e]
                bcast_b = bs.unsqueeze(2).to_broadcast([P, n_e, NT])
                search(link_, hi_, n_e, bits_, steps, l, tot, value)
                link_(ve.tensor_tensor(df, hi_, bcast_b, ALU.subtract))
                link_(ve.scalar_tensor_tensor(v_, df, 65536.0, lo_, ALU.mult, ALU.add))
                search(link_, v_, n_e, bits_, steps, l, tot, value)
                g, q = ge[:, 0, 0:n_e, :], ge[:, 1, 0:n_e, :]
                ve.tensor_tensor(g, v_, bcast_b, ALU.is_gt)
                ve.tensor_tensor(q, v_, bcast_b, ALU.is_equal).then_inc(cnt_ready[l], 1)
                tot[0] += 1
                ve.wait_ge(tot_ready[l], value(tot[0]))
                w = 2 * n_e * NT
                view = dict(g=2, e=n_e)
                sc_ = scn[:, :, 0:n_e, :]
                pr_ = pre[:, :, 0:n_e, :]
                flat_s = scn[:].rearrange("p g e i -> p (g e i)")[:, 0:w]
                inside = ps[:, 0, 0:w].rearrange("p (g e i) -> p g e i", **view)
                whole = ps[:, 0, w:2 * w]
                flat_p = pre[:].rearrange("p g e i -> p (g e i)")[:, 0:w]
                link_(ve.tensor_tensor_scan(flat_s, seg[:].rearrange("p a i -> p (a i)")[:, 0:w],
                                            whole, 0.0, ALU.mult, ALU.add))
                link_(ve.tensor_tensor(flat_p, flat_s, whole, ALU.subtract))
                link_(ve.tensor_tensor(flat_p, flat_p, ps[:, 0, 0:w], ALU.add))
                sv = flat_s.rearrange("p (g e i) -> p g e i", **view)
                pv = flat_p.rearrange("p (g e i) -> p g e i", **view)
                er_, se_, po_ = er[:, 0:n_e, :], sel[:, 0:n_e, :], pos[:, 0:n_e, :]
                link_(ve.tensor_tensor(er_, pv[:, 1], sv[:, 0, :, NT - 1:NT]
                                       .to_broadcast([P, n_e, NT]), ALU.add))
                link_(ve.scalar_tensor_tensor(df, er_, float(CAP), q, ALU.is_lt, ALU.mult))
                ve.tensor_tensor(se_, g, df, ALU.add)
                link_(ve.tensor_tensor(er_, er_, df, ALU.mult))
                link_(ve.tensor_tensor(po_, pv[:, 0], g, ALU.mult))
                link_(ve.tensor_tensor(po_, po_, er_, ALU.add))

            def ffn(l):
                for e in range(E):
                    n = 8 * l + e
                    ve.wait_ge(xg_full, n + 1)
                    if n >= 2:
                        ve.wait_ge(h_full, 2 * (n - 1))
                    ve.tensor_copy(xg[:, e % 2, :], ps[:, e % 2, 0:CAP]).then_inc(xg_ready, 1)
                    if e >= 1:
                        finish(l, e - 1)
                finish(l, E - 1)

            def finish(l, e):
                n = 8 * l + e
                ve.wait_ge(y_full, n + 1)
                y = yb[:, 2 * e:2 * e + 2, :]
                bb = b2[:, l, e * D:(e + 1) * D].unsqueeze(1).to_broadcast([P, 2, D])
                ins = ve.tensor_tensor(y, ps[:, 6 + e % 2, 0:2 * D].rearrange("p (a b) -> p a b", a=2),
                                       bb, ALU.add)
                if l == 0:
                    link(ins)
                    ins = ve.tensor_tensor(y, y, gt[:, 2 * e:2 * e + 2, D + e:D + e + 1]
                                           .to_broadcast([P, 2, D]), ALU.mult)
                ins.then_inc(y_ready, 1)

            link(ve.tensor_tensor(x[:], x[:], brow[:, 1, :].unsqueeze(1).to_broadcast([P, NT, D]),
                                  ALU.add))
            attention(0)
            meet(ve)
            project_out(0)
            meet(ve)
            normalise(x, xn, True).then_inc(ln_done, 1)
            ve.wait_ge(lg_full, 1)
            link(ve.tensor_tensor(lg[:], ps[:, 6, 0:P].rearrange("p (i e) -> p i e", e=E),
                                  rb[:].unsqueeze(1).to_broadcast([P, NT, E]), ALU.add))
            link(ve.tensor_reduce(lmx[:], lg[:], AX.X, ALU.max))
            ve.tensor_tensor(lg[:], lg[:], lmx[:].unsqueeze(2).to_broadcast([P, NT, E]),
                             ALU.subtract).then_inc(lg_shift, 1)
            ve.wait_ge(lg_exp, 1)
            link(ve.tensor_reduce(lmx[:], lg[:], AX.X, ALU.add))
            link(ve.reciprocal(lmx[:], lmx[:]))
            link(ve.tensor_tensor(lg[:], lg[:], lmx[:].unsqueeze(2).to_broadcast([P, NT, E]), ALU.mult))
            ve.tensor_copy(xn[:, :, D:AUG], lg[:]).then_inc(sc_ready, 1)
            make_keys(link, lg[:])
            route(link, hi[:], lo[:], E, 2, step0, 0, lambda v: v)
            link(ve.scalar_tensor_tensor(pos[:], pos[:], 1.0, sel[:], ALU.add, ALU.mult))
            link(ve.tensor_scalar(pos[:], pos[:], -1.0, None, ALU.add))
            with ve.Fori(0, E // 2) as it:
                for par in range(2):
                    for i in range(NT):
                        ins = ve.tensor_scalar(oh[:, par, i, :], iotab[:],
                                               pos[:, bass.ds(it * 2 + par, 1), i], None, ALU.is_equal)
                    ins.then_inc(oh_ready, 1)
                    ve.wait_ge(idx_full, it * 2 + (par + 1))
                    ve.tensor_copy(sat[:, 4 * par:4 * par + 4], ps[:, 1 + par, 0:4]
                                   ).then_inc(loop_own["oh"], 1)
                    ve.wait_ge(loop_own["oh"], it * 2 + (par + 1))
                    ve.tensor_tensor(idx[:, bass.ds(it * 4 + 2 * par, 2)],
                                     sat[:, 4 * par:4 * par + 4:2], sat[:, 4 * par + 1:4 * par + 4:2],
                                     ALU.add).then_inc(idx_ready, 1)
            meet(ve)
            ffn(0)
            meet(ve)
            ve.wait_ge(x_moved, 32)
            normalise(x, xn, True).then_inc(ln_done, 1)
            ve.wait_ge(ln_done, 3)
            link(ve.tensor_tensor(x[:], x[:], brow[:, 3, :].unsqueeze(1).to_broadcast([P, NT, D]),
                                  ALU.add))
            ve.memset(ks[64:96, :, :], 1.0)
            for c in range(NCH):
                split_rest(12 + c, False)
            meet(ve)
            attention(1)
            meet(ve)
            project_out(1)
            meet(ve)
            link(normalise(x, xn, False))
            link(ve.tensor_tensor(x[:], x[:], xn[:, :, 0:D], ALU.add))
            link(normalise(xn[:, :, 0:D], on, False))
            link(ve.tensor_tensor(on[:], on[:], lng[:].unsqueeze(1).to_broadcast([P, NT, D]), ALU.mult))
            ve.tensor_tensor(xn[:, :, 0:D], on[:], lnb[:].unsqueeze(1).to_broadcast([P, NT, D]),
                             ALU.add).then_inc(ln_done, 1)
            ve.wait_ge(ln_done, 4)
            ve.wait_ge(lg_full, 2)
            link(ve.tensor_scalar(lg[:], ps[:, 6, 0:P].rearrange("p (i e) -> p i e", e=E), 0.0, None,
                                  ALU.add))
            make_keys(link, lg[:])
            ve.memset(avail[:], 1.0)
            link(ve.memset(place[:], 0.0))
            with ve.Fori(0, E) as it:
                counter = LoopChain(ve, loop_own["route1"], it, ROUTE1_LINKS)
                lk = counter.link
                hi_e = hi[:, bass.ds(it, 1), :]
                lo_e = lo[:, bass.ds(it, 1), :]
                h1 = hie[:].unsqueeze(1)
                lk(ve.scalar_tensor_tensor(h1, hi_e, 1.0, avail[:].unsqueeze(1), ALU.add, ALU.mult))
                lk(ve.tensor_scalar(hie[:], hie[:], -1.0, None, ALU.add))
                route(lk, h1, lo_e, 1, 4, step1, 1, lambda v: it * 9 + v)
                ve.tensor_tensor(avail[:], avail[:], sel[:, 0, :], ALU.subtract)
                lk(ve.scalar_tensor_tensor(er[:, 0, :], sel[:, 0, :], ebase[:, bass.ds(it, 1)],
                                           pos[:, 0, :], ALU.mult, ALU.add))
                lk(ve.tensor_tensor(place[:], place[:], er[:, 0, :], ALU.add))
                assert counter.n == ROUTE1_LINKS, counter.n
            ve.tensor_copy(placei[:], place[:]).then_inc(place_ready, 1)
            meet(ve)
            ffn(1)
            ve.wait_ge(y_back, 16 * NT)
            for half in range(2):
                s = slice(8 * half, 8 * half + 8)
                ve.tensor_tensor(x[:, s, :], x[:, s, :], on[:, s, :], ALU.add).then_inc(out_ready, 1)

        @block.gpsimd
        def _(gp):
            own = Chain(gp, pool_own)
            link = own.link
            nb = dict(allow_small_or_imprecise_dtypes=True)
            gp.memset(identf[:], 0.0)
            gp.memset(onesf[:], 1.0)
            gp.memset(onesb[:], 1.0)
            gp.memset(seg[:], 1.0)
            gp.iota(iotaf[:], [[1, CAP]], base=0, channel_multiplier=0, **nb)
            gp.iota(tokf[:, :, 0], [[0, NT]], base=0, channel_multiplier=1, **nb)
            gp.iota(tokf[:, :, 1], [[P, NT]], base=0, channel_multiplier=0, **nb)
            gp.iota(ebase[:], [[CAP, E]], base=0, channel_multiplier=0, **nb)
            for r in range(8):
                s = 2 ** (14 - 2 * r)
                gp.iota(step0[:, r, :], [[s, 3]], base=s, channel_multiplier=0, **nb)
            for r in range(4):
                s = 2 ** (12 - 4 * r)
                gp.iota(step1[:, r, :], [[s, 15]], base=s, channel_multiplier=0, **nb)
            link(gp.iota(dist[:], [[P, 2], [-1, S]], base=0, channel_multiplier=1, **nb))
            gp.memset(seg[:, :, 0:1], 0.0)
            gp.tensor_copy(iotab[:], iotaf[:])
            gp.tensor_copy(tokid[:], tokf[:])
            gp.affine_select(tri[:], onesb[:], [[1, P]], ALU.is_gt, 0.0, base=0, channel_multiplier=-1)
            link(gp.affine_select(identf[:], identf[:], [[1, P]], ALU.not_equal, 1.0, base=0,
                                  channel_multiplier=-1))
            link(gp.tensor_copy(identb[:], identf[:]))
            for h in range(H):
                ins = gp.tensor_scalar(diag[:, h, :], identf[:], -(2.0 ** -(h + 1)), None, ALU.mult)
            ins.then_inc(pool_const, 1)

            def casts(first, count, l0q):
                for n in range(first, first + count):
                    gp.wait_ge(f_ready, n + 1)
                    if l0q:
                        gp.wait_ge(bias_ready, n - first + 1)
                    if n >= 3:
                        gp.wait_ge(img_written[n % 3], WRITTEN[n - 3])
                    gp.tensor_copy(parts[:, n % 3, 0, :], fbuf[:, n % 2, :]).then_inc(p1_ready, 1)
                    gp.wait_ge(r_ready, n + 1)
                    gp.tensor_copy(parts[:, n % 3, 1, :], rbuf[:, n % 2, :]).then_inc(p2_ready, 1)

            def attention(l):
                A = at[l]

                def copy(it, b):
                    par = b % 2
                    if it is not None or b >= 2:
                        gp.wait_ge(A["pv_done"], 4 * (b - 1) if it is None else it * 8 + 4 * (b - 1))
                    src = (v9[l][:, 2 * b:2 * b + 2] if it is None
                           else v9[l][:, bass.ds(it * 4 + 2 * b, 2)])
                    gp.tensor_copy(vb[:, par, :, :, 0:VW], src).then_inc(A["vcopy"], 1)

                copy(None, 0)
                copy(None, 1)
                with gp.Fori(0, B // 2 - 1) as it:
                    copy(it, 2)
                    copy(it, 3)

            casts(0, 8, False)
            casts(8, 4, True)
            meet(gp)
            attention(0)
            meet(gp)
            meet(gp)
            gp.wait_ge(aug_out, 16)
            for e in range(E):
                gp.wait_ge(idx_ready, e + 1)
                for half in range(2):
                    c = 2 * e + half
                    gp.indirect_dma_start(gt[:, c, :], None, xaug[:, :],
                                          bass.IndirectOffsetOnAxis(ap=idx[:, c:c + 1], axis=0)
                                          ).then_inc(row_got[e], 16)
            meet(gp)
            gp.wait_ge(x_moved, 16)
            for e in range(E):
                gp.wait_ge(y_ready, e + 1)
                if e >= 1:
                    gp.wait_ge(added, 32 * e)
                for half in range(2):
                    c = 2 * e + half
                    gp.indirect_dma_start(acc[:, :], bass.IndirectOffsetOnAxis(ap=idx[:, c:c + 1], axis=0),
                                          yb[:, c, :], None, compute_op=ALU.add).then_inc(added, 16)
            gp.wait_ge(added, 32 * E)
            meet(gp)
            casts(12, 4, False)
            meet(gp)
            attention(1)
            meet(gp)
            meet(gp)
            gp.wait_ge(place_ready, 1)
            for i in range(NT):
                gp.indirect_dma_start(nsort[:, :], bass.IndirectOffsetOnAxis(ap=placei[:, i:i + 1], axis=0),
                                      xn[:, i, 0:D], None).then_inc(rows_sorted, 16)
            meet(gp)
            gp.wait_ge(y_stored, 16 * E)
            for i in range(NT):
                gp.indirect_dma_start(on[:, i, :], None, ysort[:, :],
                                      bass.IndirectOffsetOnAxis(ap=placei[:, i:i + 1], axis=0)
                                      ).then_inc(y_back, 16)


ROUTE1_LINKS = 54
WRITTEN = [sum(16 * (6 if m < 2 * NCH else 2) for m in range(n % 3, n + 1, 3)) for n in range(4 * NCH)]


_INPUTS = None


def kernel(**inputs):
    import numpy as np
    import concourse.bacc as bacc
    from concourse.bass_utils import run_bass_kernel_spmd

    nc = bacc.Bacc("TRN2", target_bir_lowering=False, num_devices=1)
    arrays, aps = {}, {}
    for name, value in inputs.items():
        v = np.ascontiguousarray(value)
        arrays["in_" + name] = v
        aps[name] = nc.dram_tensor("in_" + name, v.shape, mybir.dt.from_np(v.dtype),
                                   kind="ExternalInput").ap()
    out = nc.dram_tensor("out", (B, S, D), F32, kind="ExternalOutput").ap()
    build(nc, aps, out)
    r = run_bass_kernel_spmd(nc, [arrays], core_ids=[0])
    return r.results[0]["out"]
```

```python
from contextlib import ExitStack

import concourse.bass as bass
from concourse import mybir

F32 = mybir.dt.float32
BF16 = mybir.dt.bfloat16
I32 = mybir.dt.int32
F16 = mybir.dt.float16
ALU = mybir.AluOpType
ACT = mybir.ActivationFunctionType
AX = mybir.AxisListType

P = 128
B, S, D = 8, 256, 128
H, HD = 16, 8
NT = B * S // P
T = B * S
E = 8
CAP = T // E
F = 512
FC = F // P
PARTS = 3
PAIRS = PARTS * PARTS * HD
ROWS = PAIRS + PARTS
VW = HD + 1
CH = 512
NCH = T // CH
BIG = float(2 ** 47)
EPS = 1e-5
TWO_ONES = 1.0 + 0x3F80 / 2 ** 23
AUG = D + E
UH = H // 2
UNITS = 2 * B
STEP1_LINKS = 28
WRITTEN = [32 * (n // 3 + 1) for n in range(4 * NCH)]
PAIRS_N = UNITS * UH // 2
PL = 16
VP = 32


class Chain:

    def __init__(self, eng, sem):
        self.eng, self.sem, self.n = eng, sem, 0

    def link(self, ins):
        self.n += 1
        ins.then_inc(self.sem, 1)
        self.eng.wait_ge(self.sem, self.n)


def build(nc, a, out):
    ctx = ExitStack()
    with ctx:
        def sb(name, shape, dt=F32):
            return ctx.enter_context(nc.sbuf_tensor(name, shape, dt))

        def sem(name):
            return ctx.enter_context(nc.semaphore(name))

        def dram(name, shape, dt=F32):
            return nc.dram_tensor(name, shape, dt, kind="Internal").ap()

        ps = ctx.enter_context(nc.psum_tensor("ps", [P, 8, 512], F32))

        kimg = [dram(f"kimg{l}", [B * PARTS * HD, H * S], BF16) for l in range(2)]
        qimg = [dram(f"qimg{l}", [B * PARTS * HD, H * S], BF16) for l in range(2)]
        xaug = dram("xaug", [T, AUG])
        acc = dram("acc", [T, D])

        identf = sb("identf", [P, P])
        identb = sb("identb", [P, P], BF16)
        onesf = sb("onesf", [P, P])
        onesb = sb("onesb", [P, P], BF16)
        tri = sb("tri", [P, P], BF16)
        tokid = sb("tokid", [P, NT])
        count16 = sb("count16", [P, PL], I32)
        spread = sb("spread", [PL, 2, P], F16)
        pick = sb("pick", [P, PL])
        step0 = sb("step0", [P, 8, 3])
        step1 = sb("step1", [P, 4, 15])
        minus = sb("minus", [P, P], BF16)
        unslope = sb("unslope", [P, 1], I32)
        rv = sb("rv", [P, 2])
        rvrep = sb("rvrep", [P, 2, P], BF16)
        rvrow = sb("rvrow", [1, 2 * S])
        bqrow = sb("bqrow", [1, P])
        bias = sb("bias", [P, 2, S], BF16)
        biasT = sb("biasT", [P, 2, S], BF16)
        x = sb("x", [P, NT, D])
        xn = sb("xn", [P, NT, AUG])
        xT = sb("xT", [P, T])
        on = sb("on", [P, NT, D])
        cT = sb("cT", [P, T])
        wst = sb("wst", [P, 8, P])
        wT = sb("wT", [P, 8, P])
        bcol = sb("bcol", [P, 4])
        brow = sb("brow", [P, 4, P])
        v9 = [sb(f"v9_{l}", [P, NT, H, VW]) for l in range(2)]
        parts = sb("parts", [P, 3, PARTS, CH], BF16)
        qs = sb("qs", [P, 2, H * S], BF16)
        ks = sb("ks", [P, 2, H * S], BF16)
        pbuf = sb("pbuf", [P, 4, 1024])
        flat_pb = pbuf[:].rearrange("p a b -> p (a b)")
        fbuf = flat_pb[:, 0:2 * CH].rearrange("p (a b) -> p a b", a=2)
        rbuf = flat_pb[:, 2 * CH:4 * CH].rearrange("p (a b) -> p a b", a=2)
        flat_qs = qs[:].rearrange("p a b -> p (a b)")
        dist = flat_qs[:, 0:1024].bitcast(F32).rearrange("p (a b) -> p a b", a=2)
        maski = flat_qs[:, 1024:2048].bitcast(I32).rearrange("p (a b) -> p a b", a=2)
        mz = flat_qs[:, 2048:3072].bitcast(F32).rearrange("p (a b) -> p a b", a=2)
        flat_xn = xn[:].rearrange("p a b -> p (a b)")
        vb = sb("vb", [P, 2, 2, H, VP])
        mx = sb("mx", [P, 2, 2 * UH])
        m3 = sb("m3", [2 * UH, 2, PARTS, P], BF16)
        mr = sb("mr", [2 * UH, P])
        ob = sb("ob", [P, 2, S])
        rec = sb("rec", [P, 2, 8])
        oq = sb("oq", [P, 2, 2 * P])
        stats = sb("stats", [P, NT, 6])
        mv = sb("mv", [P, NT, 2])
        ve_ = sb("ve_", [P, NT])
        sd = sb("sd", [P, NT])
        rs = sb("rs", [P, NT])
        tiny = sb("tiny", [P, 1])
        waiter = sb("waiter", [P, 2])
        t1 = sb("t1", [P, NT])
        nm = sb("nm", [P, NT])
        rw = sb("rw", [P, E])
        rb = sb("rb", [P, E])
        cen = sb("cen", [E, P])
        cenT = sb("cenT", [P, E])
        lng = sb("lng", [P, P])
        lnb = sb("lnb", [P, P])
        b1r = sb("b1r", [E * FC, 2, P])
        b1T = sb("b1T", [P, 2, E * FC])
        b2 = sb("b2", [P, 2, E, D])
        lg = sb("lg", [P, NT, E])
        lmx = sb("lmx", [P, NT])
        keyi = sb("keyi", [P, NT, E], I32)
        keym = sb("keym", [P, NT, E], I32)
        hi = sb("hi", [P, E, NT])
        lo = sb("lo", [P, E, NT])
        cmpb = sb("cmpb", [P, NT * 24], BF16)
        thr = sb("thr", [P, 24])
        cst = sb("cst", [P, 24])
        sat = sb("sat", [P, 24])
        nsat = sb("nsat", [P, E])
        base = sb("base", [P, E])
        base1 = sb("base1", [P, 2, 5])
        v2 = sb("v2", [P, E, NT])
        dif = sb("dif", [P, E, NT])
        ge = sb("ge", [P, 2, E, NT + 1], BF16)
        lim = sb("lim", [P, E])
        less = sb("less", [P, E, NT])
        plc = sb("plc", [P, E, NT])
        sel = sb("sel", [P, E, NT])
        plci = sb("plci", [P, E, NT], I32)
        row_i = sb("row_i", [P, E, NT], I32)
        col_i = sb("col_i", [P, E, NT], I32)
        gs = sb("gs", [PL, 2, PL], F16)
        prod = sb("prod", [P, 2, 2, PL])
        avail = sb("avail", [P, NT])
        hie = sb("hie", [P, NT])
        oh_row, oh_col, oh_tok = [flat_qs[:, k * T:(k + 1) * T].bitcast(F16).rearrange(
            "p (e i c) -> p e i c", e=E, i=NT) for k in range(3)]
        idx = [sb(f"idx{l}", [P, 2 * E], I32) for l in range(2)]
        w1 = sb("w1", [P, E, F])
        w2 = sb("w2", [P, E * FC, D])
        gt = ks[:].rearrange("p a b -> p (a b)")[:, 0:4 * E * AUG].bitcast(F32).rearrange(
            "p (c d) -> p c d", d=AUG)
        xg = sb("xg", [P, 2, CAP])
        hb = pbuf[:, 0:2, :].rearrange("p a (c s) -> p a c s", c=FC)
        yb = cT[:].rearrange("p (c d) -> p c d", d=D)

        ld = {n: sem("ld_" + n) for n in ("ctx", "x", "w", "mask", "biases", "late", "b2", "ffn0", "ffn1")}
        pool_const = sem("pool_const")
        pool_own = sem("pool_own")
        dve_own = sem("dve_own")
        act_own = sem("act_own")
        phase = sem("phase")
        filled = sem("filled")
        drained = sem("drained")
        v_full = sem("v_full")
        v_free = sem("v_free")
        f_ready = sem("f_ready")
        p1_ready = sem("p1_ready")
        r_ready = sem("r_ready")
        p2_ready = sem("p2_ready")
        p3_ready = sem("p3_ready")
        img_written = [sem(f"img_written{i}") for i in range(3)]
        rv_ready = sem("rv_ready")
        ps_rv = sem("ps_rv")
        bias_ready = sem("bias_ready")
        ln_done = sem("ln_done")
        ln_act = sem("ln_act")
        nm_ready = sem("nm_ready")
        res_out = sem("res_out")
        aug_ready = sem("aug_ready")
        ln2_done = sem("ln2_done")
        ln2_act = sem("ln2_act")
        ones_ready = sem("ones_ready")
        gained = sem("gained")
        var_ready = sem("var_ready")
        sd_ready = sem("sd_ready")
        x_moved = sem("x_moved")
        out_full = sem("out_full")
        lg_full = sem("lg_full")
        lg_shift = sem("lg_shift")
        lg_exp = sem("lg_exp")
        sc_ready = sem("sc_ready")
        aug_out = sem("aug_out")
        cnt_ready = [sem(f"cnt_ready{l}") for l in range(2)]
        tot_ready = [sem(f"tot_ready{l}") for l in range(2)]
        own_route1 = sem("own_route1")
        oh_ready = sem("oh_ready")
        g_full = sem("g_full")
        g_ready = sem("g_ready")
        idx_full = sem("idx_full")
        idx_ready = sem("idx_ready")
        row_got = [sem(f"row_got{e}") for e in range(E)]
        xg_full = sem("xg_full")
        xg_ready = sem("xg_ready")
        h_full = sem("h_full")
        h_ready = sem("h_ready")
        y_full = sem("y_full")
        y_ready = sem("y_ready")
        added = sem("added")
        f1 = {n: sem("late_" + n) for n in ("oh_ready", "g_full", "g_ready", "idx_full", "idx_ready",
                                        "row_got", "xg_full", "xg_ready", "h_full", "h_ready",
                                        "y_full", "y_ready", "added")}
        stored = sem("stored")
        at = [{n: sem(f"{n}{l}") for n in
               ("stk0", "stk1", "stk2", "stk3", "mrow0", "mrow1", "mrow2", "mrow3", "vcopy", "mx_ps",
                "mx_red", "mxT", "mx_split", "st_ps", "exp_done", "pv_done", "o_out", "oT", "o_copy", "o_rec",
                "o_norm", "own_split", "mx_read")}
              for l in range(2)]

        def dview(ap):
            return ap.rearrange("b s d -> (b s) d").rearrange("(i p) d -> p i d", p=P)

        names = [["L0_xattn_wq_w", "L0_xattn_wk_w", "L0_xattn_wv_w", "L0_xattn_out_w"],
                 ["L1_xattn_w_q", "L1_xattn_w_k", "L1_xattn_w_v", "L1_xattn_w_o"]]
        bnames = [["L0_xattn_wq_b", "L0_xattn_wk_b", "L0_xattn_wv_b", "L0_xattn_out_b"],
                  ["L1_xattn_b_q", "L1_xattn_b_k", "L1_xattn_b_v", "L1_xattn_b_o"]]
        block = ctx.enter_context(nc.Block())
        phases = {}

        def meet(eng, drain=True):
            phases[eng] = phases.get(eng, 0) + 1
            if drain:
                eng.drain().then_inc(phase, 1)
            else:
                eng.sem_inc(phase, 1)
            eng.wait_ge(phase, 5 * phases[eng])

        def bcast(ap, n):
            return ap.unsqueeze(0).to_broadcast([P, n])

        @block.sync
        def _(sp):
            for l in range(2):
                for j in range(4):
                    sp.dma_start(wst[:, 4 * l + j, :], a[names[l][j]]).then_inc(ld["w"], 16)
            for half in range(2):
                sp.dma_start(on[:, 8 * half:8 * half + 8, :],
                             dview(a["ctx_1024"])[:, 8 * half:8 * half + 8, :]).then_inc(ld["ctx"], 16)
            for half in range(2):
                sp.dma_start(x[:, 8 * half:8 * half + 8, :],
                             dview(a["x"])[:, 8 * half:8 * half + 8, :]).then_inc(ld["x"], 16)
            sp.dma_start(maski[:], a["mask_1x1xSxS2_ik0"].rearrange("a b s t -> (a b s) t")
                         .rearrange("(i p) t -> p i t", p=P)).then_inc(ld["mask"], 16)
            sp.dma_start(bqrow[:], a[bnames[0][0]].unsqueeze(0)).then_inc(ld["biases"], 16)
            for l, j in ((0, 1), (1, 0), (1, 1)):
                sp.dma_start(bcol[:, 2 * l + j:2 * l + j + 1], a[bnames[l][j]].unsqueeze(1)
                             ).then_inc(ld["biases"], 16)
            for l in range(2):
                for j in range(2):
                    sp.dma_start(brow[:, 2 * l + j, :], bcast(a[bnames[l][2 + j]], P)
                                 ).then_inc(ld["biases"], 16)

            def write_image(img, first, chunks):
                for c in chunks:
                    n = first + c
                    sp.wait_ge(p3_ready, n + 1)
                    for bb in range(2):
                        row = (2 * c + bb) * PARTS * HD
                        sp.dma_start(img[row:row + PARTS * HD, :].rearrange("r (h s) -> h r s", h=H),
                                     parts[:, n % 3, :, bb * S:bb * S + S]
                                     ).then_inc(img_written[n % 3], 16)

            def written(chunks):
                for n in chunks:
                    sp.wait_ge(img_written[n % 3], WRITTEN[n])

            def load_stack(l, b, slot, keys=True, queries=True):
                par, half = slot // 2, slot % 2
                cols = slice(half * UH * S, (half + 1) * UH * S)
                s = at[l][f"stk{slot}"]
                rows = bass.ds(b * (PARTS * HD), PARTS * HD)
                k_rows = kimg[l][rows, cols].rearrange("(d a) x -> a d x", a=PARTS)
                for i in range(PARTS if keys else 0):
                    sp.dma_start(ks[i * 24:i * 24 + 24, par, cols],
                                 k_rows[i].unsqueeze(1).to_broadcast([HD, PARTS, UH * S])
                                 ).then_inc(s, 16)
                if queries:
                    sp.dma_start(qs[0:PAIRS, par, cols],
                                 qimg[l][rows, cols].unsqueeze(0)
                                 .to_broadcast([PARTS, PARTS * HD, UH * S])).then_inc(s, 16)

            def first_keys(l):
                sp.wait_ge(ones_ready, l + 1)
                for w in range(4):
                    load_stack(l, w // 2, w, queries=False)

            def first_queries(l):
                written([(8,), (12,)][l])
                for w in range(4):
                    load_stack(l, w // 2, w, keys=False)

            def max_rows(l, slot):
                par, half = slot // 2, slot % 2
                cols = slice(half * UH * S, (half + 1) * UH * S)
                for i in range(PARTS):
                    sp.dma_start(qs[PAIRS + i:PAIRS + i + 1, par, cols], m3[:, slot % 2, i, :]
                                 ).then_inc(at[l][f"mrow{slot}"], 16)

            def attention(l):
                A = at[l]
                written([(9, 10, 11), (13, 14, 15)][l])
                for w in range(2):
                    sp.wait_ge(A["mx_split"], w + 1)
                    max_rows(l, w)
                with sp.Fori(0, UNITS // 4 - 1) as it:
                    for w in range(4):
                        b = sp.snap(it * 2 + (w // 2 + 2))
                        used = sp.snap(it * 16 + 4 * (w + 1))
                        split = sp.snap(it * 4 + (w + 3))
                        sp.wait_ge(A["st_ps"], used)
                        load_stack(l, b, w)
                        sp.wait_ge(A["mx_split"], split)
                        max_rows(l, (w + 2) % 4)
                for w in range(UNITS - 2, UNITS):
                    sp.wait_ge(A["mx_split"], w + 1)
                    max_rows(l, w % 4)

            write_image(kimg[0], 0, range(NCH))
            write_image(kimg[1], NCH, range(NCH))
            written((5, 6, 7))
            first_keys(0)
            write_image(qimg[0], 2 * NCH, [0])
            first_queries(0)
            write_image(qimg[0], 2 * NCH, range(1, NCH))
            meet(sp, drain=False)
            attention(0)
            meet(sp, drain=False)
            meet(sp, drain=False)
            sp.dma_start(acc.rearrange("(i p) d -> p i d", p=P), x[:]).then_inc(x_moved, 16)
            sp.wait_ge(sc_ready, 1)
            sp.dma_start(xaug.rearrange("(i p) c -> p i c", p=P), xn[:]).then_inc(aug_out, 16)
            sp.wait_ge(x_moved, 16)
            meet(sp, drain=False)
            sp.dma_start(x[:], acc.rearrange("(i p) d -> p i d", p=P)).then_inc(x_moved, 16)
            first_keys(1)
            write_image(qimg[1], 3 * NCH, [0])
            first_queries(1)
            write_image(qimg[1], 3 * NCH, range(1, NCH))
            meet(sp, drain=False)
            attention(1)
            meet(sp, drain=False)
            meet(sp, drain=False)
            sp.wait_ge(res_out, 3)
            sp.dma_start(dview(out), x[:]).then_inc(stored, 16)
            sp.wait_ge(aug_ready, 1)
            sp.dma_start(xaug.rearrange("(i p) c -> p i c", p=P), xn[:]).then_inc(aug_out, 16)

        @block.tensor
        def _(pe):
            ring = [0]

            def fill(instructions):
                n = ring[0]
                ring[0] += 1
                if n >= 6:
                    pe.wait_ge(drained, n - 5)
                for f in instructions:
                    last = f(ps[:, n % 6, :])
                last.then_inc(filled, 1)

            def warm_up(n=16, bank=5):
                for _ in range(n):
                    pe.matmul(ps[:, bank, :], identb[:], bias[:].rearrange("p a b -> p (a b)"),
                              start=True, stop=True)

            def tiles(src, lo_, n=4):
                return [lambda bank, j=j: pe.transpose(bank[:, j * P:j * P + P], src(lo_ + j), identf[:])
                        for j in range(n)]

            def project(w, srcT, c):
                return [lambda bank: pe.matmul(bank, wT[:, w, :], srcT[:, c * CH:c * CH + CH],
                                               start=True, stop=True)]

            def transpose_x(norm):
                for c in range(4):
                    if norm == 4 and c % 2 == 1:
                        pe.wait_ge(gained, c // 2 + 1)
                    else:
                        pe.wait_ge([ln_done, ln_act][c % 2], 2 * norm + c // 2 + 1)
                    fill(tiles(lambda i: xn[:, i, 0:D], 4 * c))

            pe.wait_ge(pool_const, 1)
            pe.wait_ge(ld["w"], 16 * 8)
            for l in range(2):
                fill(tiles(lambda j: wst[:, j, :], 4 * l))
            pe.wait_ge(ld["ctx"], 32)
            for c in range(4):
                fill(tiles(lambda i: on[:, i, :], 4 * c))
            pe.wait_ge(drained, 6)
            for l in range(2):
                for q in range(4):
                    fill(project(4 * l + 1, cT, q))
                    n = 4 * l + q
                    if n >= 2:
                        pe.wait_ge(v_free, n - 1)
                    for j in range(4):
                        i = 4 * q + j
                        mm = pe.matmul(ps[:, 6 + n % 2, j * P:j * P + P], cT[:, i * P:i * P + P],
                                       wT[:, 4 * l + 2, :], start=True, stop=True)
                    mm.then_inc(v_full, 1)
            pe.wait_ge(ld["late"], 16 * 7)
            pe.wait_ge(ld["b2"], 32)
            fill([lambda bank: pe.transpose(bank[:, 0:E], cen[:], identf[0:E, 0:E])]
                 + [lambda bank, l=l: pe.transpose(bank[:, 32 + 32 * l:64 + 32 * l], b1r[:, l, :],
                                                   identf[0:32, 0:32]) for l in range(2)])
            pe.wait_ge(v_free, 8)
            pe.wait_ge(rv_ready, 1)
            for st in range(2):
                pe.matmul(ps[:, 7, st * P:st * P + P], rvrep[:, st, :], identb[:], start=True, stop=True)
            pb = ps[:, 7, 256:512].bitcast(BF16)
            for st in range(2):
                for tt in range(2):
                    mm = pe.transpose(pb[:, tt * S + st * P:tt * S + st * P + P],
                                      bias[:, st, tt * P:tt * P + P], identb[:])
            mm.then_inc(ps_rv, 1)
            transpose_x(0)
            pe.wait_ge(bias_ready, 1)
            turned = ring[0]
            for c in range(NCH):
                pe.wait_ge(drained, turned - 3 + c)
                fill([lambda bank, c=c: pe.matmul(bank, wT[:, 0, :], xT[:, c * CH:c * CH + CH],
                                                  start=True, stop=False),
                      lambda bank: pe.matmul(bank, bqrow[:], rvrow[:], start=False, stop=True)])
            meet(pe)

            def attention(l):
                A = at[l]

                def value(it, per, c):
                    return c if it is None else it * per + c

                def max_head(it, w, h):
                    m, slot = UH * w + h, w % 4
                    if it is not None or m >= 2:
                        pe.wait_ge(A["mx_red"], value(it, 32, m - 1))
                    if h == 0:
                        pe.wait_ge(A[f"stk{slot}"], value(it, 64, 64 * (w // 4 + 1)))
                    c0 = (slot % 2 * UH + h) * S
                    for st in range(2):
                        o = ps[:, h % 2, st * S:st * S + S]
                        mm = pe.matmul(o, qs[0:PAIRS, slot // 2, c0 + st * P:c0 + st * P + P],
                                       ks[0:PAIRS, slot // 2, c0:c0 + S], start=True, stop=True)
                    mm.then_inc(A["mx_ps"], 1)

                def scores(it, u):
                    w, g = u // 4, u % 4
                    slot = w % 4
                    if it is not None or u >= 2:
                        pe.wait_ge(A["exp_done"], value(it, 16, u - 1))
                    if g == 0:
                        pe.wait_ge(A[f"mrow{slot}"], value(it, 48, 48 * (w // 4 + 1)))
                    for hh in range(2):
                        h = slot % 2 * UH + 2 * g + hh
                        for tt in range(2):
                            o = ps[:, 2 + 2 * (u % 2) + hh, tt * S:tt * S + S]
                            mm = pe.matmul(o, ks[0:ROWS, slot // 2, h * S + tt * P:h * S + tt * P + P],
                                           qs[0:ROWS, slot // 2, h * S:h * S + S],
                                           start=True, stop=l == 1)
                            if l == 0:
                                mm = pe.matmul(o, minus[:], biasT[:, tt, :], start=False, stop=True)
                    mm.then_inc(A["st_ps"], 1)

                def values(it, q, turned):
                    b, par = q // 4, q // 4 % 2
                    pe.wait_ge(A["exp_done"], value(it, 16, 2 * q + 2))
                    if q % 4 == 0:
                        pe.wait_ge(A["vcopy"], value(it, 2, b + 1))
                    if it is not None or q >= 1:
                        pe.wait_ge(A["o_out"], value(it, 8, q))
                    pe.wait_ge(A["mx_read"], value(it, 4, turned))
                    for tt in range(2):
                        for j in range(4):
                            p0 = j % 2 * 512 + tt * S
                            mm = pe.matmul(ps[VP * j:VP * j + VP, 6, 0:S],
                                           vb[:, par, tt, q % 4 * 4 + j, :],
                                           pbuf[:, (2 * q + j // 2) % 4, p0:p0 + S],
                                           start=tt == 0, stop=tt == 1, tile_position=(0, VP * j))
                    mm.then_inc(A["pv_done"], 1)

                def turn_quad(it, q):
                    pe.wait_ge(A["o_out"], value(it, 8, q + 1))
                    if it is not None or q >= 1:
                        pe.wait_ge(A["o_copy"], value(it, 8, q))
                    for st in range(2):
                        mm = pe.transpose(ps[:, 7, st * P:st * P + P], ob[:, q % 2, st * P:st * P + P],
                                          identf[:])
                    mm.then_inc(A["oT"], 1)

                def turn_maxima(it, w):
                    pe.wait_ge(A["mx_red"], value(it, 32, UH * (w + 1)))
                    if it is not None or w >= 1:
                        pe.wait_ge(A["mx_read"], value(it, 4, w))
                    if it is not None or w >= 2:
                        pe.wait_ge(A["o_out"], value(it, 8, 2 * w - 3))
                    pe.transpose(ps[0:2 * UH, 6, 2 * P:3 * P], mx[:, w % 2, :], identf[:]
                                 ).then_inc(A["mxT"], 1)

                def step(it, u):
                    w, g = u // 4, u % 4
                    if w + 2 < UNITS:
                        max_head(it, w + 2, 2 * g)
                    if u < PAIRS_N:
                        scores(it, u)
                    if w + 2 < UNITS:
                        max_head(it, w + 2, 2 * g + 1)
                    if g == 0 and w >= 1 and w + 1 < UNITS:
                        turn_maxima(it, w + 1)
                    if u % 2 == 0 and u >= 4:
                        turn_quad(it, (u - 4) // 2)
                    if u % 2 == 1 and u >= 3:
                        values(it, (u - 3) // 2, min(w + 2, UNITS))

                warm_up()
                for w in range(2):
                    for h in range(UH):
                        max_head(None, w, h)
                        warm_up(2)
                    turn_maxima(None, w)
                    warm_up(8)
                for u in range(8):
                    step(None, u)
                with pe.Fori(0, UNITS // 4 - 1) as it:
                    for u in range(8, 24):
                        step(it, u)
                for u in range(PAIRS_N - 8, PAIRS_N + 3):
                    step(None, u)

            def project_out(l):
                for c in range(4):
                    fill(tiles(lambda i: on[:, i, :], 4 * c))
                for c in range(4):
                    pe.wait_ge(drained, ring[0] - 3 + c)
                    if c >= 2:
                        pe.wait_ge(v_free, 8 + 4 * l + c - 1)
                    for j in range(4):
                        i = 4 * c + j
                        mm = pe.matmul(ps[:, 6 + c % 2, j * P:j * P + P], xT[:, i * P:i * P + P],
                                       wT[:, 4 * l + 3, :], start=True, stop=True)
                    mm.then_inc(out_full, 1)

            def logits(rhs, n):
                pe.wait_ge(drained, ring[0])
                for i in range(NT):
                    mm = pe.matmul(ps[:, 6, i * E:(i + 1) * E], xT[:, i * P:i * P + P], rhs,
                                   start=True, stop=True)
                mm.then_inc(lg_full, 1)

            def totals(l, w):
                for i in range(NT):
                    mm = pe.matmul(ps[:, 7, 0:w], onesb[:], cmpb[:, i * w:(i + 1) * w],
                                   start=i == 0, stop=i == NT - 1)
                mm.then_inc(tot_ready[l], 1)

            def prefixes(l, n_e):
                w = 2 * n_e * (NT + 1)
                o = ps[:, 7, 64:64 + w].rearrange("p (g e i) -> p g e i", g=2, e=n_e)
                pe.matmul(o, tri[:], ge[:, :, 0:n_e, :], start=True, stop=False)
                for i in range(NT):
                    mm = pe.matmul(o[:, :, :, i + 1:NT + 1], onesb[:],
                                   ge[:, :, 0:n_e, i:i + 1].to_broadcast([P, 2, n_e, NT - i]),
                                   start=False, stop=i == NT - 1)
                mm.then_inc(tot_ready[l], 1)

            def place_table(experts):
                for k, e in enumerate(experts):
                    for i in range(NT):
                        mm = pe.matmul(ps[0:PL, 6, k * PL:(k + 1) * PL], oh_row[:, e, i, :],
                                       oh_tok[:, e, i, :], start=i == 0, stop=i == NT - 1)
                return mm

            def place_list(n):
                for half in range(2):
                    c0 = 64 + half * n * PL
                    mm = pe.matmul(ps[:, 6, c0:c0 + n * PL], spread[:, half, :],
                                   gs[:, 0:n, :], start=True, stop=True)
                return mm

            def ffn():
                def rows_in(e):
                    pe.wait_ge(row_got[e], 32)
                    if e >= 2:
                        pe.wait_ge(xg_ready, e - 1)
                    for half in range(2):
                        mm = pe.transpose(ps[:, e % 2, half * P:half * P + P],
                                          gt[:, 2 * e + half, 0:D], identf[:])
                    mm.then_inc(xg_full, 1)

                def hidden(e):
                    pe.wait_ge(xg_ready, e + 1)
                    if e == 0:
                        pe.wait_ge(ld["ffn0"], 32 * E)
                    if e >= 2:
                        pe.wait_ge(h_ready, 4 * (e - 1))
                    for c in range(FC):
                        mm = pe.matmul(ps[:, 2 + 2 * (e % 2) + c // 2,
                                          (c % 2) * CAP:(c % 2) * CAP + CAP],
                                       w1[:, e, c * P:c * P + P], xg[:, e % 2, :],
                                       start=True, stop=True)
                        if c % 2 == 1:
                            mm.then_inc(h_full, 1)

                def outputs(e):
                    pe.wait_ge(h_ready, 4 * (e + 1))
                    if e == 0:
                        pe.wait_ge(idx_ready, E // 2)
                    if e >= 2:
                        pe.wait_ge(y_ready, e - 1)
                    for half in range(2):
                        for c in range(FC):
                            mm = pe.matmul(ps[:, 6 + e % 2, half * D:half * D + D],
                                           hb[:, e % 2, c, half * P:half * P + P],
                                           w2[:, e * FC + c, :], start=c == 0, stop=c == FC - 1)
                    mm.then_inc(y_full, 1)

                rows_in(0)
                for e in range(E):
                    if e + 1 < E:
                        rows_in(e + 1)
                    hidden(e)
                    if e >= 1:
                        outputs(e - 1)
                outputs(E - 1)

            def expert_step(e):
                def outputs(n, r):
                    if r == 0:
                        pe.wait_ge(f1["h_ready"], 4 * (n + 1))
                        if n >= 1:
                            pe.wait_ge(f1["y_ready"], n)
                    half = r // 2
                    o = ps[:, 5, half * D:half * D + D]
                    if r % 2 == 0:
                        pe.matmul(o, onesf[0:1, :], b2[0:1, 1, n, :], start=True, stop=False)
                    for c in (2 * (r % 2), 2 * (r % 2) + 1):
                        mm = pe.matmul(o, hb[:, 0, c, half * P:half * P + P], w2[:, n * FC + c, :],
                                       start=False, stop=c == FC - 1)
                    if r == 3:
                        mm.then_inc(f1["y_full"], 1)

                def rows_in(n):
                    pe.wait_ge(f1["row_got"], 32 * (n + 1))
                    for half in range(2):
                        mm = pe.transpose(ps[:, 0, half * P:half * P + P], gt[:, half, 0:D], identf[:])
                    mm.then_inc(f1["xg_full"], 1)

                def hidden(n, c):
                    if c == 0:
                        pe.wait_ge(f1["xg_ready"], n + 1)
                    pe.matmul(ps[:, 1 + c, 0:CAP], w1[:, n, c * P:c * P + P], xg[:, 0, :],
                              start=True, stop=True).then_inc(f1["h_full"], 1)

                def list_places(n):
                    pe.wait_ge(f1["g_ready"], n + 1)
                    place_list(1).then_inc(f1["idx_full"], 1)

                def table(n):
                    pe.wait_ge(f1["oh_ready"], n + 1)
                    place_table([0]).then_inc(f1["g_full"], 1)

                if e >= 1:
                    list_places(e - 1)
                if e < E - 1:
                    for r in range(9):
                        pe.wait_ge(cnt_ready[1], 9 * e + r + 1)
                        if r < 8:
                            totals(1, 15)
                        else:
                            prefixes(1, 1)
                        if e >= 2 and r < 4:
                            outputs(e - 2, r)
                        if e >= 1 and r == 4:
                            rows_in(e - 1)
                        if e >= 1 and r >= 5:
                            hidden(e - 1, r - 5)
                    table(e)
                else:
                    pe.wait_ge(cnt_ready[1], 9 * e + 1)
                    prefixes(1, 1)
                    table(e)
                    for r in range(4):
                        outputs(e - 2, r)
                    list_places(e)
                    warm_up(10, bank=0)
                    for n in (e - 1, e):
                        rows_in(n)
                        for c in range(FC):
                            hidden(n, c)
                        for r in range(4):
                            outputs(n, r)

            attention(0)
            meet(pe)
            project_out(0)
            meet(pe)
            warm_up(32)
            transpose_x(1)
            logits(rw[:], 1)
            for r in range(16):
                pe.wait_ge(cnt_ready[0], r + 1)
                totals(0, 24)
            pe.wait_ge(cnt_ready[0], 17)
            prefixes(0, E)
            for n in range(E // 2):
                pe.wait_ge(oh_ready, n + 1)
                if n >= 1:
                    pe.wait_ge(idx_ready, n)
                place_table([2 * n, 2 * n + 1]).then_inc(g_full, 1)
                pe.wait_ge(g_ready, n + 1)
                place_list(2).then_inc(idx_full, 1)
            ffn()
            meet(pe)
            pe.wait_ge(x_moved, 32)
            warm_up()
            transpose_x(2)
            turned = ring[0]
            for c in range(NCH):
                pe.wait_ge(drained, turned - 3 + c)
                fill(project(4, xT, c))
            meet(pe)
            attention(1)
            meet(pe)
            project_out(1)
            meet(pe)
            pe.wait_ge(var_ready, 5)
            warm_up()
            transpose_x(4)
            logits(cenT[:], 2)
            pe.wait_ge(ld["ffn1"], 32 * E)
            for e in range(E):
                expert_step(e)

        @block.scalar
        def _(act):
            ring = [0]
            act.wait_ge(pool_const, 1)

            def drain(dst):
                n = ring[0]
                ring[0] += 1
                act.wait_ge(filled, n + 1)
                return act.copy(dst, ps[:, n % 6, 0:dst.shape[-1]])

            def drain_x():
                for c in range(4):
                    drain(xT[:, c * CH:c * CH + CH]).then_inc(drained, 1)

            def chunk(n, bias_, first=False, scale=1.0):
                m = ring[0]
                ring[0] += 1
                act.wait_ge(filled, m + 1)
                src = ps[:, m % 6, :]
                if n >= 2:
                    act.wait_ge(r_ready, n - 1)
                b_ = 0.0 if bias_ is None else bias_
                act.activation(fbuf[:, n % 2, :], src, ACT.Identity, bias=b_, scale=scale
                               ).then_inc(f_ready, 1)
                if n >= 3:
                    act.wait_ge(img_written[n % 3], WRITTEN[n - 3])
                act.activation(parts[:, n % 3, 0, :], src, ACT.Identity, bias=b_, scale=scale
                               ).then_inc(p1_ready, 1)
                if not first:
                    second(n - 1)
                act.wait_ge(f_ready, n + 1)
                act.wait_ge(p1_ready, n + 1)
                act.sem_inc(drained, 1)

            def root(norm):
                act.activation(tiny[:], tiny[:], ACT.Sqrt)
                act.wait_ge(var_ready, norm + 1)
                act.activation(sd[:], ve_[:], ACT.Sqrt).then_inc(sd_ready, 1)

            def apply_norm(norm, src, dst, signal=ln_act):
                act.wait_ge(nm_ready, norm + 1)
                for c in (1, 3):
                    for i in range(4 * c, 4 * c + 4):
                        ins = act.activation(dst[:, i, 0:D], src[:, i, 0:D], ACT.Identity,
                                             bias=nm[:, i:i + 1], scale=rs[:, i:i + 1])
                    ins.then_inc(signal or ln2_act, 1)

            def second(n):
                act.wait_ge(r_ready, n + 1)
                act.copy(parts[:, n % 3, 1, :], rbuf[:, n % 2, :]).then_inc(p2_ready, 1)

            for l in range(2):
                drain(wT[:, 4 * l:4 * l + 4, :].rearrange("p a b -> p (a b)")).then_inc(drained, 1)
            for c in range(4):
                drain(cT[:, c * CH:c * CH + CH]).then_inc(drained, 1)
            root(0)
            act.wait_ge(ld["biases"], 16 * 8)
            for l in range(2):
                for c in range(NCH):
                    chunk(4 * l + c, bcol[:, 2 * l + 1:2 * l + 2], first=l + c == 0)
                    if 4 * l + c == 3:
                        apply_norm(0, x, xn)
            second(7)
            n = ring[0]
            ring[0] += 1
            act.wait_ge(filled, n + 1)
            act.copy(cenT[:], ps[:, n % 6, 0:E])
            act.copy(b1T[:].rearrange("p l c -> p (l c)"), ps[:, n % 6, 32:96]).then_inc(drained, 1)
            drain_x()
            for c in range(NCH):
                chunk(8 + c, None, first=c == 0, scale=unslope[:].bitcast(F32))
            second(11)
            meet(act)

            def attention(l):
                A = at[l]

                def step(it, u):
                    def value(per, c):
                        return c if it is None else it * per + c

                    if u < PAIRS_N:
                        act.wait_ge(A["st_ps"], value(16, u + 1))
                        if it is not None or u >= 4:
                            act.wait_ge(A["pv_done"], value(8, (u - 4) // 2 + 1))
                        b0 = 2 + 2 * (u % 2)
                        if l == 0:
                            for hh in range(2):
                                h = u % 8 * 2 + hh
                                ins = act.activation(pbuf[:, u % 4, hh * 2 * S:(hh + 1) * 2 * S],
                                                     ps[:, b0 + hh, :], ACT.Exp, bias=0.0,
                                                     scale=2.0 ** -(h + 1))
                        else:
                            ins = act.activation(pbuf[:, u % 4, :],
                                                 ps[:, b0:b0 + 2, :].rearrange("p a b -> p (a b)"),
                                                 ACT.Exp, bias=0.0, scale=HD ** -0.5)
                        ins.then_inc(A["exp_done"], 1)
                    if u % 2 == 1 and u >= 3:
                        q = (u - 3) // 2
                        act.wait_ge(A["pv_done"], value(8, q + 1))
                        if it is not None or q >= 2:
                            act.wait_ge(A["oT"], value(8, q - 1))
                        act.copy(ob[:, q % 2, :], ps[:, 6, 0:S]).then_inc(A["o_out"], 1)
                    if u % 2 == 0 and u >= 4:
                        q = (u - 4) // 2
                        act.wait_ge(A["oT"], value(8, q + 1))
                        if it is not None or q >= 2:
                            act.wait_ge(A["o_norm"], value(8, q - 1))
                        act.copy(oq[:, q % 2, :], ps[:, 7, 0:2 * P]).then_inc(A["o_copy"], 1)

                for u in range(8):
                    step(None, u)
                with act.Fori(0, UNITS // 4 - 1) as it:
                    for u in range(8, 24):
                        step(it, u)
                for u in range(PAIRS_N - 8, PAIRS_N + 3):
                    step(None, u)

            def ffn():
                def hidden(e):
                    if e >= 2:
                        act.wait_ge(y_full, e - 1)
                    for c in range(FC):
                        act.wait_ge(h_full, 2 * e + c // 2 + 1)
                        act.activation(hb[:, e % 2, c, :],
                                       ps[:, 2 + 2 * (e % 2) + c // 2,
                                          (c % 2) * CAP:(c % 2) * CAP + CAP],
                                       ACT.Relu, bias=b1T[:, 0, e * FC + c:e * FC + c + 1], scale=1.0
                                       ).then_inc(h_ready, 1)
                for e in range(E):
                    hidden(e)

            def expert_step(it, e):
                def value(per, c):
                    return c if it is None else it * per + c

                def table(n):
                    act.wait_ge(f1["g_full"], value(1, n + 1))
                    act.copy(gs[:, 0, :], ps[0:PL, 6, 0:PL]).then_inc(f1["g_ready"], 1)

                def outputs(n):
                    act.wait_ge(f1["y_full"], value(1, n + 1))
                    y = (yb[:, 2 * n:2 * n + 2, :] if it is None
                         else yb[:, bass.ds(it * 2 + 2 * n, 2), :])
                    act.copy(y, ps[:, 5, 0:2 * D].rearrange("p (a b) -> p a b", a=2)
                             ).then_inc(f1["y_ready"], 1)

                def hidden(n):
                    act.wait_ge(f1["xg_full"], value(1, n + 1))
                    act.copy(xg[:, 0, :], ps[:, 0, 0:CAP]).then_inc(f1["xg_ready"], 1)
                    for c in range(FC):
                        act.wait_ge(f1["h_full"], value(4, 4 * n + c + 1))
                        b0 = n * FC + c
                        bias_ = (b1T[:, 1, b0:b0 + 1] if it is None
                                 else b1T[:, 1, bass.ds(it * FC + b0, 1)])
                        act.activation(hb[:, 0, c, :], ps[:, 1 + c, 0:CAP], ACT.Gelu_apprx_tanh,
                                       bias=bias_, scale=1.0).then_inc(f1["h_ready"], 1)

                if it is not None or e >= 1:
                    table(e - 1)
                if e == E - 1:
                    table(e)
                if it is not None or e >= 2:
                    outputs(e - 2)
                if it is not None or e >= 1:
                    hidden(e - 1)
                if e == E - 1:
                    outputs(e - 1)
                    hidden(e)
                    outputs(e)

            attention(0)
            meet(act)
            drain_x()
            meet(act)
            root(1)
            apply_norm(1, x, xn)
            drain_x()
            act.wait_ge(lg_shift, 1)
            act.activation(lg[:], lg[:], ACT.Exp).then_inc(lg_exp, 1)
            for n in range(E // 2):
                act.wait_ge(g_full, n + 1)
                act.copy(gs[:].rearrange("p a b -> p (a b)"), ps[0:PL, 6, 0:2 * PL]
                         ).then_inc(g_ready, 1)
            ffn()
            meet(act)
            root(2)
            apply_norm(2, x, xn)
            drain_x()
            for c in range(NCH):
                chunk(12 + c, bcol[:, 2:3], first=c == 0)
            second(15)
            meet(act)
            attention(1)
            meet(act)
            drain_x()
            meet(act)
            root(3)
            apply_norm(3, x, xn)
            root(4)
            apply_norm(4, xn, on, signal=None)
            drain_x()
            expert_step(None, 1)
            with act.Fori(0, E - 3) as it:
                expert_step(it, 2)
            expert_step(None, E - 1)

        @block.vector
        def _(ve):
            own = Chain(ve, dve_own)
            link = own.link
            norms = [0]

            def spread_of(src):
                for i in range(NT):
                    ins = ve.bn_stats(stats[:, i, :], src[:, i, 0:D])
                link(ins)
                for i in range(NT):
                    ins = ve.bn_aggr(mv[:, i, :], stats[:, i, :])
                link(ins)
                norms[0] += 1
                ve.tensor_scalar(ve_[:], mv[:, :, 1], EPS, None, ALU.add).then_inc(var_ready, 1)

            def apply_norm(src, dst, masked=False, signal=None):
                ve.wait_ge(sd_ready, norms[0])
                link(ve.reciprocal(rs[:], sd[:]))
                link(ve.tensor_tensor(t1[:], rs[:], rs[:], ALU.mult))
                link(ve.tensor_tensor(t1[:], t1[:], ve_[:], ALU.mult))
                link(ve.tensor_scalar(t1[:], t1[:], -0.5, 1.5, ALU.mult, ALU.add))
                link(ve.tensor_tensor(rs[:], rs[:], t1[:], ALU.mult))
                if masked:
                    by_half = rs[:].rearrange("p (b i) -> p b i", i=2)
                    link(ve.tensor_tensor(by_half, by_half, rv[:].unsqueeze(1)
                                          .to_broadcast([P, B, 2]), ALU.mult))
                ve.scalar_tensor_tensor(nm[:], mv[:, :, 0], -1.0, rs[:], ALU.mult, ALU.mult
                                        ).then_inc(nm_ready, 1)
                for c in (0, 2):
                    for i in range(4 * c, 4 * c + 4):
                        ins = ve.tensor_scalar(dst[:, i, 0:D], src[:, i, 0:D], mv[:, i, 0:1],
                                               rs[:, i:i + 1], ALU.subtract, ALU.mult)
                    ins.then_inc(ln_done if signal is None else signal, 1)

            def ones_rows():
                link(ve.memset(ks[64:96, :, :].bitcast(F32), TWO_ONES))
                ve.sem_inc(ones_ready, 1)

            def rest(n):
                ve.wait_ge(f_ready, n + 1)
                ve.wait_ge(p1_ready, n + 1)
                if n >= 2:
                    ve.wait_ge(p3_ready, n - 1)
                ve.tensor_tensor(rbuf[:, n % 2, :], fbuf[:, n % 2, :], parts[:, n % 3, 0, :],
                                 ALU.subtract).then_inc(r_ready, 1)

            def third(n):
                ve.wait_ge(p2_ready, n + 1)
                ve.tensor_tensor(parts[:, n % 3, 2, :], rbuf[:, n % 2, :], parts[:, n % 3, 1, :],
                                 ALU.subtract).then_inc(p3_ready, 1)

            ones_rows()
            ve.memset(ge[:], 0.0)
            for l in range(2):
                ve.memset(v9[l][:, :, :, HD:VW], 1.0)
            ve.wait_ge(pool_const, 2)
            link(ve.tensor_scalar(unslope[:], unslope[:], 3, None, ALU.arith_shift_right))
            link(ve.tensor_scalar(unslope[:], unslope[:], 128, None, ALU.add))
            link(ve.tensor_scalar(unslope[:], unslope[:], 23, None, ALU.arith_shift_left))
            ve.tensor_reduce(pick[:], identf[:].rearrange("p (k c) -> p c k", c=PL), AX.X, ALU.add)
            ve.wait_ge(ld["x"], 32)
            spread_of(x)
            ve.wait_ge(ld["mask"], 16)
            link(ve.tensor_scalar(mz[:], maski[:], 0, None, ALU.is_equal))
            link(ve.tensor_reduce(rv[:], mz[:], AX.X, ALU.min))
            link(ve.tensor_scalar(rv[:], rv[:], -1.0, 1.0, ALU.mult, ALU.add))
            link(ve.scalar_tensor_tensor(mz[:], mz[:], BIG, dist[:], ALU.mult, ALU.max))
            for st in range(2):
                ve.tensor_scalar(bias[:, st, :], mz[:, st, :], rv[:, st:st + 1], None, ALU.mult)
                ins = ve.tensor_scalar(rvrep[:, st, :], onesf[:], rv[:, st:st + 1], None, ALU.mult)
            ins.then_inc(rv_ready, 1)
            ve.wait_ge(ld["biases"], 16 * 8)
            for n in range(8):
                l, q = n // 4, n % 4
                ve.wait_ge(v_full, n + 1)
                ve.tensor_tensor(v9[l][:, 4 * q:4 * q + 4, :, 0:HD],
                                 ps[:, 6 + n % 2, :].rearrange("p (i h d) -> p i h d", i=4, h=H),
                                 brow[:, 2 * l, :].rearrange("p (h d) -> p h d", h=H).unsqueeze(1)
                                 .to_broadcast([P, 4, H, HD]), ALU.add).then_inc(v_free, 1)
                rest(n)
                if n >= 1:
                    third(n - 1)
                if n == 2:
                    apply_norm(x, xn, masked=True)
            third(7)
            ve.wait_ge(ps_rv, 1)
            ve.tensor_copy(rvrow[:, 0:S], ps[0:1, 7, 0:256])
            ve.tensor_copy(rvrow[:, S:2 * S], ps[0:1, 7, 0:256])
            link(ve.tensor_copy(biasT[:].rearrange("p a b -> p (a b)"), ps[:, 7, 256:512].bitcast(BF16)))
            ve.sem_inc(bias_ready, 1)
            for n in range(8, 12):
                rest(n)
                if n >= 9:
                    third(n - 1)
            third(11)
            meet(ve)

            def attention(l):
                A = at[l]

                def value(it, per, c):
                    return c if it is None else it * per + c

                def reduce_head(it, w, h):
                    ve.wait_ge(A["mx_ps"], value(it, 32, UH * w + h + 1))
                    if l == 0:
                        ve.memset(waiter[:, h % 2:h % 2 + 1], 0.0)
                        for st in range(2):
                            ins = ve.tensor_tensor_reduce(
                                flat_xn[:, (h % 2 * 2 + st) * S:(h % 2 * 2 + st + 1) * S],
                                ps[:, h % 2, st * S:st * S + S], bias[:, st, :], 1.0, -3.0e38,
                                ALU.subtract, ALU.max, mx[:, w % 2, 2 * h + st:2 * h + st + 1])
                    else:
                        ins = ve.tensor_reduce(mx[:, w % 2, 2 * h:2 * h + 2],
                                               ps[:, h % 2, :].rearrange("p (a b) -> p a b", a=2),
                                               AX.X, ALU.max)
                    ins.then_inc(A["mx_red"], 1)

                def split_max(it, w, stage):
                    src = ps[0:2 * UH, 6, 2 * P:3 * P]
                    part = m3[:, w % 2]
                    if stage == 0:
                        ve.wait_ge(A["mxT"], value(it, 4, w + 1))
                        if it is not None or w >= 2:
                            ve.wait_ge(A[f"mrow{(w - 2) % 4}"], value(it, 48, 48 * ((w - 2) // 4 + 1)))
                        ve.tensor_scalar(part[:, 0, :], src, -1.0, None, ALU.mult
                                         ).then_inc(A["own_split"], 1)
                    elif stage == 1:
                        ve.wait_ge(A["own_split"], value(it, 8, 2 * w + 1))
                        ve.scalar_tensor_tensor(mr[:], src, -1.0, part[:, 0, :], ALU.mult,
                                                ALU.subtract).then_inc(A["mx_read"], 1)
                    elif stage == 2:
                        ve.wait_ge(A["mx_read"], value(it, 4, w + 1))
                        ve.tensor_copy(part[:, 1, :], mr[:]).then_inc(A["own_split"], 1)
                    else:
                        ve.wait_ge(A["own_split"], value(it, 8, 2 * w + 2))
                        ve.tensor_tensor(part[:, 2, :], mr[:], part[:, 1, :], ALU.subtract
                                         ).then_inc(A["mx_split"], 1)

                def invert_sums(it, q):
                    ve.wait_ge(A["o_copy"], value(it, 8, q + 1))
                    o = oq[:, q % 2, :].rearrange("p (i h d) -> p i h d", i=2, h=4)
                    ve.reciprocal(rec[:, q % 2, :].rearrange("p (i h) -> p i h", i=2), o[:, :, :, HD]
                                  ).then_inc(A["o_rec"], 1)

                def step(it, u):
                    w, g = u // 4, u % 4
                    ahead = w + 2 < UNITS
                    split = w >= 1 and w + 1 < UNITS
                    if g == 1 and split:
                        split_max(it, w + 1, 1)
                    if ahead:
                        reduce_head(it, w + 2, 2 * g)
                    if g == 1 and split:
                        split_max(it, w + 1, 2)
                    if u % 2 == 0 and u >= 6:
                        invert_sums(it, (u - 6) // 2)
                    if ahead:
                        reduce_head(it, w + 2, 2 * g + 1)
                    if g < 2 and split:
                        split_max(it, w + 1, 3 * g)

                for w in range(2):
                    for h in range(UH):
                        reduce_head(None, w, h)
                    for stage in range(4):
                        split_max(None, w, stage)
                for u in range(8):
                    step(None, u)
                with ve.Fori(0, UNITS // 4 - 1) as it:
                    for u in range(8, 24):
                        step(it, u)
                for u in range(PAIRS_N - 8, PAIRS_N + 5):
                    step(None, u)

            def project_out(l):
                for c in range(4):
                    ve.wait_ge(out_full, 4 * l + c + 1)
                    ve.tensor_tensor(x[:, 4 * c:4 * c + 4, :].rearrange("p a b -> p (a b)"),
                                     ps[:, 6 + c % 2, :],
                                     x[:, 4 * c:4 * c + 4, :].rearrange("p a b -> p (a b)"),
                                     ALU.add).then_inc(v_free, 1)

            def make_keys(link_, src):
                bits = src.bitcast(I32)
                link_(ve.tensor_scalar(keym[:], bits, 31, None, ALU.arith_shift_right))
                link_(ve.tensor_scalar(keym[:], keym[:], -2 ** 31, None, ALU.bitwise_or))
                link_(ve.tensor_tensor(keyi[:], bits, keym[:], ALU.bitwise_xor))
                link_(ve.tensor_scalar(keym[:], keyi[:], 16, None, ALU.logical_shift_right))
                ve.tensor_copy(hi[:].rearrange("p e i -> p i e"), keym[:])
                link_(ve.tensor_scalar(keyi[:], keyi[:], 65535, None, ALU.bitwise_and))
                link_(ve.tensor_copy(lo[:].rearrange("p e i -> p i e"), keyi[:]))

            def search_all(data, tot):
                th = thr[:].rearrange("p (e j) -> p e j", e=E)
                cs = cst[:].rearrange("p (e j) -> p e j", e=E)
                cm = cmpb[:].rearrange("p (i e j) -> p i e j", i=NT, e=E)
                by_tile = data.rearrange("p e i -> p i e").unsqueeze(3).to_broadcast([P, NT, E, 3])

                def offsets(r):
                    return step0[:, r, :].unsqueeze(1).to_broadcast([P, E, 3])

                ve.memset(base[:], 0.0)
                link(ve.tensor_copy(th, offsets(0)))
                for r in range(8):
                    step = float(2 ** (14 - 2 * r))
                    ve.tensor_tensor(cm, by_tile, th.unsqueeze(1).to_broadcast([P, NT, E, 3]),
                                     ALU.is_ge).then_inc(cnt_ready[0], 1)
                    if r < 7:
                        link(ve.tensor_tensor(cs, base[:].unsqueeze(2).to_broadcast([P, E, 3]),
                                              offsets(r + 1), ALU.add))
                    tot[0] += 1
                    ve.wait_ge(tot_ready[0], tot[0])
                    link(ve.tensor_scalar(sat[:], ps[:, 7, 0:24], float(CAP), None, ALU.is_ge))
                    link(ve.tensor_reduce(nsat[:], sat[:].rearrange("p (e j) -> p e j", e=E), AX.X,
                                          ALU.add))
                    if r < 7:
                        ve.scalar_tensor_tensor(th, nsat[:].unsqueeze(2).to_broadcast([P, E, 3]), step,
                                                cs, ALU.mult, ALU.add)
                    link(ve.scalar_tensor_tensor(base[:], nsat[:], step, base[:], ALU.mult, ALU.add))

            def search_one(lk, data, bs, first, value, meanwhile=None):
                cm = cmpb[:, 0:NT * 15].rearrange("p (i j) -> p i j", i=NT)
                for r in range(4):
                    ve.scalar_tensor_tensor(cm, data.unsqueeze(2).to_broadcast([P, NT, 15]),
                                            bs[:, r:r + 1],
                                            step1[:, r, :].unsqueeze(1).to_broadcast([P, NT, 15]),
                                            ALU.subtract, ALU.is_ge).then_inc(cnt_ready[1], 1)
                    if r == 0 and meanwhile:
                        meanwhile()
                    ve.wait_ge(tot_ready[1], value(first + r))
                    lk(ve.tensor_scalar(sat[:, 0:15], ps[:, 7, 0:15], float(CAP), None, ALU.is_ge))
                    lk(ve.tensor_tensor_reduce(sat[:, 0:15], sat[:, 0:15], onesf[:, 0:15],
                                               float(2 ** (12 - 4 * r)), bs[:, r:r + 1], ALU.mult,
                                               ALU.add, bs[:, r + 1:r + 2]))

            def take(lk, n_e, l, total):
                w = 2 * n_e * (NT + 1)
                o = ps[:, 7, 64:64 + w].rearrange("p (g e i) -> p g e i", g=2, e=n_e)
                lim_bc = lim[:, 0:n_e].unsqueeze(2).to_broadcast([P, n_e, NT])
                above, on_it = ge[:, 0, 0:n_e, 0:NT], ge[:, 1, 0:n_e, 0:NT]
                ls, pl, se = less[:, 0:n_e, :], plc[:, 0:n_e, :], sel[:, 0:n_e, :]
                pi = plci[:, 0:n_e, :]
                ve.wait_ge(tot_ready[l], total)
                lk(ve.tensor_scalar(lim[:, 0:n_e], o[:, 0, :, NT], -1.0, float(CAP), ALU.mult, ALU.add))
                ve.tensor_tensor(ls, o[:, 1, :, 0:NT], lim_bc, ALU.is_lt)
                lk(ve.tensor_tensor(pl, o[:, 1, :, 0:NT], lim_bc, ALU.min))
                ve.tensor_tensor(ls, ls, on_it, ALU.mult)
                lk(ve.tensor_tensor(pl, pl, o[:, 0, :, 0:NT], ALU.add))
                lk(ve.tensor_tensor(se, above, ls, ALU.add))
                lk(ve.scalar_tensor_tensor(pl, pl, 1.0, se, ALU.add, ALU.mult))
                lk(ve.tensor_scalar(pi, pl, -1.0, None, ALU.add))
                ve.tensor_scalar(row_i[:, 0:n_e, :], pi, 4, None, ALU.arith_shift_right)
                lk(ve.tensor_scalar(col_i[:, 0:n_e, :], pi, PL - 1, None, ALU.bitwise_and))

            def one_hot(lk, e0, n_e):
                es = slice(e0, e0 + n_e)
                full = [P, n_e, NT, PL]
                to = count16[:].unsqueeze(1).unsqueeze(1).to_broadcast(full)
                ve.tensor_tensor(oh_row[:, es], row_i[:, es].unsqueeze(3).to_broadcast(full), to,
                                 ALU.is_equal)
                lk(ve.tensor_tensor(oh_col[:, es], col_i[:, es].unsqueeze(3).to_broadcast(full), to,
                                    ALU.is_equal))
                return ve.tensor_tensor(oh_tok[:, es], oh_col[:, es],
                                        tokid[:].unsqueeze(1).unsqueeze(3).to_broadcast(full), ALU.mult)

            def read_list(lk, dst, n):
                src = ps[:, 6, 64:64 + 2 * n * PL].rearrange("p (h e c) -> p (h e) c", h=2, c=PL)
                pr = prod[:].rearrange("p h e c -> p (h e) c")[:, 0:2 * n, :]
                lk(ve.tensor_tensor(pr, src, pick[:].unsqueeze(1).to_broadcast([P, 2 * n, PL]),
                                    ALU.mult))
                with nc.allow_low_precision(reason="a whole number below 2048 out of one term"):
                    return ve.tensor_reduce(dst, pr.rearrange("p (h e) c -> p e h c", h=2), AX.X,
                                            ALU.add)

            def ffn():
                for e in range(E):
                    ve.wait_ge(xg_full, e + 1)
                    if e >= 2:
                        ve.wait_ge(h_full, 2 * (e - 1))
                    ve.tensor_copy(xg[:, e % 2, :], ps[:, e % 2, 0:CAP]).then_inc(xg_ready, 1)
                    if e >= 2:
                        finish(e - 2)
                finish(E - 2)
                finish(E - 1)

            def finish(e):
                ve.wait_ge(y_full, e + 1)
                y = yb[:, 2 * e:2 * e + 2, :]
                bb = b2[:, 0, e, :].unsqueeze(1).to_broadcast([P, 2, D])
                link(ve.tensor_tensor(y, ps[:, 6 + e % 2, 0:2 * D].rearrange("p (a b) -> p a b", a=2),
                                      bb, ALU.add))
                ve.tensor_tensor(y, y, gt[:, 2 * e:2 * e + 2, D + e:D + e + 1]
                                 .to_broadcast([P, 2, D]), ALU.mult).then_inc(y_ready, 1)

            def expert_step(it, e):
                def value(per, c):
                    return c if it is None else it * per + c

                done = [STEP1_LINKS * e]

                def lk(ins):
                    done[0] += 1
                    ins.then_inc(own_route1, 1)
                    ve.wait_ge(own_route1, value(STEP1_LINKS, done[0]))

                def read(n):
                    ve.wait_ge(f1["idx_full"], value(1, n + 1))
                    c = slice(2 * n, 2 * n + 2) if it is None else bass.ds(it * 2 + 2 * n, 2)
                    read_list(lk, idx[1][:, c].unsqueeze(1), 1).then_inc(f1["idx_ready"], 1)

                if e < E - 1:
                    e_ = slice(e, e + 1) if it is None else bass.ds(it + e, 1)
                    lk(ve.tensor_tensor(hie[:].unsqueeze(1), hi[:, e_, :], avail[:].unsqueeze(1),
                                        ALU.mult))
                    n0 = 9 * e + 1
                    if e == 0:
                        done[0] += 1
                        ve.sem_inc(own_route1, 1)
                    search_one(lk, hie[:], base1[:, 0, :], n0, lambda c: value(9, c),
                               (lambda: read(e - 1)) if e >= 1 else None)
                    lk(ve.tensor_scalar(dif[:, 0, :], hie[:], base1[:, 0, 4:5], 65536.0, ALU.subtract,
                                        ALU.mult))
                    v = v2[:, 0, :]
                    lk(ve.tensor_tensor(v.unsqueeze(1), dif[:, 0:1, :], lo[:, e_, :], ALU.add))
                    search_one(lk, v, base1[:, 1, :], n0 + 4, lambda c: value(9, c))
                    ve.tensor_scalar(ge[:, 0, 0, 0:NT], v, base1[:, 1, 4:5], None, ALU.is_gt)
                    ve.tensor_scalar(ge[:, 1, 0, 0:NT], v, base1[:, 1, 4:5], None, ALU.is_equal
                                     ).then_inc(cnt_ready[1], 1)
                    take(lk, 1, 1, value(9, n0 + 8))
                    ve.tensor_tensor(avail[:], avail[:], sel[:, 0, :], ALU.subtract)
                else:
                    read(e - 1)
                    ve.tensor_copy(ge[:, 0, 0, 0:NT], avail[:])
                    ve.memset(ge[:, 1, 0, 0:NT], 0.0).then_inc(cnt_ready[1], 1)
                    take(lk, 1, 1, 9 * e + 1)
                one_hot(lk, 0, 1).then_inc(f1["oh_ready"], 1)
                if e < E - 1:
                    assert done[0] == STEP1_LINKS * (e + 1), done[0] - STEP1_LINKS * e
                else:
                    read(e)

            def read_pair(n):
                ve.wait_ge(idx_full, n + 1)
                read_list(link, idx[0][:, 4 * n:4 * n + 4].rearrange("p (e h) -> p e h", h=2), 2
                          ).then_inc(idx_ready, 1)

            attention(0)
            meet(ve)
            project_out(0)
            meet(ve)
            spread_of(x)
            apply_norm(x, xn)
            ve.wait_ge(lg_full, 1)
            link(ve.tensor_tensor(lg[:], ps[:, 6, 0:P].rearrange("p (i e) -> p i e", e=E),
                                  rb[:].unsqueeze(1).to_broadcast([P, NT, E]), ALU.add))
            link(ve.tensor_reduce(lmx[:], lg[:], AX.X, ALU.max))
            ve.tensor_tensor(lg[:], lg[:], lmx[:].unsqueeze(2).to_broadcast([P, NT, E]),
                             ALU.subtract).then_inc(lg_shift, 1)
            ve.wait_ge(lg_exp, 1)
            link(ve.tensor_reduce(lmx[:], lg[:], AX.X, ALU.add))
            link(ve.reciprocal(lmx[:], lmx[:]))
            link(ve.tensor_tensor(lg[:], lg[:], lmx[:].unsqueeze(2).to_broadcast([P, NT, E]), ALU.mult))
            ve.tensor_copy(xn[:, :, D:AUG], lg[:]).then_inc(sc_ready, 1)
            make_keys(link, lg[:])
            tot = [0]
            base_bc = base[:].unsqueeze(2).to_broadcast([P, E, NT])
            search_all(hi[:], tot)
            link(ve.tensor_tensor(dif[:], hi[:], base_bc, ALU.subtract))
            link(ve.scalar_tensor_tensor(v2[:], dif[:], 65536.0, lo[:], ALU.mult, ALU.add))
            search_all(v2[:], tot)
            ve.tensor_tensor(ge[:, 0, :, 0:NT], v2[:], base_bc, ALU.is_gt)
            ve.tensor_tensor(ge[:, 1, :, 0:NT], v2[:], base_bc, ALU.is_equal).then_inc(cnt_ready[0], 1)
            take(link, E, 0, tot[0] + 1)
            for n in range(E // 2):
                one_hot(link, 2 * n, 2).then_inc(oh_ready, 1)
                if n >= 1:
                    read_pair(n - 1)
            read_pair(E // 2 - 1)
            ffn()
            meet(ve)
            ones_rows()
            ve.wait_ge(x_moved, 32)
            spread_of(x)
            apply_norm(x, xn)
            for n in range(12, 16):
                rest(n)
                if n >= 13:
                    third(n - 1)
            third(15)
            meet(ve)
            attention(1)
            meet(ve)
            project_out(1)
            meet(ve)
            spread_of(x)
            apply_norm(x, xn)
            ve.wait_ge(ln_done, 8)
            ve.wait_ge(ln_act, 8)
            spread_of(xn)
            apply_norm(xn, on, signal=ln2_done)
            ve.wait_ge(res_out, 3)
            for c in (0, 2, 1, 3):
                ve.wait_ge([ln2_done, ln2_act][c % 2], c // 2 + 1)
                ts = slice(4 * c, 4 * c + 4)
                link(ve.tensor_tensor(on[:, ts, :], on[:, ts, :],
                                      lng[:].unsqueeze(1).to_broadcast([P, 4, D]), ALU.mult))
                ve.tensor_tensor(xn[:, ts, 0:D], on[:, ts, :],
                                 lnb[:].unsqueeze(1).to_broadcast([P, 4, D]), ALU.add
                                 ).then_inc([ln_done, gained][c % 2], 1)
            ve.wait_ge(ln_done, 10)
            ve.wait_ge(gained, 2)
            ve.sem_inc(aug_ready, 1)
            ve.memset(avail[:], 1.0)
            ve.memset(base1[:, 0, 0:1], 1.0)
            ve.memset(base1[:, 1, 0:1], 0.0)
            ve.wait_ge(lg_full, 2)
            link(ve.tensor_scalar(lg[:], ps[:, 6, 0:P].rearrange("p (i e) -> p i e", e=E), 0.0, None,
                                  ALU.add))
            make_keys(link, lg[:])
            link(ve.tensor_scalar(hi[:], hi[:], 1.0, None, ALU.add))
            expert_step(None, 0)
            with ve.Fori(0, E - 2) as it:
                expert_step(it, 1)
            expert_step(None, E - 1)

        @block.gpsimd
        def _(gp):
            own = Chain(gp, pool_own)
            link = own.link
            nb = dict(allow_small_or_imprecise_dtypes=True)
            gp.memset(tiny[:], 1.0)
            link(gp.memset(identf[:], 0.0))
            link(gp.affine_select(identf[:], identf[:], [[1, P]], ALU.not_equal, 1.0, base=0,
                                  channel_multiplier=-1))
            gp.tensor_copy(identb[:], identf[:]).then_inc(pool_const, 1)
            gp.memset(onesf[:], 1.0)
            gp.memset(onesb[:], 1.0)
            gp.memset(spread[:], 1.0)
            gp.iota(tokid[:], [[P, NT]], base=0, channel_multiplier=1, **nb)
            gp.iota(count16[:], [[1, PL]], base=0, channel_multiplier=0)
            gp.iota(unslope[:], [[0, 1]], base=0, channel_multiplier=1)
            for r in range(8):
                s = 2 ** (14 - 2 * r)
                gp.iota(step0[:, r, :], [[s, 3]], base=s, channel_multiplier=0, **nb)
            for r in range(4):
                s = 2 ** (12 - 4 * r)
                gp.iota(step1[:, r, :], [[s, 15]], base=s, channel_multiplier=0, **nb)
            link(gp.iota(dist[:], [[P, 2], [-1, S]], base=0, channel_multiplier=1, **nb))
            link(gp.affine_select(spread[:], spread[:], [[8 * PL, 2], [1, P]], ALU.is_ge, 0.0, base=0,
                                  channel_multiplier=-PL))
            link(gp.affine_select(spread[:], spread[:], [[-8 * PL, 2], [-1, P]], ALU.is_ge, 0.0,
                                  base=PL - 1, channel_multiplier=PL))
            gp.affine_select(tri[:], onesb[:], [[1, P]], ALU.is_gt, 0.0, base=0, channel_multiplier=-1
                             ).then_inc(pool_const, 1)
            for dst, src in ((rw[:], a["L0_ffn_router_w"]),
                             (rb[:], bcast(a["L0_ffn_router_b"], E)),
                             (cen[:], a["L1_ffn_centroids"]),
                             (lng[:], bcast(a["L1_ffn_ln_g"], P)),
                             (lnb[:], bcast(a["L1_ffn_ln_b"], P)),
                             (b1r[:, 0, :], a["L0_ffn_b1"].rearrange("e (c p) -> (e c) p", p=P)),
                             (b1r[:, 1, :], a["L1_ffn_b1"].rearrange("e (c p) -> (e c) p", p=P))):
                gp.dma_start(dst, src).then_inc(ld["late"], 16)
            gp.memset(vb[:], 0.0)
            gp.tensor_scalar(minus[:], identf[:], -1.0, None, ALU.mult)
            gp.dma_start(b2[:, 0, :, :].rearrange("p e d -> p (e d)"),
                         bcast(a["L0_ffn_b2"].rearrange("e d -> (e d)"), E * D)).then_inc(ld["b2"], 16)
            gp.dma_start(b2[0:1, 1, :, :].rearrange("p e d -> p (e d)"),
                         a["L1_ffn_b2"].rearrange("e d -> (e d)").unsqueeze(0)).then_inc(ld["b2"], 16)

            def load_expert(l, it, e):
                es = slice(e, e + 1) if it is None else bass.ds(it * 2 + e, 1)
                cs = slice(e * FC, (e + 1) * FC) if it is None else bass.ds(it * 2 * FC + e * FC, FC)
                gp.dma_start(w1[:, es, :], a[f"L{l}_ffn_w1"].rearrange("e d f -> d e f")[:, es, :]
                             ).then_inc(ld[f"ffn{l}"], 16)
                gp.dma_start(w2[:, cs, :], a[f"L{l}_ffn_w2"].rearrange("e (c p) d -> p (e c) d", p=P)
                             [:, cs, :]).then_inc(ld[f"ffn{l}"], 16)

            def add_to_residual(term, norm):
                gp.wait_ge(ln_done, 2 * norm + 2)
                gp.wait_ge(ln_act, 2 * norm + 2)
                gp.tensor_tensor(x[:], x[:], term, ALU.add).then_inc(res_out, 1)

            def out_bias(l):
                return brow[:, 2 * l + 1, :].unsqueeze(1).to_broadcast([P, NT, D])

            def attention(l):
                A = at[l]

                def copy(it, b):
                    par = b % 2
                    if it is not None or b >= 2:
                        gp.wait_ge(A["pv_done"], 4 * (b - 1) if it is None else it * 8 + 4 * (b - 1))
                    src = (v9[l][:, 2 * b:2 * b + 2] if it is None
                           else v9[l][:, bass.ds(it * 4 + 2 * b, 2)])
                    gp.tensor_copy(vb[:, par, :, :, 0:VW], src).then_inc(A["vcopy"], 1)

                def normalise(it, q):
                    b, h0 = q // 4, q % 4 * 4 * HD
                    gp.wait_ge(A["o_rec"], q + 1 if it is None else it * 8 + (q + 1))
                    o = oq[:, q % 2, :].rearrange("p (i h d) -> p i h d", i=2, h=4)
                    dst = (on[:, 2 * b:2 * b + 2, h0:h0 + 4 * HD] if it is None
                           else on[:, bass.ds(it * 4 + 2 * b, 2), h0:h0 + 4 * HD])
                    gp.tensor_tensor(dst.rearrange("p i (h d) -> p i h d", h=4), o[:, :, :, 0:HD],
                                     rec[:, q % 2, :].rearrange("p (i h) -> p i h", i=2).unsqueeze(3)
                                     .to_broadcast([P, 2, 4, HD]), ALU.mult).then_inc(A["o_norm"], 1)

                def batch(it, b, experts=(), more=True):
                    for q in range(4 * b, 4 * b + 4):
                        normalise(it, q)
                    for e in experts:
                        load_expert(l, it, e)
                    if more:
                        copy(it, b + 2)

                copy(None, 0)
                copy(None, 1)
                batch(None, 0, experts=(0, 6))
                batch(None, 1, experts=(1, 7))
                with gp.Fori(0, B // 2 - 2) as it:
                    batch(it, 2, experts=(2,))
                    batch(it, 3, experts=(3,))
                batch(None, B - 2, more=False)
                batch(None, B - 1, more=False)

            def gather(l, c, slot, done):
                gp.indirect_dma_start(gt[:, slot, :], None, xaug[:, :],
                                      bass.IndirectOffsetOnAxis(ap=idx[l][:, c:c + 1], axis=0)
                                      ).then_inc(done, 16)

            def scatter_add(dst, l, c, done):
                gp.indirect_dma_start(dst, bass.IndirectOffsetOnAxis(ap=idx[l][:, c:c + 1], axis=0),
                                      yb[:, c, :], None, compute_op=ALU.add).then_inc(done, 16)

            gp.wait_ge(ld["biases"], 16 * 8)
            add_to_residual(out_bias(0), 0)
            meet(gp)
            attention(0)
            meet(gp)
            meet(gp)
            gp.wait_ge(aug_out, 16)
            for e in range(E):
                gp.wait_ge(idx_ready, e // 2 + 1)
                for half in range(2):
                    gather(0, 2 * e + half, 2 * e + half, row_got[e])
            gp.wait_ge(x_moved, 16)
            for e in range(E):
                gp.wait_ge(y_ready, e + 1)
                if e >= 1:
                    gp.wait_ge(added, 32 * e)
                for c in (2 * e, 2 * e + 1):
                    scatter_add(acc, 0, c, added)
            gp.wait_ge(added, 32 * E)
            meet(gp)
            add_to_residual(out_bias(1), 2)
            meet(gp)
            attention(1)
            meet(gp)
            meet(gp)
            add_to_residual(xn[:, :, 0:D], 3)
            gp.wait_ge(aug_out, 32)
            gp.wait_ge(stored, 16)
            for e in range(E + 2):
                if e >= 2:
                    gp.wait_ge(f1["y_ready"], e - 1)
                    if e >= 3:
                        gp.wait_ge(f1["added"], 32 * (e - 2))
                    for half in range(2):
                        scatter_add(out.rearrange("b s d -> (b s) d"), 1, 2 * (e - 2) + half,
                                    f1["added"])
                if e < E:
                    gp.wait_ge(f1["idx_ready"], e + 1)
                    if e >= 1:
                        gp.wait_ge(f1["xg_full"], e)
                    for half in range(2):
                        gather(1, 2 * e + half, half, f1["row_got"])
            gp.wait_ge(f1["added"], 32 * E)


def kernel(**inputs):
    import numpy as np
    import concourse.bacc as bacc
    from concourse.bass_utils import run_bass_kernel_spmd

    nc = bacc.Bacc("TRN2", target_bir_lowering=False, num_devices=1)
    arrays, aps = {}, {}
    for name, value in inputs.items():
        v = np.ascontiguousarray(value)
        arrays["in_" + name] = v
        aps[name] = nc.dram_tensor("in_" + name, v.shape, mybir.dt.from_np(v.dtype),
                                   kind="ExternalInput").ap()
    out = nc.dram_tensor("out", (B, S, D), F32, kind="ExternalOutput").ap()
    build(nc, aps, out)
    r = run_bass_kernel_spmd(nc, [arrays], core_ids=[0])
    return r.results[0]["out"]
```
